# Optimizing a Trainium2 kernel written in Bass

```python
import numpy as np
import jax
import jax.numpy as jnp

def _softmax(x, axis=-1):
    return jax.nn.softmax(x, axis=axis)

def _gelu(x):
    return jax.nn.gelu(x, approximate=True)

def _silu(x):
    return jax.nn.silu(x)

def _sigmoid(x):
    return jax.nn.sigmoid(x)

def _layernorm(x, axis=-1, eps=1e-05):
    m = jnp.mean(x, axis=axis, keepdims=True)
    v = jnp.var(x, axis=axis, keepdims=True)
    return (x - m) / jnp.sqrt(v + eps)

def _scatter_add(tgt, idx, src, axis=0):
    return tgt.at[idx].add(src)

def _segment_sum(src, seg, n):
    return jax.ops.segment_sum(src, seg, n)
kernel_name = 'mk_xattn_ffn_d4_seqx_r8_bd6989'

def setup_inputs(seed: int=0):
    np.random.seed(seed)
    _w = jnp.asarray

    def _rec_inputs():
        import jax
        import jax.numpy as jnp
        _rk = jax.random.key(seed)
        x = 7.22e-05 + 1 * jax.random.normal(jax.random.fold_in(_rk, 1), (8, 256, 128), jnp.float32)
        _lenS = 256 - jax.random.randint(jax.random.fold_in(_rk, 7), (8,), 0, max(1, 256 // 4) + 1, jnp.int32)
        _lenS2 = 64 - jax.random.randint(jax.random.fold_in(_rk, 8), (8,), 0, max(1, 64 // 4) + 1, jnp.int32)
        _ctx_1024P = jax.random.normal(jax.random.fold_in(_rk, 11), (8, 16, 128), jnp.float32)
        _ctx_1024c = jax.random.dirichlet(jax.random.fold_in(_rk, 511), 0.3 * jnp.ones((16,), jnp.float32), (8, 64))
        _ctx_1024t = jnp.einsum('bsk,bkd->bsd', _ctx_1024c, _ctx_1024P)
        _ctx_1024t = _ctx_1024t * jax.lax.rsqrt(jnp.mean(jnp.square(_ctx_1024t)) + 1e-12) * 0.953939
        ctx_1024 = -0.000514642 + 1.00011 * (_ctx_1024t + 0.3 * jax.random.normal(jax.random.fold_in(_rk, 611), (8, 64, 128), jnp.float32))
        _validS = jnp.arange(256)[None, :] < _lenS[:, None]
        _validS2 = jnp.arange(64)[None, :] < _lenS2[:, None]
        _causal = jnp.tril(jnp.ones((256, 256), dtype=bool))
        mask_SxS2_if1 = jnp.where(jnp.ones((256, 64), dtype=bool), 1, 0).astype(jnp.int32)
        mask_BxS2_bk0 = jnp.logical_not(jnp.broadcast_to(_validS2[:, :], (8, 64)))
        return (x, ctx_1024, mask_SxS2_if1, mask_BxS2_bk0)
    x, ctx_1024, mask_SxS2_if1, mask_BxS2_bk0 = _rec_inputs()

    def _L0_xattn_setup():
        import jax, jax.numpy as jnp
        import numpy as np
        B, L_ENC, L_DEC, D = (16, 64, 128, 128)
        key = jax.random.key(seed)
        k1, k2, k3, k4, k5, k6 = jax.random.split(key, 6)
        encoder_hc = jax.random.normal(k1, (B, L_ENC, D), dtype=jnp.float32)
        decoder_hq = jax.random.normal(k2, (B, L_DEC, D), dtype=jnp.float32)
        w_sim = jax.random.normal(k3, (3 * D,), dtype=jnp.float32) * 0.02
        b_sim = jax.random.normal(k4, (1,), dtype=jnp.float32) * 0.02
        W_qv = jax.random.normal(k5, (4 * D, D), dtype=jnp.float32) * 0.02
        b_qv = jax.random.normal(k6, (D,), dtype=jnp.float32) * 0.02
        return {'encoder_hc': encoder_hc, 'decoder_hq': decoder_hq, 'w_sim': w_sim, 'b_sim': b_sim, 'W_qv': W_qv, 'b_qv': b_qv}
    _L0_xattn_all = _L0_xattn_setup()
    _L0_xattn_in = {k: v for k, v in _L0_xattn_all.items() if k in ('w_sim', 'b_sim', 'W_qv', 'b_qv')}
    del _L0_xattn_all

    def _L0_ffn_setup():
        import jax, jax.numpy as jnp
        import numpy as np
        from jax import lax
        D = 128
        E = 8
        F = 512
        TOP_K = 2
        key = jax.random.key(seed)
        ks = jax.random.split(key, 8)
        s = 0.02
        return {'x': jax.random.normal(ks[0], (4, 256, D), dtype=jnp.float32), 'gate_w': jax.random.normal(ks[1], (D, E), dtype=jnp.float32) * s, 'gate_b': jnp.zeros((E,), dtype=jnp.float32), 'w1': jax.random.normal(ks[2], (E, D, F), dtype=jnp.float32) * s, 'b1': jnp.zeros((E, F), dtype=jnp.float32), 'w2': jax.random.normal(ks[3], (E, F, D), dtype=jnp.float32) * s, 'b2': jnp.zeros((E, D), dtype=jnp.float32)}
    _L0_ffn_all = _L0_ffn_setup()
    _L0_ffn_in = {k: v for k, v in _L0_ffn_all.items() if k in ('gate_w', 'gate_b', 'w1', 'b1', 'w2', 'b2')}
    del _L0_ffn_all

    def _L1_xattn_setup():
        import jax, jax.numpy as jnp
        import numpy as np
        E = 128
        H = 16
        D = E // H
        key = jax.random.key(seed)
        ks = jax.random.split(key, 12)
        N, S, T = (4, 256, 256)
        inp = {'query': jax.random.normal(ks[0], (N, S, E), jnp.float32), 'key': jax.random.normal(ks[1], (N, T, E), jnp.float32), 'value': jax.random.normal(ks[2], (N, T, E), jnp.float32), 'attn_mask': jnp.ones((S, T), jnp.int32), 'Wq': jax.random.normal(ks[3], (E, E), jnp.float32) / np.sqrt(E), 'bq': jax.random.normal(ks[4], (E,), jnp.float32) * 0.01, 'Wk': jax.random.normal(ks[5], (E, E), jnp.float32) / np.sqrt(E), 'bk': jax.random.normal(ks[6], (E,), jnp.float32) * 0.01, 'Wv': jax.random.normal(ks[7], (E, E), jnp.float32) / np.sqrt(E), 'bv': jax.random.normal(ks[8], (E,), jnp.float32) * 0.01, 'Wo': jax.random.normal(ks[9], (E, E), jnp.float32) / np.sqrt(E), 'bo': jax.random.normal(ks[10], (E,), jnp.float32) * 0.01}
        return inp
    _L1_xattn_all = _L1_xattn_setup()
    _L1_xattn_in = {k: v for k, v in _L1_xattn_all.items() if k in ('Wq', 'bq', 'Wk', 'bk', 'Wv', 'bv', 'Wo', 'bo')}
    del _L1_xattn_all

    def _L1_ffn_setup():
        import jax, jax.numpy as jnp
        import numpy as np
        B, S, H = (2, 128, 128)
        KD, NH, K = (128, 8, 8)
        NE = 8192
        NK = 32
        EPS = 1e-05
        key = jax.random.key(seed)
        ks = jax.random.split(key, 5)
        inputs = jax.random.normal(ks[0], (B, S, H), jnp.float32)
        bn_gamma = jnp.ones((H,), jnp.float32)
        bn_beta = jnp.zeros((H,), jnp.float32)
        w_q = jax.random.normal(ks[1], (2 * NH * KD, H), jnp.float32) * (1.0 / np.sqrt(H))
        keys_p = jax.random.normal(ks[2], (NH, NK, 2, KD), jnp.float32) * 0.02
        lim = float(np.sqrt(6.0 / (NE + H)))
        down = jax.random.uniform(ks[3], (NE, H), jnp.float32, -lim, lim)
        up = jax.random.uniform(ks[4], (NE, H), jnp.float32, -lim, lim)
        return {'inputs': inputs, 'bn_gamma': bn_gamma, 'bn_beta': bn_beta, 'w_q': w_q, 'keys_p': keys_p, 'down': down, 'up': up}
    _L1_ffn_all = _L1_ffn_setup()
    _L1_ffn_in = {k: v for k, v in _L1_ffn_all.items() if k in ('bn_gamma', 'bn_beta', 'w_q', 'keys_p', 'down', 'up')}
    del _L1_ffn_all

    def _L2_xattn_setup():
        import jax, jax.numpy as jnp
        import numpy as np
        DIM = 128
        HEADS = 16
        HEAD_DIM = DIM // HEADS
        B, N, S = (4, 512, 64)
        key = jax.random.key(seed)
        ks = jax.random.split(key, 9)
        scale = DIM ** (-0.5)
        return {'x': jax.random.normal(ks[0], (B, N, DIM), dtype=jnp.float32), 'context': jax.random.normal(ks[1], (B, S, DIM), dtype=jnp.float32), 'context_mask': jax.random.uniform(ks[2], (B, S)) < 0.2, 'q_w': jax.random.normal(ks[3], (DIM, DIM), dtype=jnp.float32) * scale, 'q_b': jnp.zeros((DIM,), dtype=jnp.float32), 'kv_w': jax.random.normal(ks[4], (DIM, 2 * DIM), dtype=jnp.float32) * scale, 'kv_b': jnp.zeros((2 * DIM,), dtype=jnp.float32), 'proj_w': jax.random.normal(ks[5], (DIM, DIM), dtype=jnp.float32) * scale, 'proj_b': jnp.zeros((DIM,), dtype=jnp.float32)}
    _L2_xattn_all = _L2_xattn_setup()
    _L2_xattn_in = {k: v for k, v in _L2_xattn_all.items() if k in ('q_w', 'q_b', 'kv_w', 'kv_b', 'proj_w', 'proj_b')}
    del _L2_xattn_all

    def _L2_ffn_setup():
        import jax, jax.numpy as jnp
        from jax import lax
        import numpy as np
        D_MODEL = 128
        HIDDEN = 64
        N_EXPERTS = 32
        TOP_K = 2
        B, S = (1, 512)

        def _moe_group(x2, router_w, wg, wu, wd, top_k):
            T = x2.shape[0]
            n_experts = router_w.shape[1]
            logits = x2 @ router_w
            scores = jax.nn.softmax(logits, axis=-1)
            expert_weights, expert_indices = lax.top_k(scores, top_k)
            flat_e = expert_indices.reshape(-1)
            flat_w = expert_weights.reshape(-1)
            flat_t = jnp.repeat(jnp.arange(T), top_k)
            order = jnp.argsort(flat_e)
            tok = flat_t[order]
            xs = x2[tok]
            group_sizes = jnp.bincount(flat_e, length=n_experts).astype(jnp.int32)
            gate = lax.ragged_dot(xs, wg, group_sizes)
            up = lax.ragged_dot(xs, wu, group_sizes)
            ys = lax.ragged_dot(jax.nn.silu(gate) * up, wd, group_sizes)
            ys = ys * flat_w[order][:, None]
            return jnp.zeros_like(x2).at[tok].add(ys)
        key = jax.random.key(seed)
        ks = jax.random.split(key, 9)
        w = lambda k, shape: jax.random.normal(k, shape, dtype=jnp.float32) * 0.02
        return {'x': jax.random.normal(ks[0], (B, S, D_MODEL), dtype=jnp.float32), 'router_w0': w(ks[1], (D_MODEL, N_EXPERTS)), 'wg0': w(ks[2], (N_EXPERTS, D_MODEL, HIDDEN)), 'wu0': w(ks[3], (N_EXPERTS, D_MODEL, HIDDEN)), 'wd0': w(ks[4], (N_EXPERTS, HIDDEN, D_MODEL)), 'router_w1': w(ks[5], (D_MODEL, N_EXPERTS)), 'wg1': w(ks[6], (N_EXPERTS, D_MODEL, HIDDEN)), 'wu1': w(ks[7], (N_EXPERTS, D_MODEL, HIDDEN)), 'wd1': w(ks[8], (N_EXPERTS, HIDDEN, D_MODEL))}
    _L2_ffn_all = _L2_ffn_setup()
    _L2_ffn_in = {k: v for k, v in _L2_ffn_all.items() if k in ('router_w0', 'wg0', 'wu0', 'wd0', 'router_w1', 'wg1', 'wu1', 'wd1')}
    del _L2_ffn_all

    def _L3_xattn_setup():
        import jax, jax.numpy as jnp
        import numpy as np
        N_HEAD, MODEL_DIM, KEY_DIM, VALUE_DIM = (16, 128, 64, 64)
        B, S = (4, 256)
        EPS = 1e-05
        TEMP = float(np.sqrt(KEY_DIM))
        key = jax.random.key(seed)
        ks = jax.random.split(key, 12)
        d = {'query': jax.random.normal(ks[0], (B, S, MODEL_DIM), jnp.float32), 'key': jax.random.normal(ks[1], (B, S, MODEL_DIM), jnp.float32), 'value': jax.random.normal(ks[2], (B, S, MODEL_DIM), jnp.float32), 'Wq': jax.random.normal(ks[3], (MODEL_DIM, N_HEAD * KEY_DIM), jnp.float32) * np.sqrt(2.0 / (MODEL_DIM + KEY_DIM)), 'bq': jnp.zeros((N_HEAD * KEY_DIM,), jnp.float32), 'Wk': jax.random.normal(ks[4], (MODEL_DIM, N_HEAD * KEY_DIM), jnp.float32) * np.sqrt(2.0 / (MODEL_DIM + KEY_DIM)), 'bk': jnp.zeros((N_HEAD * KEY_DIM,), jnp.float32), 'Wv': jax.random.normal(ks[5], (MODEL_DIM, N_HEAD * VALUE_DIM), jnp.float32) * np.sqrt(2.0 / (MODEL_DIM + VALUE_DIM)), 'bv': jnp.zeros((N_HEAD * VALUE_DIM,), jnp.float32), 'Wo': jax.random.normal(ks[6], (N_HEAD * VALUE_DIM, MODEL_DIM), jnp.float32) * np.sqrt(2.0 / (N_HEAD * VALUE_DIM + MODEL_DIM)), 'bo': jnp.zeros((MODEL_DIM,), jnp.float32), 'ln_gamma': jnp.ones((MODEL_DIM,), jnp.float32), 'ln_beta': jnp.zeros((MODEL_DIM,), jnp.float32)}
        return d
    _L3_xattn_all = _L3_xattn_setup()
    _L3_xattn_in = {k: v for k, v in _L3_xattn_all.items() if k in ('Wq', 'bq', 'Wk', 'bk', 'Wv', 'bv', 'Wo', 'bo', 'ln_gamma', 'ln_beta')}
    del _L3_xattn_all

    def _L3_ffn_setup():
        import jax, jax.numpy as jnp
        import numpy as np
        B, S, H = (2, 256, 128)
        E, F, K = (64, 64, 8)
        G, TG = (8, 4)
        SCALE = 2.5
        F_SH = 64

        def _gate(x, gate_w, gate_bias):
            scores = jax.nn.sigmoid(x @ gate_w.T)
            sc = scores + gate_bias[None, :]
            T = x.shape[0]
            group_scores = jax.lax.top_k(sc.reshape(T, G, E // G), 2)[0].sum(-1)
            _, gidx = jax.lax.top_k(group_scores, TG)
            gmask = jnp.zeros((T, G), sc.dtype).at[jnp.arange(T)[:, None], gidx].set(1.0)
            smask = jnp.repeat(gmask, E // G, axis=1)
            masked = jnp.where(smask > 0, sc, -jnp.inf)
            _, tidx = jax.lax.top_k(masked, K)
            tw = jnp.take_along_axis(scores, tidx, axis=1)
            tw = tw / (tw.sum(-1, keepdims=True) + 1e-20)
            return (tidx, tw * SCALE)
        key = jax.random.key(seed)
        ks = jax.random.split(key, 9)

        def w(k, shape, fan_in):
            return jax.random.normal(k, shape, jnp.float32) / np.float32(np.sqrt(fan_in))
        return {'hidden_states': jax.random.normal(ks[0], (B, S, H), jnp.float32), 'gate_w': w(ks[1], (E, H), H), 'gate_bias': jax.random.normal(ks[2], (E,), jnp.float32) * 0.01, 'We_gate': w(ks[3], (E, H, F), H), 'We_up': w(ks[4], (E, H, F), H), 'We_down': w(ks[5], (E, F, H), F), 'Ws_gate': w(ks[6], (H, F_SH), H), 'Ws_up': w(ks[7], (H, F_SH), H), 'Ws_down': w(ks[8], (F_SH, H), F_SH)}
    _L3_ffn_all = _L3_ffn_setup()
    _L3_ffn_in = {k: v for k, v in _L3_ffn_all.items() if k in ('gate_w', 'gate_bias', 'We_gate', 'We_up', 'We_down', 'Ws_gate', 'Ws_up', 'Ws_down')}
    del _L3_ffn_all
    return {'x': x, 'ctx_1024': ctx_1024, 'mask_SxS2_if1': mask_SxS2_if1, 'mask_BxS2_bk0': mask_BxS2_bk0, 'L0_xattn_w_sim': _L0_xattn_in['w_sim'], 'L0_xattn_b_sim': _L0_xattn_in['b_sim'], 'L0_xattn_W_qv': _L0_xattn_in['W_qv'], 'L0_xattn_b_qv': _L0_xattn_in['b_qv'], 'L0_ffn_gate_w': _L0_ffn_in['gate_w'], 'L0_ffn_gate_b': _L0_ffn_in['gate_b'], 'L0_ffn_w1': _L0_ffn_in['w1'], 'L0_ffn_b1': _L0_ffn_in['b1'], 'L0_ffn_w2': _L0_ffn_in['w2'], 'L0_ffn_b2': _L0_ffn_in['b2'], 'L1_xattn_Wq': _L1_xattn_in['Wq'], 'L1_xattn_bq': _L1_xattn_in['bq'], 'L1_xattn_Wk': _L1_xattn_in['Wk'], 'L1_xattn_bk': _L1_xattn_in['bk'], 'L1_xattn_Wv': _L1_xattn_in['Wv'], 'L1_xattn_bv': _L1_xattn_in['bv'], 'L1_xattn_Wo': _L1_xattn_in['Wo'], 'L1_xattn_bo': _L1_xattn_in['bo'], 'L1_ffn_bn_gamma': _L1_ffn_in['bn_gamma'], 'L1_ffn_bn_beta': _L1_ffn_in['bn_beta'], 'L1_ffn_w_q': _L1_ffn_in['w_q'], 'L1_ffn_keys_p': _L1_ffn_in['keys_p'], 'L1_ffn_down': _L1_ffn_in['down'], 'L1_ffn_up': _L1_ffn_in['up'], 'L2_xattn_q_w': _L2_xattn_in['q_w'], 'L2_xattn_q_b': _L2_xattn_in['q_b'], 'L2_xattn_kv_w': _L2_xattn_in['kv_w'], 'L2_xattn_kv_b': _L2_xattn_in['kv_b'], 'L2_xattn_proj_w': _L2_xattn_in['proj_w'], 'L2_xattn_proj_b': _L2_xattn_in['proj_b'], 'L2_ffn_router_w0': _L2_ffn_in['router_w0'], 'L2_ffn_wg0': _L2_ffn_in['wg0'], 'L2_ffn_wu0': _L2_ffn_in['wu0'], 'L2_ffn_wd0': _L2_ffn_in['wd0'], 'L2_ffn_router_w1': _L2_ffn_in['router_w1'], 'L2_ffn_wg1': _L2_ffn_in['wg1'], 'L2_ffn_wu1': _L2_ffn_in['wu1'], 'L2_ffn_wd1': _L2_ffn_in['wd1'], 'L3_xattn_Wq': _L3_xattn_in['Wq'], 'L3_xattn_bq': _L3_xattn_in['bq'], 'L3_xattn_Wk': _L3_xattn_in['Wk'], 'L3_xattn_bk': _L3_xattn_in['bk'], 'L3_xattn_Wv': _L3_xattn_in['Wv'], 'L3_xattn_bv': _L3_xattn_in['bv'], 'L3_xattn_Wo': _L3_xattn_in['Wo'], 'L3_xattn_bo': _L3_xattn_in['bo'], 'L3_xattn_ln_gamma': _L3_xattn_in['ln_gamma'], 'L3_xattn_ln_beta': _L3_xattn_in['ln_beta'], 'L3_ffn_gate_w': _L3_ffn_in['gate_w'], 'L3_ffn_gate_bias': _L3_ffn_in['gate_bias'], 'L3_ffn_We_gate': _L3_ffn_in['We_gate'], 'L3_ffn_We_up': _L3_ffn_in['We_up'], 'L3_ffn_We_down': _L3_ffn_in['We_down'], 'L3_ffn_Ws_gate': _L3_ffn_in['Ws_gate'], 'L3_ffn_Ws_up': _L3_ffn_in['Ws_up'], 'L3_ffn_Ws_down': _L3_ffn_in['Ws_down']}

def reference(x, ctx_1024, mask_SxS2_if1, mask_BxS2_bk0, L0_xattn_w_sim, L0_xattn_b_sim, L0_xattn_W_qv, L0_xattn_b_qv, L0_ffn_gate_w, L0_ffn_gate_b, L0_ffn_w1, L0_ffn_b1, L0_ffn_w2, L0_ffn_b2, L1_xattn_Wq, L1_xattn_bq, L1_xattn_Wk, L1_xattn_bk, L1_xattn_Wv, L1_xattn_bv, L1_xattn_Wo, L1_xattn_bo, L1_ffn_bn_gamma, L1_ffn_bn_beta, L1_ffn_w_q, L1_ffn_keys_p, L1_ffn_down, L1_ffn_up, L2_xattn_q_w, L2_xattn_q_b, L2_xattn_kv_w, L2_xattn_kv_b, L2_xattn_proj_w, L2_xattn_proj_b, L2_ffn_router_w0, L2_ffn_wg0, L2_ffn_wu0, L2_ffn_wd0, L2_ffn_router_w1, L2_ffn_wg1, L2_ffn_wu1, L2_ffn_wd1, L3_xattn_Wq, L3_xattn_bq, L3_xattn_Wk, L3_xattn_bk, L3_xattn_Wv, L3_xattn_bv, L3_xattn_Wo, L3_xattn_bo, L3_xattn_ln_gamma, L3_xattn_ln_beta, L3_ffn_gate_w, L3_ffn_gate_bias, L3_ffn_We_gate, L3_ffn_We_up, L3_ffn_We_down, L3_ffn_Ws_gate, L3_ffn_Ws_up, L3_ffn_Ws_down):
    import jax
    import jax.numpy as jnp

    def _L0_xattn_ref(encoder_hc, decoder_hq, w_sim, b_sim, W_qv, b_qv):
        import jax, jax.numpy as jnp
        import numpy as np
        B, L_ENC, L_DEC, D = (16, 64, 128, 128)
        d = encoder_hc.shape[-1]
        w1, w2, w3 = (w_sim[:d], w_sim[d:2 * d], w_sim[2 * d:])
        Sim = (encoder_hc @ w1)[:, :, None] + (decoder_hq @ w2)[:, None, :] + jnp.einsum('bid,bjd->bij', encoder_hc * w3, decoder_hq) + b_sim[0]
        A = jax.nn.softmax(Sim, axis=2)
        hq_hat = jnp.einsum('bij,bjd->bid', A, decoder_hq)
        Batt = jax.nn.softmax(jnp.max(Sim, axis=2), axis=1)
        hc_bar = jnp.einsum('bi,bid->bd', Batt, encoder_hc)[:, None, :]
        hc_hat = jnp.broadcast_to(hc_bar, encoder_hc.shape)
        feats = jnp.concatenate([encoder_hc, hq_hat, encoder_hc * hq_hat, encoder_hc * hc_hat], axis=-1)
        hcq = feats @ W_qv + b_qv
        return hcq

    def _L0_ffn_ref(x, gate_w, gate_b, w1, b1, w2, b2):
        import jax, jax.numpy as jnp
        import numpy as np
        from jax import lax
        D = 128
        E = 8
        F = 512
        TOP_K = 2
        B, S, _ = x.shape
        flat = x.reshape(-1, D)
        T = flat.shape[0]
        logits = flat @ gate_w + gate_b
        topv, topi = lax.top_k(logits, TOP_K)
        topw = jax.nn.softmax(topv.astype(jnp.float32), axis=-1).astype(x.dtype)
        routing = jnp.zeros_like(logits).at[jnp.arange(T)[:, None], topi].set(topw)

        def body(acc, params):
            W1e, b1e, W2e, b2e, we = params
            h = jax.nn.gelu(flat @ W1e + b1e, approximate=False)
            out = h @ W2e + b2e
            return (acc + out * we[:, None], None)
        init = jnp.zeros_like(flat)
        final, _ = lax.scan(body, init, (w1, b1, w2, b2, routing.T))
        return final.reshape(B, S, D)

    def _L1_xattn_ref(query, key, value, attn_mask, Wq, bq, Wk, bk, Wv, bv, Wo, bo):
        import jax, jax.numpy as jnp
        import numpy as np
        E = 128
        H = 16
        D = E // H
        N, S, _ = query.shape
        T = key.shape[1]
        q = (query @ Wq.T + bq).reshape(N, S, H, D).transpose(0, 2, 1, 3)
        k = (key @ Wk.T + bk).reshape(N, T, H, D).transpose(0, 2, 1, 3)
        v = (value @ Wv.T + bv).reshape(N, T, H, D).transpose(0, 2, 1, 3)
        scores = jnp.einsum('nhsd,nhtd->nhst', q, k) / np.sqrt(D).astype(np.float32)
        scores = jnp.where(attn_mask == 0, jnp.float32(-jnp.inf), scores)
        attn = jax.nn.softmax(scores, axis=-1)
        out = jnp.einsum('nhst,nhtd->nhsd', attn, v)
        out = out.transpose(0, 2, 1, 3).reshape(N, S, E)
        return out @ Wo.T + bo

    def _L1_ffn_ref(inputs, bn_gamma, bn_beta, w_q, keys_p, down, up):
        import jax, jax.numpy as jnp
        import numpy as np
        B, S, H = (2, 128, 128)
        KD, NH, K = (128, 8, 8)
        NE = 8192
        NK = 32
        EPS = 1e-05
        b, s, d = inputs.shape
        x = inputs.reshape(b * s, d)
        mean = x.mean(axis=0)
        var = x.var(axis=0)
        xn = (x - mean) * jax.lax.rsqrt(var + EPS) * bn_gamma + bn_beta
        xn = xn.reshape(b, s, d)
        q = (xn @ w_q.T).reshape(b, s, 2, NH, KD).transpose(2, 0, 1, 3, 4)
        sim = jnp.einsum('pbnhd,hkpd->pbnhk', q, keys_p)
        scores, idx = jax.lax.top_k(sim, K)
        all_scores = (scores[0][..., :, None] + scores[1][..., None, :]).reshape(b, s, NH, K * K)
        all_idx = (idx[0][..., :, None] * NK + idx[1][..., None, :]).reshape(b, s, NH, K * K)
        sc, pk = jax.lax.top_k(all_scores, K)
        indices = jnp.take_along_axis(all_idx, pk, axis=-1)
        wd = down[indices]
        hmid = jnp.einsum('bnd,bnhkd->bnhk', inputs, wd)
        hmid = jax.nn.sigmoid(sc) * jax.nn.gelu(hmid, approximate=False)
        wu = up[indices]
        return jnp.einsum('bnhk,bnhkd->bnd', hmid, wu)

    def _L2_xattn_ref(x, context, context_mask, q_w, q_b, kv_w, kv_b, proj_w, proj_b):
        import jax, jax.numpy as jnp
        import numpy as np
        DIM = 128
        HEADS = 16
        HEAD_DIM = DIM // HEADS
        B, N, S = (4, 512, 64)
        b, n, c = x.shape
        s = context.shape[1]
        h, d = (HEADS, HEAD_DIM)
        scale = d ** (-0.5)
        q = (x @ q_w + q_b).reshape(b, n, h, d)
        kv = (context @ kv_w + kv_b).reshape(b, s, 2, h, d)
        k = kv[:, :, 0]
        v = kv[:, :, 1]
        attn = jnp.einsum('bnhd,bshd->bhns', q, k) * scale
        attn = jnp.where(context_mask[:, None, None, :], -jnp.inf, attn)
        attn = jax.nn.softmax(attn, axis=-1)
        out = jnp.einsum('bhns,bshd->bnhd', attn, v).reshape(b, n, c)
        return out @ proj_w + proj_b

    def _L2_ffn_ref(x, router_w0, wg0, wu0, wd0, router_w1, wg1, wu1, wd1):
        import jax, jax.numpy as jnp
        from jax import lax
        import numpy as np
        D_MODEL = 128
        HIDDEN = 64
        N_EXPERTS = 32
        TOP_K = 2
        B, S = (1, 512)

        def _moe_group(x2, router_w, wg, wu, wd, top_k):
            T = x2.shape[0]
            n_experts = router_w.shape[1]
            logits = x2 @ router_w
            scores = jax.nn.softmax(logits, axis=-1)
            expert_weights, expert_indices = lax.top_k(scores, top_k)
            flat_e = expert_indices.reshape(-1)
            flat_w = expert_weights.reshape(-1)
            flat_t = jnp.repeat(jnp.arange(T), top_k)
            order = jnp.argsort(flat_e)
            tok = flat_t[order]
            xs = x2[tok]
            group_sizes = jnp.bincount(flat_e, length=n_experts).astype(jnp.int32)
            gate = lax.ragged_dot(xs, wg, group_sizes)
            up = lax.ragged_dot(xs, wu, group_sizes)
            ys = lax.ragged_dot(jax.nn.silu(gate) * up, wd, group_sizes)
            ys = ys * flat_w[order][:, None]
            return jnp.zeros_like(x2).at[tok].add(ys)
        b, s, d = x.shape
        x2 = x.reshape(-1, d)
        out0 = _moe_group(x2, router_w0, wg0, wu0, wd0, TOP_K)
        out1 = _moe_group(x2, router_w1, wg1, wu1, wd1, TOP_K)
        out = (out0 * TOP_K + out1 * TOP_K) / (TOP_K + TOP_K)
        return out.reshape(b, s, d)

    def _L3_xattn_ref(query, key, value, Wq, bq, Wk, bk, Wv, bv, Wo, bo, ln_gamma, ln_beta):
        import jax, jax.numpy as jnp
        import numpy as np
        N_HEAD, MODEL_DIM, KEY_DIM, VALUE_DIM = (16, 128, 64, 64)
        B, S = (4, 256)
        EPS = 1e-05
        TEMP = float(np.sqrt(KEY_DIM))
        b, sq, _ = query.shape
        residual = query
        q = (query @ Wq + bq).reshape(b, sq, N_HEAD, KEY_DIM)
        k = (key @ Wk + bk).reshape(b, key.shape[1], N_HEAD, KEY_DIM)
        v = (value @ Wv + bv).reshape(b, value.shape[1], N_HEAD, VALUE_DIM)
        scores = jnp.einsum('bqhd,bkhd->bhqk', q, k) / TEMP
        attn = jax.nn.softmax(scores, axis=-1)
        out = jnp.einsum('bhqk,bkhd->bqhd', attn, v).reshape(b, sq, N_HEAD * VALUE_DIM)
        out = out @ Wo + bo + residual
        mu = jnp.mean(out, axis=-1, keepdims=True)
        var = jnp.var(out, axis=-1, keepdims=True)
        return (out - mu) * jax.lax.rsqrt(var + EPS) * ln_gamma + ln_beta

    def _L3_ffn_ref(hidden_states, gate_w, gate_bias, We_gate, We_up, We_down, Ws_gate, Ws_up, Ws_down):
        import jax, jax.numpy as jnp
        import numpy as np
        B, S, H = (2, 256, 128)
        E, F, K = (64, 64, 8)
        G, TG = (8, 4)
        SCALE = 2.5
        F_SH = 64

        def _gate(x, gate_w, gate_bias):
            scores = jax.nn.sigmoid(x @ gate_w.T)
            sc = scores + gate_bias[None, :]
            T = x.shape[0]
            group_scores = jax.lax.top_k(sc.reshape(T, G, E // G), 2)[0].sum(-1)
            _, gidx = jax.lax.top_k(group_scores, TG)
            gmask = jnp.zeros((T, G), sc.dtype).at[jnp.arange(T)[:, None], gidx].set(1.0)
            smask = jnp.repeat(gmask, E // G, axis=1)
            masked = jnp.where(smask > 0, sc, -jnp.inf)
            _, tidx = jax.lax.top_k(masked, K)
            tw = jnp.take_along_axis(scores, tidx, axis=1)
            tw = tw / (tw.sum(-1, keepdims=True) + 1e-20)
            return (tidx, tw * SCALE)
        b, s, h = hidden_states.shape
        x = hidden_states.reshape(-1, h).astype(jnp.float32)
        tidx, tw = _gate(x, gate_w, gate_bias)
        T = x.shape[0]
        w_dense = jnp.zeros((T, E), tw.dtype).at[jnp.arange(T)[:, None], tidx].add(tw)

        def body(acc, ws):
            wg, wu, wdn, cw = ws
            hmid = jax.nn.silu(x @ wg) * (x @ wu)
            return (acc + cw[:, None] * (hmid @ wdn), None)
        y, _ = jax.lax.scan(body, jnp.zeros_like(x), (We_gate, We_up, We_down, w_dense.T))
        y = y.reshape(b, s, h)
        shared = jax.nn.silu(hidden_states @ Ws_gate) * (hidden_states @ Ws_up) @ Ws_down
        return y + shared
    x = x + _L0_xattn_ref(_layernorm(x, axis=-1), ctx_1024, L0_xattn_w_sim, L0_xattn_b_sim, L0_xattn_W_qv, L0_xattn_b_qv)
    x = x + _L0_ffn_ref(_layernorm(x, axis=-1), L0_ffn_gate_w, L0_ffn_gate_b, L0_ffn_w1, L0_ffn_b1, L0_ffn_w2, L0_ffn_b2)
    x = x + _L1_xattn_ref(_layernorm(x, axis=-1), ctx_1024, ctx_1024, mask_SxS2_if1, L1_xattn_Wq, L1_xattn_bq, L1_xattn_Wk, L1_xattn_bk, L1_xattn_Wv, L1_xattn_bv, L1_xattn_Wo, L1_xattn_bo)
    x = x + _L1_ffn_ref(_layernorm(x, axis=-1), L1_ffn_bn_gamma, L1_ffn_bn_beta, L1_ffn_w_q, L1_ffn_keys_p, L1_ffn_down, L1_ffn_up)
    x = x + _L2_xattn_ref(_layernorm(x, axis=-1), ctx_1024, mask_BxS2_bk0, L2_xattn_q_w, L2_xattn_q_b, L2_xattn_kv_w, L2_xattn_kv_b, L2_xattn_proj_w, L2_xattn_proj_b)
    x = x + _L2_ffn_ref(_layernorm(x, axis=-1), L2_ffn_router_w0, L2_ffn_wg0, L2_ffn_wu0, L2_ffn_wd0, L2_ffn_router_w1, L2_ffn_wg1, L2_ffn_wu1, L2_ffn_wd1)
    x = x + _L3_xattn_ref(_layernorm(x, axis=-1), ctx_1024, ctx_1024, L3_xattn_Wq, L3_xattn_bq, L3_xattn_Wk, L3_xattn_bk, L3_xattn_Wv, L3_xattn_bv, L3_xattn_Wo, L3_xattn_bo, L3_xattn_ln_gamma, L3_xattn_ln_beta)
    x = x + _L3_ffn_ref(_layernorm(x, axis=-1), L3_ffn_gate_w, L3_ffn_gate_bias, L3_ffn_We_gate, L3_ffn_We_up, L3_ffn_We_down, L3_ffn_Ws_gate, L3_ffn_Ws_up, L3_ffn_Ws_down)
    return x

_drawn_inputs = setup_inputs


def setup_inputs(seed=0):
    import zlib

    import numpy as np

    out = dict(_drawn_inputs(seed))
    spreads = {'L0_ffn_gate_b': (0.0, 0.1),
     'L0_ffn_b1': (0.0, 0.1),
     'L0_ffn_b2': (0.0, 0.1),
     'L1_ffn_bn_gamma': (1.0, 0.6),
     'L1_ffn_bn_beta': (0.0, 0.491),
     'L2_xattn_q_b': (0.0, 0.1),
     'L2_xattn_kv_b': (0.0, 0.1),
     'L2_xattn_proj_b': (0.0, 0.1),
     'L3_xattn_bq': (0.0, 0.1),
     'L3_xattn_bk': (0.0, 0.8),
     'L3_xattn_bv': (0.0, 0.1),
     'L3_xattn_bo': (0.0, 0.1),
     'L3_xattn_ln_gamma': (1.0, 0.2),
     'L3_xattn_ln_beta': (0.0, 0.1)}
    factors = {'L1_xattn_bq': 6.244,
     'L1_xattn_bk': 8.0,
     'L1_ffn_w_q': 3.0,
     'L1_ffn_keys_p': 2.961,
     'L1_ffn_down': 2.994,
     'L1_ffn_up': 2.686,
     'L2_ffn_router_w0': 8.0,
     'L2_ffn_wg0': 8.0,
     'L2_ffn_wu0': 8.0,
     'L2_ffn_wd0': 8.0,
     'L2_ffn_router_w1': 8.0,
     'L2_ffn_wg1': 8.0,
     'L2_ffn_wu1': 8.0,
     'L2_ffn_wd1': 8.0}
    for name, (base, spread) in spreads.items():
        noise = np.random.default_rng([zlib.crc32(name.encode()), seed]).standard_normal(out[name].shape)
        drawn = base * np.exp(spread * noise) if base else spread * noise
        out[name] = jnp.asarray(drawn.astype(out[name].dtype))
    for name, factor in factors.items():
        out[name] = (out[name] * factor).astype(out[name].dtype)
    return out
```

```python
from contextlib import ExitStack

import concourse.bass as bass
from concourse import mybir

F32 = mybir.dt.float32
BF16 = mybir.dt.bfloat16
I32 = mybir.dt.int32
U32 = mybir.dt.uint32
U8 = mybir.dt.uint8
ALU = mybir.AluOpType
ACT = mybir.ActivationFunctionType
AX = mybir.AxisListType

P = 128
D = 128
B, S, C = 8, 256, 64
T = B * S
NT = T // P
BLK = 512
NB = T // BLK
TPB = BLK // P
H = 16
HC = H * C
EPS = 1e-5
FAR = -1.0e30
PARTS = 3
E0, F0, K0 = 8, 512, 4
E2, E3, FH = 32, 64, 64
PAIRS = 16
NH, NK, KT8 = 8, 32, 8
NE = NK * NK
G3, GE, TG = 8, 8, 4


class Tally:

    def __init__(self, eng, sem):
        self.eng, self.sem, self.n = eng, sem, 0

    def mark(self, ins):
        ins.then_inc(self.sem, 1)
        self.n = self.n + 1
        return ins

    def wait(self):
        self.eng.wait_ge(self.sem, self.n)

    def settle(self, ins):
        self.mark(ins)
        self.wait()

    def enter(self, i, per):
        self.base, self.per = self.n, per
        self.n = self.base + i * per

    def leave(self, times):
        self.n = self.base + times * self.per


def known(n, least):
    return not isinstance(n, int) or n >= least


def rolled(eng, total, unroll, step):
    for n in range(unroll):
        step(n, n)
    with eng.Fori(1, total // unroll) as i:
        for r in range(unroll):
            step(i * unroll + r, r)


def run_steps(eng, total, unroll, step):
    for n in range(unroll):
        step(n, n)
    with eng.Fori(1, total // unroll - 1) as i:
        for r in range(unroll):
            step(i * unroll + r, r)
    for n in range(total - unroll, total):
        step(n, n % unroll)


COLS = {}
ROWS = {}


def _place(table, names):
    at = 0
    for name, width in names:
        table[name] = (at, width)
        at += width
    return at


NCOLS = _place(COLS, [("w_sim", 3), ("b1_0", E0 * K0), ("bq1", 1), ("bk1", 1), ("bv1", 1), ("gamma", 1), ("beta", 1),
                      ("bq2", 1), ("bk2", 1), ("bv2", 1), ("bq3", 8), ("bk3", 8), ("bv3", 8)])
NROWS = _place(ROWS, [("b_qv", D), ("bo1", D), ("bo2", D), ("bo3", D), ("ln_gamma", D), ("ln_beta", D),
                      ("gate_b", E0), ("gate_bias", E3), ("b_sim", 1)])


class Core:

    def __init__(self, nc, ctx, dram):
        self.nc, self.ctx, self.dram = nc, ctx, dram
        self.own_sems, self.last_sems = [], []

        def sb(name, shape, dt=F32):
            return ctx.enter_context(nc.sbuf_tensor(name, shape, dt))

        self.X = sb("X", [P, NT, D])
        self.XN = sb("XN", [P, NT, D])
        self.XT = sb("XT", [P, T])
        self.RA = sb("RA", [P, 12288])
        self.RB = sb("RB", [P, 16384])
        self.RC = sb("RC", [P, 8448])
        self.RW = sb("RW", [P, 4096])
        self.identf = sb("identf", [P, P])
        self.identb = sb("identb", [P, P], BF16)
        self.pair_sel = sb("pair_sel", [PARTS * E2, PAIRS, P], BF16)
        self.one_sel = sb("one_sel", [PARTS * E0, E0, P], BF16)
        self.head16 = sb("head16", [P, H])
        self.head2 = sb("head2", [P, 2])
        self.iota = sb("iota", [P, E2])
        self.before = sb("before", [P, G3 * G3])
        self.gates = sb("gates", [P, 2 * E2 + E3])
        self.eps = sb("eps", [P, 1])
        self.cols = sb("cols", [P, NCOLS])
        self.rows = sb("rows", [P, NROWS])
        self.ctxT = sb("ctxT", [P, B * C])
        self.stats = sb("stats", [P, NT, 6])
        self.mom = sb("mom", [P, 8, NT])
        self.PS = ctx.enter_context(nc.psum_tensor("PS", [P, 8, BLK], F32))
        self.PB = self.PS[:].bitcast(BF16)

    def sem(self, name):
        self.own_sems.append(self.nc.alloc_semaphore(name=name))
        return self.own_sems[-1]

    def lasting_sem(self, name):
        return self.ctx.enter_context(self.nc.semaphore(name))

    def clear_last(self, pool):
        if self.last_sems:
            self.nc.clear_and_free_semaphores(self.last_sems)
        self.last_sems, self.own_sems = self.own_sems, []

    def col(self, name, k=0):
        at, _ = COLS[name]
        return self.cols[:, at + k:at + k + 1]

    def row(self, name):
        at, width = ROWS[name]
        return self.rows[:, at:at + width]


def over(ap, axis, n):
    ap = ap.unsqueeze(axis)
    shape = list(ap.shape)
    shape[axis] = n
    return ap.broadcast_to(shape)



class Norm:

    def __init__(self, k, name, src, turn=True):
        self.k, self.src, self.turn = k, src, turn
        self.var_ready = k.sem(f"{name}_var_ready")
        self.std_ready = k.sem(f"{name}_std_ready")
        self.xn_ready = k.sem(f"{name}_xn_ready")
        self.xt_turned = k.sem(f"{name}_xt_turned")
        self.xt_ready = k.sem(f"{name}_xt_ready")


def norm_vector(dve, k, nm, own):
    st, mom = k.stats, k.mom
    mean2, dif, m2, difsq, var, mean, std, rstd = (mom[:, j, :] for j in range(8))
    with dve.Fori(0, NT // 4) as i:
        own.enter(i, 4)
        for r in range(4):
            own.mark(dve.bn_stats(st[:, i * 4 + r, :], nm.src[:, i * 4 + r, :]))
    own.leave(NT // 4)
    own.wait()
    own.mark(dve.tensor_tensor(mean2, st[:, :, 1], st[:, :, 4], ALU.add))
    own.mark(dve.tensor_tensor(dif, st[:, :, 1], st[:, :, 4], ALU.subtract))
    own.settle(dve.tensor_tensor(m2, st[:, :, 2], st[:, :, 5], ALU.add))
    own.mark(dve.tensor_scalar(mean, mean2, 0.5, None, ALU.mult))
    own.settle(dve.scalar_tensor_tensor(difsq, dif, D / 4.0, dif, ALU.mult, ALU.mult))
    dve.tensor_tensor(var, difsq, m2, ALU.add).then_inc(nm.var_ready, 1)
    dve.wait_ge(nm.std_ready, 1)
    own.settle(dve.reciprocal(rstd, std))
    for t in range(NT):
        dve.tensor_scalar(k.XN[:, t, :], nm.src[:, t, :], mean[:, t:t + 1], rstd[:, t:t + 1],
                          ALU.subtract, ALU.mult).then_inc(nm.xn_ready, 1)


def norm_scalar(act, k, nm):
    act.wait_ge(nm.var_ready, 1)
    act.activation(k.mom[:, 6, :], k.mom[:, 4, :], ACT.Sqrt, bias=k.eps[:, 0:1],
                   scale=1.0 / D).then_inc(nm.std_ready, 1)
    if nm.turn:
        for b in range(NB):
            act.wait_ge(nm.xt_turned, b + 1)
            act.activation(k.XT[:, bass.ts(b, BLK)], k.PS[:, b, :], ACT.Copy).then_inc(nm.xt_ready, 1)


def norm_tensor(pe, k, nm):
    for t in range(NT):
        pe.wait_ge(nm.xn_ready, t + 1)
        mm = pe.transpose(k.PS[:, t // TPB, bass.ts(t % TPB, P)], k.XN[:, t, :], k.identf[:])
        if t % TPB == TPB - 1:
            mm.then_inc(nm.xt_turned, 1)



def setup(k):
    nc, dram = k.nc, k.dram
    made = k.lasting_sem("setup_made")
    k.x_loaded, k.small_loaded, k.ctx_loaded = k.lasting_sem("x_loaded"), k.lasting_sem("small_loaded"), k.lasting_sem("ctx_loaded")
    k.l0x_loaded, k.l0f_loaded = k.lasting_sem("l0x_loaded"), k.lasting_sem("l0f_loaded")
    k.att_loaded, k.keys_loaded = k.lasting_sem("att_loaded"), k.lasting_sem("keys_loaded")
    k.l2f_loaded, k.l3x_loaded = k.lasting_sem("l2f_loaded"), k.lasting_sem("l3x_loaded")
    k.l3f_loaded, k.l3d_loaded = k.lasting_sem("l3f_loaded"), k.lasting_sem("l3d_loaded")
    zeroed = k.lasting_sem("setup_zeroed")

    k.ctxK = k.RB[0:C, 0:B * D].rearrange("p (b d) -> p b d", b=B)
    k.Wqv = k.RB[:, 1024:1536].rearrange("p (c n) -> p c n", c=4)
    k.W1_0 = k.RA[:, 0:4096].rearrange("p (e f) -> p e f", e=E0)
    k.W2_0 = k.RA[:, 4096:8192].rearrange("p (e f n) -> p e f n", e=E0, f=K0)
    k.b2_0 = k.RA[0:E0, 8192:8320]
    k.gw0 = k.RA[:, 8320:8328]
    k.Wa = [k.RC[:, at:at + 512].rearrange("p (m n) -> p m n", m=4) for at in (5120, 5632)]
    k.mask1 = k.RC[:, 6144:6272].bitcast(I32).rearrange("p (j c) -> p j c", j=2)
    k.mask2 = k.RC[:, 6272:6400].bitcast(U8).rearrange("p (b c) -> p b c", b=B)
    k.masks = k.RC[:, 6400:6784].bitcast(BF16)
    k.mask1_add = k.masks[:, 0:2 * C].rearrange("p (j c) -> p j c", j=2)
    k.mask2_add = k.masks[:, 2 * C:(2 + B) * C].rearrange("p (b c) -> p b c", b=B)
    k.masks_made = k.lasting_sem("masks_made")

    with nc.Block() as block:

        @block.sync
        def _(sp):
            xv = dram["x"].rearrange("(t p) d -> p t d", p=P)
            for q in range(4):
                sp.dma_start(k.X[:, 4 * q:4 * q + 4, :], xv[:, 4 * q:4 * q + 4, :]).then_inc(k.x_loaded, 16)
            sp.dma_start(k.ctxT[:], dram["ctxT"]).then_inc(k.ctx_loaded, 16)
            sp.dma_start(k.cols[:], dram["cols"]).then_inc(k.small_loaded, 16)
            sp.dma_start(k.rows[:], dram["rows"].broadcast_to([P, NROWS])).then_inc(k.small_loaded, 16)
            sp.dma_start(k.gates[:, 0:2 * E2], dram["router2"]).then_inc(k.small_loaded, 16)
            sp.dma_start(k.gates[:, 2 * E2:], dram["gw3"]).then_inc(k.small_loaded, 16)
            sp.dma_start(k.ctxK, dram["ctxK"]).then_inc(k.l0x_loaded, 16)
            sp.dma_start(k.Wqv, dram["Wqv"]).then_inc(k.l0x_loaded, 16)
            sp.dma_start(k.W1_0, dram["w1_0"]).then_inc(k.l0f_loaded, 16)
            sp.dma_start(k.W2_0, dram["w2_0"]).then_inc(k.l0f_loaded, 16)
            sp.dma_start(k.b2_0, dram["b2_0"]).then_inc(k.l0f_loaded, 16)
            sp.dma_start(k.gw0, dram["gw0"]).then_inc(k.l0f_loaded, 16)
            for n in range(2):
                sp.dma_start(k.Wa[n], dram[f"wa{n + 1}"]).then_inc(k.att_loaded, 16)
            sp.dma_start(k.mask1, dram["mask1"]).then_inc(k.att_loaded, 16)
            sp.dma_start(k.RC[:, 6272:6400].bitcast(I32),
                         dram["mask2"].broadcast_to([P, B * C // 4])).then_inc(k.att_loaded, 16)
            sp.dma_start(k.RC[:, 0:2048], dram["w_q"]).then_inc(k.keys_loaded, 16)
            sp.dma_start(k.RC[:, 2048:2560], dram["keysT"]).then_inc(k.keys_loaded, 16)
            sp.dma_start(k.RC[:, 2560:3584], dram["downT"]).then_inc(k.keys_loaded, 16)
            sp.dma_start(k.RC[:, 3584:4608], dram["up"]).then_inc(k.keys_loaded, 16)

        @block.vector
        def _(dve):
            dve.memset(k.eps[:], EPS)
            dve.memset(k.head16[:], 1.0).then_inc(zeroed, 1)
            dve.memset(k.head2[:], 0.0).then_inc(zeroed, 1)
            dve.memset(k.pair_sel[:], 0.0).then_inc(zeroed, 1)
            dve.memset(k.one_sel[:], 0.0).then_inc(zeroed, 1)
            dve.wait_ge(k.att_loaded, 64)
            dve.tensor_scalar(k.mask1_add, k.mask1, 0, FAR, ALU.is_equal, ALU.mult).then_inc(k.masks_made, 1)
            dve.tensor_scalar(k.mask2_add, k.mask2, 0, FAR, ALU.not_equal, ALU.mult).then_inc(k.masks_made, 1)

        @block.gpsimd
        def _(pool):
            own = Tally(pool, made)
            own.settle(pool.iota(k.iota[:], pattern=[[1, E2]], base=0, channel_multiplier=0,
                               allow_small_or_imprecise_dtypes=True))
            own.settle(pool.memset(k.identf[:], 0.0))
            own.settle(pool.memset(k.identb[:], 0.0))
            for m in (k.identf, k.identb):
                own.settle(pool.affine_select(out=m[:], in_=m[:], compare_op=ALU.not_equal, fill=1.0, base=0,
                                            pattern=[[-1, P]], channel_multiplier=1))
            pool.wait_ge(zeroed, 4)
            own.settle(pool.affine_select(out=k.head16[:], in_=k.head16[:], compare_op=ALU.is_ge, fill=0.0, base=0,
                                          pattern=[[-(P // H), H]], channel_multiplier=1))
            own.settle(pool.affine_select(out=k.head16[:], in_=k.head16[:], compare_op=ALU.is_ge, fill=0.0,
                                          base=P // H - 1, pattern=[[P // H, H]], channel_multiplier=-1))
            own.settle(pool.memset(k.head2[0:64, 0:1], 1.0))
            own.settle(pool.memset(k.head2[64:P, 1:2], 1.0))
            own.settle(pool.memset(k.before[:], 1.0))
            own.settle(pool.affine_select(out=k.before[:], in_=k.before[:], compare_op=ALU.is_gt, fill=0.0, base=0,
                                          pattern=[[1, G3], [-1, G3]], channel_multiplier=0))
            for part in range(PARTS):
                own.settle(pool.affine_select(out=k.pair_sel[:], in_=k.pair_sel[:], compare_op=ALU.not_equal,
                                              fill=1.0, base=-part * E2, pattern=[[-2, PAIRS], [-1, 2], [0, FH]],
                                              channel_multiplier=1))
                own.settle(pool.affine_select(out=k.one_sel[:], in_=k.one_sel[:], compare_op=ALU.not_equal,
                                              fill=1.0, base=-part * E0, pattern=[[-1, E0], [0, P]],
                                              channel_multiplier=1))



def similarity_attention(k):
    nc, PS, RB = k.nc, k.PS, k.RB
    nm = Norm(k, "l0x", k.X)
    vec, sca = k.sem("l0x_vector"), k.sem("l0x_scalar")
    w_ready, sim_ready = k.sem("l0x_w_ready"), k.sem("l0x_sim_ready")
    max_ready, shifted, exped = k.sem("l0x_max_ready"), k.sem("l0x_shifted"), k.sem("l0x_exped")
    a_ready, at_turned, at_ready = k.sem("l0x_a_ready"), k.sem("l0x_at_turned"), k.sem("l0x_at_ready")
    mt_ready, bshift, bexp = k.sem("l0x_mt_ready"), k.sem("l0x_bshift"), k.sem("l0x_bexp")
    batt_ready, bc_turned, bc_ready = k.sem("l0x_batt_ready"), k.sem("l0x_bc_turned"), k.sem("l0x_bc_ready")
    hc_done, w14_ready = k.sem("l0x_hc_done"), k.sem("l0x_w14_ready")
    hq_done, hq_ready, f3_ready = k.sem("l0x_hq_done"), k.sem("l0x_hq_ready"), k.sem("l0x_f3_ready")
    out_done, biased = k.sem("l0x_out_done"), k.sem("l0x_biased")

    R = RB[:, 1536:2048]
    w2b = RB[:, 2048:2176]
    sim = RB[:, 2304:3328].rearrange("p (t c) -> p t c", t=NT)
    w14 = RB[:, 3328:4352].rearrange("p (b n) -> p b n", b=B)
    AT = RB[0:C, 4352:6400]
    HQ = RB[:, 6400:8448]
    F3 = RB[:, 8448:10496]
    qmax = k.RW[:, 0:NT]
    qsum = k.RW[:, 16:32]
    qrec = k.RW[:, 32:48]
    batt = k.RW[0:B, 64:64 + S]
    bsum = k.RW[0:B, 400:401]
    brec = k.RW[0:B, 401:402]
    bmax = k.RW[0:B, 402:403]
    bcol = k.RW[:, 416:432].rearrange("p (j b) -> p j b", j=2)
    hc = k.RW[:, 432:440]
    ones = k.RB[:, 2176:2304]
    SIM, MT, BC, HC = 4, 6, 6, 7
    sim_ps = PS[:, SIM:SIM + 2, :].rearrange("p a (t c) -> p (a t) c", c=C)
    q2 = qmax.rearrange("p (b j) -> p j b", j=2)

    with nc.Block() as block:

        @block.gpsimd
        def _(pool):
            k.clear_last(pool)
            pool.wait_ge(nm.xn_ready, NT)
            pool.wait_ge(k.small_loaded, 64)
            pool.tensor_tensor(k.X[:], k.X[:], over(k.row("b_qv"), 1, NT), ALU.add).then_inc(biased, 1)

        @block.vector
        def _(dve):
            own = Tally(dve, vec)
            dve.wait_ge(k.x_loaded, 64)
            norm_vector(dve, k, nm, own)
            own.mark(dve.memset(ones, 1.0))
            dve.wait_ge(k.ctx_loaded, 16)
            dve.wait_ge(k.small_loaded, 64)
            own.settle(dve.tensor_scalar(R, k.ctxT[:], k.col("w_sim", 2), k.col("w_sim", 0), ALU.mult, ALU.add))
            dve.tensor_scalar(w2b, ones, k.col("w_sim", 1), None, ALU.mult).then_inc(w_ready, 1)
            dve.wait_ge(sim_ready, 1)
            own.settle(dve.tensor_scalar(sim, sim_ps, k.row("b_sim"), None, ALU.add))
            dve.tensor_reduce(qmax, sim, AX.X, ALU.max).then_inc(max_ready, 1)
            dve.wait_ge(max_ready, 1)
            dve.tensor_tensor(sim, sim, over(qmax, 2, C), ALU.subtract).then_inc(shifted, 1)
            dve.wait_ge(mt_ready, 1)
            own.settle(dve.tensor_reduce(bmax, PS[0:B, MT, 0:S], AX.X, ALU.max))
            dve.tensor_scalar(batt, PS[0:B, MT, 0:S], bmax, None, ALU.subtract).then_inc(bshift, 1)
            dve.wait_ge(exped, 1)
            own.settle(dve.tensor_reduce(qsum, sim, AX.X, ALU.add))
            own.settle(dve.reciprocal(qrec, qsum))
            dve.tensor_tensor(sim, sim, over(qrec, 2, C), ALU.mult).then_inc(a_ready, 1)
            dve.wait_ge(bexp, 1)
            own.settle(dve.reciprocal(brec, bsum))
            dve.tensor_scalar(batt, batt, brec, None, ALU.mult).then_inc(batt_ready, 1)
            dve.wait_ge(bc_turned, 1)
            dve.tensor_copy(bcol, PS[:, BC, 0:2 * B].rearrange("p (j b) -> p j b", j=2)).then_inc(bc_ready, 1)
            dve.wait_ge(hc_done, 1)
            own.settle(dve.tensor_copy(hc, PS[:, HC, 0:B]))
            dve.wait_ge(k.l0x_loaded, 32)
            for b in range(B):
                ins = dve.scalar_tensor_tensor(w14[:, b, :], k.Wqv[:, 3, :], hc[:, b:b + 1], k.Wqv[:, 0, :],
                                               ALU.mult, ALU.add)
            ins.then_inc(w14_ready, 1)
            for q in range(NB):
                dve.wait_ge(hq_done, q + 1)
                dve.tensor_tensor(F3[:, bass.ts(q, BLK)], k.XT[:, bass.ts(q, BLK)], PS[:, q, :],
                                  ALU.mult).then_inc(f3_ready, 1)
            dve.wait_ge(biased, 1)
            for q in range(NB):
                dve.wait_ge(out_done, q + 1)
                xq = k.X[:, TPB * q:TPB * (q + 1), :].rearrange("p t d -> p (t d)")
                dve.tensor_tensor(xq, xq, PS[:, 4 + q, :], ALU.add)

        @block.scalar
        def _(act):
            norm_scalar(act, k, nm)
            act.wait_ge(shifted, 1)
            act.activation(sim, sim, ACT.Exp).then_inc(exped, 1)
            act.wait_ge(bshift, 1)
            act.activation(batt, batt, ACT.Exp, accum_out=bsum).then_inc(bexp, 1)
            act.wait_ge(at_turned, 1)
            for q in range(NB):
                act.activation(AT[:, bass.ts(q, BLK)], PS[0:C, q, :], ACT.Copy).then_inc(at_ready, 1)
            for q in range(NB):
                act.wait_ge(hq_done, q + 1)
                act.wait_ge(f3_ready, q + 1)
                act.activation(HQ[:, bass.ts(q, BLK)], PS[:, q, :], ACT.Copy).then_inc(hq_ready, 1)

        @block.tensor
        def _(pe):
            norm_tensor(pe, k, nm)
            pe.wait_ge(w_ready, 1)
            pe.wait_ge(nm.xt_ready, NB)
            for t in range(NT):
                b = t // 2
                pe.matmul(sim_ps[:, t, :], k.XT[:, bass.ts(t, P)], R[:, bass.ts(b, C)], start=True, stop=False)
                mm = pe.matmul(sim_ps[:, t, :], w2b, k.ctxT[:, bass.ts(b, C)], start=False, stop=True)
            mm.then_inc(sim_ready, 1)
            pe.wait_ge(max_ready, 1)
            for j in range(2):
                mm = pe.transpose(PS[0:B, MT, bass.ts(j, P)], q2[:, j, :], k.identf[:])
            mm.then_inc(mt_ready, 1)
            pe.wait_ge(a_ready, 1)
            for t in range(NT):
                mm = pe.transpose(PS[0:C, t // TPB, bass.ts(t % TPB, P)], sim[:, t, :], k.identf[:])
            mm.then_inc(at_turned, 1)
            pe.wait_ge(batt_ready, 1)
            for j in range(2):
                mm = pe.transpose(PS[:, BC, bass.ts(j, B)], batt[:, bass.ts(j, P)], k.identf[0:B, 0:B])
            mm.then_inc(bc_turned, 1)
            pe.wait_ge(bc_ready, 1)
            for b in range(B):
                for j in range(2):
                    mm = pe.matmul(PS[:, HC, b:b + 1], k.XN[:, 2 * b + j, :], bcol[:, j, b:b + 1],
                                   start=(j == 0), stop=(j == 1))
            mm.then_inc(hc_done, 1)
            pe.wait_ge(k.l0x_loaded, 32)
            for b in range(B):
                pe.wait_ge(at_ready, NB)
                mm = pe.matmul(PS[:, b // 2, bass.ts(b % 2, S)], k.ctxK[:, b, :], AT[:, bass.ts(b, S)],
                               start=True, stop=True)
                if b % 2:
                    mm.then_inc(hq_done, 1)
            pe.wait_ge(w14_ready, 1)
            pe.wait_ge(hq_ready, NB)
            for t in range(NT):
                o = PS[:, 4 + t // TPB, bass.ts(t % TPB, P)]
                pe.matmul(o, k.XT[:, bass.ts(t, P)], w14[:, t // 2, :], start=True, stop=False)
                pe.matmul(o, HQ[:, bass.ts(t, P)], k.Wqv[:, 1, :], start=False, stop=False)
                mm = pe.matmul(o, F3[:, bass.ts(t, P)], k.Wqv[:, 2, :], start=False, stop=True)
                if t % TPB == TPB - 1:
                    mm.then_inc(out_done, 1)



class Step:

    def __init__(self, gate, up, down, bias=0.0, spread=None, fresh=True):
        self.gate, self.up, self.down, self.bias = gate, up, down, bias
        self.spread, self.fresh = spread, fresh
        self.rows = gate.shape[1]


class Experts:

    GATE, UP, SPREAD, ACC, TURN = 0, 2, 4, 6, 7

    def __init__(self, k, name, passes, func, loaded):
        self.k, self.passes, self.func, self.loaded = k, passes, func, loaded
        self.gate_ready = k.sem(f"{name}_gate_ready")
        self.acted = k.sem(f"{name}_acted")
        self.up_ready = k.sem(f"{name}_up_ready")
        self.multiplied = k.sem(f"{name}_multiplied")
        self.spread_ready = k.sem(f"{name}_spread_ready")
        self.hidden_ready = k.sem(f"{name}_hidden_ready")
        self.down_done = k.sem(f"{name}_down_done")
        self.acc_read = k.sem(f"{name}_acc_read")
        self.out_turned = k.sem(f"{name}_out_turned")
        self.out_added = k.sem(f"{name}_out_added")
        self.paced = k.sem(f"{name}_paced")
        W = k.RW
        self.A = [W[:, bass.ts(s, BLK)] for s in range(2)]
        self.M = [W[:, bass.ts(2 + s, BLK)] for s in range(2)]
        self.HID = [W[:, bass.ts(4 + s, BLK)] for s in range(2)]
        self.OT = W[:, bass.ts(6, BLK)]
        self.K = len(passes[0])
        self.no, self.last, n = [], {}, -1
        for c, st in enumerate(passes[0]):
            n += st.spread is not None and st.fresh
            self.no.append(n)
            if st.spread is not None:
                self.last[n] = c
        self.KS = n + 1


def experts_tensor(pe, e, WT, extra=None):
    k, K, PS = e.k, e.K, e.k.PS

    def down(j, c, st):
        pe.wait_ge(e.hidden_ready, j * K + c + 1)
        pe.matmul(PS[:, e.ACC, :], st.down, e.HID[c % 2][0:st.rows, :], start=(c == 0 and extra is None),
                  stop=(c == K - 1)).then_inc(e.down_done, 1)

    for g, steps in enumerate(e.passes):
        with pe.Fori(0, NB) as i:
            j = i + g * NB
            x = k.XT[:, bass.ts(i, BLK)]
            if extra is not None:
                extra(pe, i)
            for c, st in enumerate(steps):
                m = j * K + c
                if c >= 2:
                    pe.wait_ge(e.acted, m - 1)
                if st.rows < P:
                    pe.sem_inc(e.paced, 1)
                pe.matmul(PS[0:st.rows, e.GATE + c % 2, :], st.gate, x, start=True,
                          stop=True).then_inc(e.gate_ready, 1)
                if st.up is not None:
                    if c >= 2:
                        pe.wait_ge(e.multiplied, m - 1)
                    if st.rows < P:
                        pe.sem_inc(e.paced, 1)
                    pe.matmul(PS[0:st.rows, e.UP + c % 2, :], st.up, x, start=True,
                              stop=True).then_inc(e.up_ready, 1)
                if st.spread is not None and st.fresh:
                    n = e.no[c]
                    if n >= 2:
                        pe.wait_ge(e.hidden_ready, j * K + e.last[n - 2] + 1)
                    sel, group = st.spread
                    if n >= 2 and sel.shape[0] <= 32:
                        pe.sem_inc(e.paced, 1)
                    pe.matmul(PS[:, e.SPREAD + n % 2, :], sel, WT[:, group, bass.ts(i, BLK)], start=True,
                              stop=True).then_inc(e.spread_ready, 1)
                if c >= 1:
                    down(j, c - 1, steps[c - 1])
            down(j, K - 1, steps[K - 1])
            pe.wait_ge(e.acc_read, j + 1)
            for r in range(TPB):
                mm = pe.transpose(PS[:, e.TURN, bass.ts(r, P)], e.OT[:, bass.ts(r, P)], k.identf[:])
            mm.then_inc(e.out_turned, 1)


def experts_scalar(act, e):
    PS, K = e.k.PS, e.K
    act.preload_act_table(e.func)
    for g, steps in enumerate(e.passes):
        with act.Fori(0, NB) as i:
            j = i + g * NB
            for c, st in enumerate(steps):
                m = j * K + c
                act.wait_ge(e.gate_ready, m + 1)
                if c >= 2:
                    act.wait_ge(e.hidden_ready, m - 1)
                act.activation(e.A[c % 2][0:st.rows, :], PS[0:st.rows, e.GATE + c % 2, :], e.func,
                               bias=st.bias).then_inc(e.acted, 1)
            act.wait_ge(e.down_done, (j + 1) * K)
            act.activation(e.OT, PS[:, e.ACC, :], ACT.Copy).then_inc(e.acc_read, 1)


def experts_vector(dve, e):
    k, PS, K = e.k, e.k.PS, e.K
    for g, steps in enumerate(e.passes):
        with dve.Fori(0, NB) as i:
            j = i + g * NB
            for c, st in enumerate(steps):
                m = j * K + c
                rows = slice(0, st.rows)
                a, hid = e.A[c % 2][rows, :], e.HID[c % 2][rows, :]
                dve.wait_ge(e.acted, m + 1)
                if c >= 2:
                    dve.wait_ge(e.down_done, m - 1)
                if st.up is not None:
                    dve.wait_ge(e.up_ready, m + 1)
                    if st.spread is None:
                        dve.tensor_tensor(hid, a, PS[rows, e.UP + c % 2, :], ALU.mult).then_inc(e.multiplied, 1)
                        dve.wait_ge(e.multiplied, m + 1)
                        dve.sem_inc(e.hidden_ready, 1)
                        continue
                    dve.tensor_tensor(e.M[c % 2], a, PS[:, e.UP + c % 2, :], ALU.mult).then_inc(e.multiplied, 1)
                    dve.wait_ge(e.multiplied, m + 1)
                    a = e.M[c % 2]
                dve.wait_ge(e.spread_ready, j * e.KS + e.no[c] + 1)
                dve.tensor_tensor(hid, a, PS[:, e.SPREAD + e.no[c] % 2, :], ALU.mult).then_inc(e.hidden_ready, 1)
            dve.wait_ge(e.out_turned, j + 1)
            x = k.X[:, bass.ts(i, TPB), :].rearrange("p t d -> p (t d)")
            dve.tensor_tensor(x, x, PS[:, e.TURN, :], ALU.add).then_inc(e.out_added, 1)



class Route:

    LOGITS = 4

    def __init__(self, k, name, experts, groups):
        self.k, self.E, self.G, self.R = k, experts, groups, NT * groups
        n = NT * groups * experts
        RB = k.RB
        self.rows = lambda at: RB[:, at:at + n].rearrange("p (r e) -> p r e", e=experts)
        self.L, self.W, self.T1, self.T2 = (self.rows(at) for at in (0, 1024, 2048, 3072))
        self.parts = RB[:, 4096:4096 + n * PARTS // 2].bitcast(BF16).rearrange(
            "p (r a e) -> p r a e", a=PARTS, e=experts)
        self.top = RB[:, 5632:5632 + 8 * self.R].rearrange("p (r j) -> p r j", j=8)
        self.at = RB[:, 5888:5888 + 8 * self.R].bitcast(U32).rearrange("p (r j) -> p r j", j=8)
        self.z = RB[:, 6144:6144 + self.R]
        self.rz = RB[:, 6208:6208 + self.R]
        self.WT = RB[0:PARTS * experts, 6272:6272 + groups * T // 2].bitcast(BF16).rearrange(
            "p (g t) -> p g t", g=groups)
        self.WT32 = RB[0:experts, 8320:8320 + T]
        self.logits_ready = k.sem(f"{name}_logits_ready")
        self.shifted = k.sem(f"{name}_route_shifted")
        self.exped = k.sem(f"{name}_route_exped")
        self.parts_ready = k.sem(f"{name}_parts_ready")
        self.parts_turned = k.sem(f"{name}_parts_turned")
        self.wt_ready = k.sem(f"{name}_wt_ready")
        self.logits = k.PS[:, self.LOGITS:self.LOGITS + 2, :].rearrange("p a f -> p (a f)")[:, 0:n]
        self.NWT = 2 * groups


def route_logits(pe, k, r, nm, gate):
    pe.wait_ge(nm.xt_ready, NB)
    w = r.G * r.E
    for t in range(NT):
        mm = pe.matmul(r.logits[:, bass.ts(t, w)], k.XT[:, bass.ts(t, P)], gate, start=True, stop=True)
    mm.then_inc(r.logits_ready, 1)


def route_top2(dve, k, r, own, bias, renormalise):
    dve.wait_ge(r.logits_ready, 1)
    lg = r.logits.rearrange("p (r e) -> p r e", e=r.E)
    if bias is None:
        own.settle(dve.tensor_copy(r.L, lg))
    else:
        own.settle(dve.tensor_tensor(r.L, lg, over(bias, 1, r.R), ALU.add))
    for j in range(r.R):
        own.mark(dve.max(r.top[:, j, :], r.L[:, j, :]))
    own.wait()
    dve.tensor_tensor(r.W, r.L, r.top[:, :, 0:1].broadcast_to([P, r.R, r.E]), ALU.subtract).then_inc(r.shifted, 1)
    for j in range(r.R):
        own.mark(dve.max_index(r.at[:, j, :], r.top[:, j, :], r.L[:, j, :]))
    own.wait()
    iota = over(k.iota[:, 0:r.E], 1, r.R)
    own.mark(dve.tensor_tensor(r.T1, iota, r.at[:, :, 0:1].broadcast_to([P, r.R, r.E]), ALU.is_equal))
    own.settle(dve.tensor_tensor(r.T2, iota, r.at[:, :, 1:2].broadcast_to([P, r.R, r.E]), ALU.is_equal))
    own.settle(dve.tensor_tensor(r.T1, r.T1, r.T2, ALU.add))
    dve.wait_ge(r.exped, 1)
    if not renormalise:
        own.settle(dve.tensor_reduce(r.z, r.W, AX.X, ALU.add))
    own.settle(dve.tensor_tensor(r.W, r.W, r.T1, ALU.mult))
    if renormalise:
        own.settle(dve.tensor_reduce(r.z, r.W, AX.X, ALU.add))
    own.settle(dve.reciprocal(r.rz, r.z))
    if not renormalise:
        own.settle(dve.tensor_scalar(r.rz, r.rz, 0.5, None, ALU.mult))
    own.settle(dve.tensor_tensor(r.W, r.W, over(r.rz, 2, r.E), ALU.mult))
    route_parts(dve, r, own)


def route_parts(dve, r, own):
    own.settle(dve.tensor_copy(r.parts[:, :, 0, :], r.W))
    own.settle(dve.tensor_tensor(r.T1, r.W, r.parts[:, :, 0, :], ALU.subtract))
    own.settle(dve.tensor_copy(r.parts[:, :, 1, :], r.T1))
    own.settle(dve.tensor_tensor(r.T1, r.T1, r.parts[:, :, 1, :], ALU.subtract))
    dve.tensor_copy(r.parts[:, :, 2, :], r.T1).then_inc(r.parts_ready, 1)


def route_exp(act, r):
    act.wait_ge(r.shifted, 1)
    act.activation(r.W, r.W, ACT.Exp).then_inc(r.exped, 1)


def route_turn(pe, k, r, whole=False):
    pe.wait_ge(r.parts_ready, 1)
    n = PARTS * r.E
    for g in range(r.G):
        for t in range(NT):
            mm = pe.transpose(k.PB[0:n, 2 * g + t // 8, bass.ts(t % 8, P)],
                              r.parts[:, t * r.G + g, :, :].rearrange("p a e -> p (a e)"), k.identb[:])
    if whole:
        for t in range(NT):
            mm = pe.transpose(k.PS[0:r.E, 4 + t // TPB, bass.ts(t % TPB, P)], r.W[:, t, :], k.identf[:])
    mm.then_inc(r.parts_turned, 1)


def route_store(act, k, r, whole=False):
    act.wait_ge(r.parts_turned, 1)
    n = PARTS * r.E
    for g in range(r.G):
        for h in range(2):
            act.activation(r.WT[:, g, bass.ts(h, T // 2)], k.PB[0:n, 2 * g + h, :], ACT.Copy).then_inc(r.wt_ready, 1)
    if whole:
        for q in range(NB):
            act.activation(r.WT32[:, bass.ts(q, BLK)], k.PS[0:r.E, 4 + q, :], ACT.Copy).then_inc(r.wt_ready, 1)



def gelu_experts(k):
    nm, r = Norm(k, "l0f", k.X), Route(k, "l0f", E0, 1)
    steps = [Step(k.W1_0[:, e, bass.ts(f, P)], None, k.W2_0[:, e, f, :], bias=k.col("b1_0", e * K0 + f),
                  spread=(k.one_sel[:, e, :], 0), fresh=(f == 0)) for e in range(E0) for f in range(K0)]
    ex = Experts(k, "l0f", [steps], ACT.Gelu, (k.l0f_loaded, 64))
    vec = k.sem("l0f_vector")

    def bias2(pe, i):
        pe.matmul(k.PS[:, ex.ACC, :], k.b2_0, r.WT32[:, bass.ts(i, BLK)], start=True, stop=False)

    with k.nc.Block() as block:

        @block.gpsimd
        def _(pool):
            k.clear_last(pool)

        @block.vector
        def _(dve):
            own = Tally(dve, vec)
            norm_vector(dve, k, nm, own)
            route_top2(dve, k, r, own, k.row("gate_b"), renormalise=True)
            experts_vector(dve, ex)

        @block.scalar
        def _(act):
            norm_scalar(act, k, nm)
            route_exp(act, r)
            route_store(act, k, r, whole=True)
            experts_scalar(act, ex)

        @block.tensor
        def _(pe):
            norm_tensor(pe, k, nm)
            pe.wait_ge(k.l0f_loaded, 64)
            route_logits(pe, k, r, nm, k.gw0)
            route_turn(pe, k, r, whole=True)
            pe.wait_ge(r.wt_ready, r.NWT + NB)
            experts_tensor(pe, ex, r.WT, extra=bias2)



class Heads:

    def __init__(self, name, chunks, wq, wk, wv, wo, bq, bk, bv, scale, head_mask, QT, VT,
                 mask=None, per_tile=False):
        self.name, self.chunks = name, chunks
        self.wq, self.wk, self.wv, self.wo = wq, wk, wv, wo
        self.bq, self.bk, self.bv, self.scale = bq, bk, bv, scale
        self.head_mask, self.QT, self.VT = head_mask, QT, VT
        self.mask, self.per_tile = mask, per_tile


def heads_attention(k, hd, bias_row, weights_loaded, before=None, after=None):
    nc, PS = k.nc, k.PS
    nm = Norm(k, hd.name, k.X)
    target = k.XN if after else k.X
    s = lambda what: k.sem(f"{hd.name}_{what}")
    vec = s("vector")
    k_ready, k_masked, v_ready, v_biased = s("k_ready"), s("k_masked"), s("v_ready"), s("v_biased")
    v_spread, vw_ready, vw_stored = s("v_spread"), s("vw_ready"), s("vw_stored")
    q_ready, q_stored, score_ready, shifted = s("q_ready"), s("q_stored"), s("score_ready"), s("shifted")
    exped, summed, normed, p_turned, p_stored = s("exped"), s("summed"), s("normed"), s("p_turned"), s("p_stored")
    out_ready, out_added, biased = s("out_ready"), s("out_added"), s("biased")

    NC, HPC = hd.chunks, H // hd.chunks
    Kall = k.RB[:, 0:8192].rearrange("p (b h c) -> p b h c", b=B, h=H)
    Kflat = k.RB[:, 0:8192].rearrange("p (b n) -> p b n", b=B)
    VW = k.RB[:, 8192:16384].rearrange("p (b c n) -> p b c n", b=B, n=D)
    VWflat = k.RB[:, 8192:16384].rearrange("p (b n) -> p b n", b=B)
    SS = [k.RW[:, bass.ts(r, HC)] for r in range(2)]
    PT = k.RW[:, 2 * HC:3 * HC]
    VM = SS
    small = k.RW[:, 3 * HC:]
    top = [small[:, 512 + 16 * r:528 + 16 * r] for r in range(2)]
    tot = [small[:, 544 + 16 * r:560 + 16 * r] for r in range(2)]
    rec = [small[:, 576 + 16 * r:592 + 16 * r] for r in range(2)]
    PTB, OUT, Q = 4, 6, 7
    score = [PS[:, 2 * r:2 * r + 2, :].rearrange("p a f -> p (a f)") for r in range(2)]
    vw_ps = [PS[:, 4 + 2 * r:6 + 2 * r, :].rearrange("p a f -> p (a f)") for r in range(2)]
    turn_ps = PS[:, PTB:PTB + 2, :].rearrange("p a f -> p (a f)")
    JOBS = max(1, NC // 2)
    CPJ = NC // JOBS

    with nc.Block() as block:

        if before is not None:
            @block.sync
            def _(sp):
                before(sp)

        @block.vector
        def _(dve):
            own = Tally(dve, vec)
            for c in range(NC):
                dve.wait_ge(k_ready, c + 1)
                kc = PS[:, 4 + c % 2, :].rearrange("p (b c) -> p b c", b=B)
                for h in range(HPC):
                    ins = dve.tensor_scalar(Kall[:, :, c * HPC + h, :], kc, hd.bk(c), hd.head_mask[:, h:h + 1],
                                            ALU.add, ALU.mult)
                ins.then_inc(k_masked, 1)
            dve.wait_ge(v_biased, NC)

            def spread_values(b, r):
                if known(b, 2):
                    dve.wait_ge(vw_ready, b - 1)
                if NC == 1:
                    v = over(hd.VT[:, 0, bass.ts(b, C)], 1, H)
                    m = over(hd.head_mask, 2, C)
                    o = VM[r].rearrange("p (h c) -> p h c", c=C)
                else:
                    v = over(hd.VT[:, :, bass.ts(b, C)], 2, HPC)
                    m = over(over(hd.head_mask, 1, NC), 3, C)
                    o = VM[r].rearrange("p (n h c) -> p n h c", h=HPC, c=C)
                dve.tensor_tensor(o, v, m, ALU.mult).then_inc(v_spread, 1)

            rolled(dve, B, 2, spread_values)
            norm_vector(dve, k, nm, own)
            dve.wait_ge(biased, 1)
            dve.wait_ge(vw_ready, B)

            def add_out(n):
                dve.wait_ge(out_ready, n + 1)
                x = target[:, n, :]
                dve.tensor_tensor(x, x, PS[:, OUT, 0:D], ALU.add).then_inc(out_added, 1)

            def total(n, r):
                dve.wait_ge(exped, n + 1)
                own.settle(dve.tensor_reduce(tot[r], SS[r].rearrange("p (h c) -> p h c", c=C), AX.X, ALU.add))
                dve.reciprocal(rec[r], tot[r]).then_inc(summed, 1)

            def step(n, r):
                r = r % 2
                dve.wait_ge(score_ready, n + 1)
                sv = score[r].rearrange("p (h c) -> p h c", c=C)
                own.settle(dve.tensor_reduce(top[r], sv, AX.X, ALU.max))
                dve.tensor_tensor(SS[r].rearrange("p (h c) -> p h c", c=C), sv, over(top[r], 2, C),
                                  ALU.subtract).then_inc(shifted, 1)
                if known(n, 3):
                    add_out(n - 3)
                if known(n, 1):
                    total(n - 1, 1 - r)

            for n in range(4):
                step(n, n)
            with dve.Fori(1, NT // 4) as i:
                own.enter(i - 1, 8)
                for r in range(4):
                    step(i * 4 + r, r)
            own.leave(NT // 4 - 1)
            total(NT - 1, 1)
            for n in range(NT - 3, NT):
                add_out(n)
            if after:
                after.vector(dve, own, out_added)

        @block.scalar
        def _(act):
            for c in range(NC):
                act.wait_ge(v_ready, c + 1)
                act.activation(hd.VT[:, c, :], PS[:, 6 + c % 2, :], ACT.Identity, bias=hd.bv(c)).then_inc(v_biased, 1)
            with act.Fori(0, B // 2) as i:
                for r in range(2):
                    b = i * 2 + r
                    act.wait_ge(vw_ready, b + 1)
                    act.activation(VWflat[:, b, :], vw_ps[r], ACT.Copy).then_inc(vw_stored, 1)
            norm_scalar(act, k, nm)

            def store_q(b, slot, j):
                act.wait_ge(q_ready, b * JOBS + j + 1)
                for c in range(CPJ):
                    ins = act.activation(hd.QT[slot][:, j * CPJ + c, :], PS[:, Q, bass.ts(c, S)], ACT.Identity,
                                         bias=hd.bq(j * CPJ + c))
                ins.then_inc(q_stored, 1)

            def exp(n, r):
                act.wait_ge(shifted, n + 1)
                act.activation(SS[r], SS[r], ACT.Exp, scale=hd.scale).then_inc(exped, 1)

            def step(n, r, ahead):
                if not isinstance(n, int) or n + 1 < NT:
                    exp(n + 1, (r + 1) % 2)
                act.wait_ge(p_turned, n + 1)
                if known(n, 1):
                    act.wait_ge(out_ready, n)
                act.activation(PT, turn_ps, ACT.Copy).then_inc(p_stored, 1)
                for b, slot, j in ahead:
                    store_q(b, slot, j)

            for b in range(2):
                for j in range(JOBS):
                    store_q(b, b, j)
            exp(0, 0)
            attention_steps(act, step, JOBS)
            if after:
                after.scalar(act)

        @block.gpsimd
        def _(pool):
            k.clear_last(pool)
            pool.wait_ge(nm.xn_ready, NT)
            if after:
                pool.wait_ge(nm.xt_turned, NB)
            pool.tensor_tensor(target[:], target[:], over(k.row(bias_row), 1, NT), ALU.add).then_inc(biased, 1)
            with pool.Fori(0, NT // 2) as i:
                for r in range(2):
                    pool.wait_ge(summed, i * 2 + r + 1)
                    sv = SS[r].rearrange("p (h c) -> p h c", c=C)
                    pool.tensor_tensor(sv, sv, over(rec[r], 2, C), ALU.mult).then_inc(normed, 1)
            if after:
                after.gpsimd(pool)

        @block.tensor
        def _(pe):
            for sm, n in weights_loaded:
                pe.wait_ge(sm, n)
            for c in range(NC):
                if c >= 2:
                    pe.wait_ge(k_masked, c - 1)
                pe.matmul(PS[:, 4 + c % 2, :], hd.wk(c), k.ctxT[:], start=True, stop=True).then_inc(k_ready, 1)
                if c >= 2:
                    pe.wait_ge(v_biased, c - 1)
                pe.matmul(PS[:, 6 + c % 2, :], hd.wv(c), k.ctxT[:], start=True, stop=True).then_inc(v_ready, 1)
            pe.wait_ge(k_masked, NC)
            pe.wait_ge(v_biased, NC)

            def value_products(b, r):
                pe.wait_ge(v_spread, b + 1)
                if known(b, 2):
                    pe.wait_ge(vw_stored, b - 1)
                for c in range(8):
                    mm = pe.matmul(vw_ps[r][:, bass.ts(c, D)], VM[r][:, bass.ts(c, P)], hd.wo(c),
                                   start=True, stop=True)
                mm.then_inc(vw_ready, 1)

            rolled(pe, B, 2, value_products)
            norm_tensor(pe, k, nm)
            pe.wait_ge(vw_stored, B)
            pe.wait_ge(nm.xt_ready, NB)

            def make_q(b, slot, j):
                pe.wait_ge(q_stored, b * JOBS + j)
                for c in range(CPJ):
                    mm = pe.matmul(PS[:, Q, bass.ts(c, S)], hd.wq(j * CPJ + c), k.XT[:, bass.ts(b, S)],
                                   start=True, stop=True)
                mm.then_inc(q_ready, 1)

            def scores(n, b, r):
                pe.wait_ge(q_stored, (b + 1) * JOBS)
                q = lambda c, slot=r // 2: hd.QT[slot][:, c, bass.ts(r % 2, P)]
                to = score[r % 2]
                masked = hd.mask is not None
                if NC == 1:
                    for half in range(2):
                        mm = pe.matmul(to[:, bass.ts(half, BLK)], q(0), Kflat[:, b, bass.ts(half, BLK)],
                                       start=True, stop=not masked)
                        if masked:
                            m = hd.mask[:, r % 2, :] if hd.per_tile else hd.mask[:, b, :]
                            mm = pe.matmul(to[:, bass.ts(half, BLK)].rearrange("p (h c) -> p h c", c=C),
                                           k.identb[:], over(m, 1, H // 2), start=False, stop=True)
                else:
                    for c in range(NC):
                        mm = pe.matmul(to[:, bass.ts(c, P)], q(c), Kflat[:, b, bass.ts(c, P)], start=True, stop=True)
                mm.then_inc(score_ready, 1)

            def turn(n, r):
                pe.wait_ge(normed, n + 1)
                if known(n, 1):
                    pe.wait_ge(p_stored, n)
                for c in range(8):
                    mm = pe.transpose(turn_ps[:, bass.ts(c, P)], SS[r % 2][:, bass.ts(c, P)], k.identf[:])
                mm.then_inc(p_turned, 1)

            def output(n, b):
                pe.wait_ge(p_stored, n + 1)
                if known(n, 1):
                    pe.wait_ge(out_added, n)
                for c in range(8):
                    mm = pe.matmul(PS[:, OUT, 0:D], PT[:, bass.ts(c, P)], VW[:, b, c, :], start=(c == 0), stop=(c == 7))
                mm.then_inc(out_ready, 1)

            def step(n, r, ahead):
                turn(n, r)
                ahead = list(ahead)
                if ahead:
                    make_q(*ahead[0])
                if known(n, 1):
                    output(n - 1, step.b0 + (r - 1) // 2)
                for job in ahead[1:]:
                    make_q(*job)
                if not isinstance(n, int) or n + 2 < NT:
                    scores(n + 2, step.b0 + (r + 2) // 2, (r + 2) % 4)

            for b in range(2):
                for j in range(JOBS):
                    make_q(b, b, j)
            scores(0, 0, 0)
            scores(1, 0, 1)
            attention_steps(pe, step, JOBS)
            output(NT - 1, B - 1)


def attention_steps(eng, step, jobs):
    def ahead(b, r):
        share = range(0, (jobs + 1) // 2) if r % 2 == 0 else range((jobs + 1) // 2, jobs)
        return [(b + 2 + r // 2, r // 2, j) for j in share]

    for n in range(4):
        step.b0 = 0
        step(n, n, ahead(0, n))
    with eng.Fori(1, NT // 4 - 1) as i:
        step.b0 = i * 2
        for r in range(4):
            step(i * 4 + r, r, ahead(i * 2, r))
    for r in range(4):
        step.b0 = B - 2
        step(NT - 4 + r, r, [])


def narrow_attention(k, n, wa, mask, per_tile, before=None):
    place = k.RW[:, 3 * HC:3 * HC + 512]
    QT = [place[:, bass.ts(r, S)].rearrange("p (c q) -> p c q", c=1) for r in range(2)]
    VT = k.RW[:, 2 * HC:2 * HC + B * C].rearrange("p (c n) -> p c n", c=1)
    hd = Heads(f"l{n}x", 1, lambda c: wa[:, 0, :], lambda c: wa[:, 1, :], lambda c: wa[:, 2, :], lambda c: wa[:, 3, :],
               lambda c: k.col(f"bq{n}"), lambda c: k.col(f"bk{n}"), lambda c: k.col(f"bv{n}"),
               (D // H) ** -0.5, k.head16[:], QT, VT, mask, per_tile)
    heads_attention(k, hd, f"bo{n}", [(k.att_loaded, 64), (k.masks_made, 2)], before)


def attention_1(k):
    narrow_attention(k, 1, k.Wa[0], k.mask1_add, True)



def product_keys(k):
    nc, PS, RA, RB, RC = k.nc, k.PS, k.RA, k.RB, k.RC
    nm = Norm(k, "l1f", k.X)
    s = lambda what: k.sem(f"l1f_{what}")
    vec, paced = s("vector"), s("paced")
    wf_ready, wf_stored, bn_var, bn_std, bn_ready = s("wf_ready"), s("wf_stored"), s("bn_var"), s("bn_std"), s("bn_ready")
    z_ready, z_stored = s("z_ready"), s("z_stored")
    xb_ready, s_ready, s_stored, top_done = s("xb_ready"), s("s_ready"), s("s_stored"), s("top_done")
    a_pool, a_vector, sig_ready, g_ready, g_turned = s("a_pool"), s("a_vector"), s("sig_ready"), s("g_ready"), s("g_turned")
    m_ready, out_ready, out_added = s("m_ready"), s("out_ready"), s("out_added")

    w_q = RC[:, 0:2048].rearrange("p (n d) -> p n d", n=2 * NH)
    keysT = RC[:, 2048:2560].rearrange("p (n c) -> p n c", n=2 * NH)
    downT = RC[:, 2560:3584].rearrange("p (n c) -> p n c", n=8)
    up = RC[:, 3584:4608].rearrange("p (n c) -> p n c", n=8)
    Wf = RC[:, 4608:5120]
    zT = RB[:, :].rearrange("p (n t) -> p n t", n=8)
    A = [RA[:, bass.ts(h, NE)] for h in range(NH)]
    SG = [RA[:, bass.ts(8 + r, NE)] for r in range(4)]
    Ssb = [k.RW[:, bass.ts(r, 512)] for r in range(2)]
    M = [k.RW[:, bass.ts(1 + r, 1024)] for r in range(2)]
    xb = [k.RW[:, bass.ts(24 + r, P)] for r in range(2)]
    cand = k.RW[:, 3328:3840]
    t8 = k.RW[:, 3840:3968].rearrange("p (n j) -> p n j", j=8)
    v8 = k.RW[:, 3968:4032].rearrange("p (n j) -> p n j", j=8)
    bn = k.stats[:].rearrange("p t s -> p (t s)")
    mv, bstd, brstd, scale, shift, tmp = (k.mom[:, j, 0:2] for j in range(6))
    SP, GT, OUT, WF = 0, 1, 5, 7
    gt = [PS[:, GT + 2 * r:GT + 2 * r + 2, :].rearrange("p a f -> p (a f)") for r in range(2)]
    ON_VECTOR = 2
    ON_POOL = NH - ON_VECTOR

    def pair_scores(r, h):
        s0 = over(Ssb[r][:, bass.ts(h, NK)], 2, NK)
        s1 = over(Ssb[r][:, bass.ts(NH + h, NK)], 1, NK)
        return A[h].rearrange("p (a b) -> p a b", a=NK), s0, s1

    with nc.Block() as block:

        @block.vector
        def _(dve):
            own = Tally(dve, vec)
            norm_vector(dve, k, nm, own)
            for q in range(NB):
                dve.wait_ge(nm.xt_ready, q + 1)
                own.mark(dve.bn_stats(bn[:, bass.ts(q, 6)], k.XT[:, bass.ts(q, BLK)]))
            own.wait()
            dve.bn_aggr(mv, bn[:, 0:24]).then_inc(bn_var, 1)
            dve.wait_ge(bn_std, 1)
            own.settle(dve.reciprocal(brstd[:, 0:1], bstd[:, 0:1]))
            own.settle(dve.tensor_tensor(scale[:, 0:1], brstd[:, 0:1], k.col("gamma"), ALU.mult))
            own.settle(dve.tensor_tensor(tmp[:, 0:1], scale[:, 0:1], mv[:, 0:1], ALU.mult))
            dve.tensor_tensor(shift[:, 0:1], k.col("beta"), tmp[:, 0:1], ALU.subtract).then_inc(bn_ready, 1)

            def picks(n, r):
                dve.wait_ge(s_stored, n + 1)
                dve.sem_inc(paced, 1)
                for j in range(2 * NH):
                    own.mark(dve.max(t8[:, j, :], Ssb[r][:, bass.ts(j, NK)]))
                own.wait()
                own.settle(dve.tensor_tensor(cand.rearrange("p (h a b) -> p h a b", h=NH, a=8),
                                             over(t8[:, 0:NH, :], 3, 8), over(t8[:, NH:, :], 2, 8), ALU.add))
                dve.sem_inc(paced, 1)
                for h in range(NH):
                    own.mark(dve.max(v8[:, h, :], cand[:, bass.ts(h, 64)]))
                own.wait()
                for h in range(ON_POOL, NH):
                    if known(n, 1):
                        dve.wait_ge(g_turned, n * NH)
                    dve.tensor_tensor(*pair_scores(r, h), ALU.add).then_inc(a_vector, 1)

            def weigh(n, r):
                dve.wait_ge(g_turned, (n + 1) * NH)
                if known(n, 2):
                    dve.wait_ge(out_ready, n - 1)
                dve.tensor_tensor(M[r].rearrange("p (c t) -> p c t", c=8), gt[r].rearrange("p (c t) -> p c t", c=8),
                                  zT[:, :, bass.ts(n, P)], ALU.mult).then_inc(m_ready, 1)

            def add_out(n):
                dve.wait_ge(out_ready, n + 1)
                dve.tensor_tensor(k.X[:, n, :], k.X[:, n, :], PS[:, OUT, 0:D], ALU.add).then_inc(out_added, 1)

            def step(n, r):
                picks(n, r)
                if known(n, 1):
                    weigh(n - 1, 1 - r)
                for h in range(NH):
                    dve.wait_ge(sig_ready, n * NH + h + 1)
                    if h >= ON_POOL:
                        dve.wait_ge(a_vector, n * ON_VECTOR + h - ON_POOL + 1)
                    dve.scalar_tensor_tensor(A[h], A[h], v8[:, h, 7:8], SG[h % 4], ALU.is_ge,
                                             ALU.mult).then_inc(g_ready, 1)
                if known(n, 1):
                    add_out(n - 1)

            per = 2 * NH + 1 + NH
            for n in range(2):
                step(n, n)
            with dve.Fori(1, NT // 2) as i:
                own.enter(i - 1, 2 * per)
                for r in range(2):
                    step(i * 2 + r, r)
            own.leave(NT // 2 - 1)
            dve.wait_ge(z_stored, 8 * NB)
            weigh(NT - 1, 1)
            add_out(NT - 1)

        @block.scalar
        def _(act):
            act.wait_ge(wf_ready, 1)
            act.activation(Wf, PS[:, WF, :], ACT.Copy).then_inc(wf_stored, 1)
            norm_scalar(act, k, nm)
            act.wait_ge(bn_var, 1)
            act.activation(bstd[:, 0:1], mv[:, 1:2], ACT.Sqrt, bias=k.eps[:, 0:1]).then_inc(bn_std, 1)
            act.preload_act_table(ACT.Gelu)
            with act.Fori(0, NB) as i:
                for c in range(8):
                    act.wait_ge(z_ready, i * 8 + c + 1)
                    act.activation(zT[:, c, bass.ts(i, BLK)], PS[:, c, :], ACT.Gelu).then_inc(z_stored, 1)
            act.wait_ge(bn_ready, 1)
            act.preload_act_table(ACT.Sigmoid)

            def batch_normed(n, r):
                if known(n, 2):
                    act.wait_ge(s_ready, n - 1)
                act.activation(xb[r], k.XT[:, bass.ts(n, P)], ACT.Identity, bias=shift[:, 0:1],
                               scale=scale[:, 0:1]).then_inc(xb_ready, 1)

            def store_s(n, r):
                act.wait_ge(s_ready, n + 1)
                if known(n, 2):
                    act.wait_ge(a_pool, (n - 1) * ON_POOL)
                    act.wait_ge(a_vector, (n - 1) * ON_VECTOR)
                act.activation(Ssb[r], PS[:, SP, :], ACT.Copy).then_inc(s_stored, 1)

            def sigmoid(n, h):
                if h < ON_POOL:
                    act.wait_ge(a_pool, n * ON_POOL + h + 1)
                else:
                    act.wait_ge(a_vector, n * ON_VECTOR + h - ON_POOL + 1)
                if known(n, 1) or h >= 4:
                    act.wait_ge(g_ready, n * NH + h - 3)
                act.activation(SG[h % 4], A[h], ACT.Sigmoid).then_inc(sig_ready, 1)

            def step(n, r):
                for h in range(4):
                    sigmoid(n, h)
                if not isinstance(n, int) or n + 1 < NT:
                    store_s(n + 1, 1 - r)
                if not isinstance(n, int) or n + 2 < NT:
                    batch_normed(n + 2, r)
                for h in range(4, NH):
                    sigmoid(n, h)

            batch_normed(0, 0)
            batch_normed(1, 1)
            store_s(0, 0)
            run_steps(act, NT, 2, step)

        @block.gpsimd
        def _(pool):
            k.clear_last(pool)

            def step(n, r):
                pool.wait_ge(s_stored, n + 1)
                for h in range(ON_POOL):
                    if known(n, 1):
                        pool.wait_ge(g_turned, (n - 1) * NH + h + 1)
                    pool.tensor_tensor(*pair_scores(r, h), ALU.add).then_inc(a_pool, 1)
            run_steps(pool, NT, 2, step)

        @block.tensor
        def _(pe):
            pe.wait_ge(k.keys_loaded, 64)
            for n in range(2 * NH):
                mm = pe.matmul(PS[:, WF, bass.ts(n, NK)], w_q[:, n, :], keysT[:, n, :], start=True, stop=True)
            mm.then_inc(wf_ready, 1)
            norm_tensor(pe, k, nm)
            pe.wait_ge(wf_stored, 1)
            pe.wait_ge(nm.xt_ready, NB)

            def project(i, _):
                for c in range(8):
                    if known(i, 1):
                        pe.wait_ge(z_stored, i * 8 + c - 7)
                    pe.matmul(PS[:, c, :], downT[:, c, :], k.XT[:, bass.ts(i, BLK)], start=True,
                              stop=True).then_inc(z_ready, 1)

            rolled(pe, NB, 1, project)
            pe.wait_ge(z_stored, 8 * NB)

            def halves(n, r):
                pe.wait_ge(xb_ready, n + 1)
                if known(n, 1):
                    pe.wait_ge(s_stored, n)
                pe.matmul(PS[:, SP, :], xb[r], Wf, start=True, stop=True).then_inc(s_ready, 1)

            def turn(n, r, h):
                pe.wait_ge(g_ready, n * NH + h + 1)
                for c in range(8):
                    mm = pe.matmul(gt[r][:, bass.ts(c, P)], A[h][:, bass.ts(c, P)], k.identf[:],
                                   start=(h == 0 and c % 4 == 0), stop=(h == NH - 1), skip_group_check=True)
                mm.then_inc(g_turned, 1)

            def output(n, r):
                pe.wait_ge(m_ready, n + 1)
                if known(n, 1):
                    pe.wait_ge(out_added, n)
                for c in range(8):
                    mm = pe.matmul(PS[:, OUT, 0:D], M[r][:, bass.ts(c, P)], up[:, c, :], start=(c == 0), stop=(c == 7))
                mm.then_inc(out_ready, 1)

            def step(n, r):
                if not isinstance(n, int) or n + 1 < NT:
                    halves(n + 1, 1 - r)
                for h in range(4):
                    turn(n, r, h)
                if known(n, 1):
                    output(n - 1, 1 - r)
                for h in range(4, NH):
                    turn(n, r, h)

            halves(0, 0)
            run_steps(pe, NT, 2, step)
            output(NT - 1, 1)


def attention_2(k):
    def load(sp):
        sp.wait_ge(k.l0f_loaded, 64)
        for g in range(2):
            for n, m in enumerate("gud"):
                sp.dma_start(k.RA[:, 6144 * g + 2048 * n:6144 * g + 2048 * (n + 1)],
                             k.dram[f"w{m}2_{g}"]).then_inc(k.l2f_loaded, 16)
    narrow_attention(k, 2, k.Wa[1], k.mask2_add, False, before=load)



def silu_experts(k):
    nm, r = Norm(k, "l2f", k.X), Route(k, "l2f", E2, 2)
    passes = []
    for g in range(2):
        w = [k.RA[:, 6144 * g + 2048 * n:6144 * g + 2048 * (n + 1)] for n in range(3)]
        passes.append([Step(w[0][:, bass.ts(c, P)], w[1][:, bass.ts(c, P)], w[2][:, bass.ts(c, D)],
                            spread=(k.pair_sel[:, c, :], g)) for c in range(PAIRS)])
    ex = Experts(k, "l2f", passes, ACT.Silu, (k.l2f_loaded, 96))
    vec = k.sem("l2f_vector")

    with k.nc.Block() as block:

        @block.sync
        def _(sp):
            sp.wait_ge(k.keys_loaded, 64)
            sp.wait_ge(k.att_loaded, 64)
            sp.dma_start(k.RC[:, 0:4096], k.dram["wg3"]).then_inc(k.l3f_loaded, 16)
            sp.dma_start(k.RC[:, 4096:8192], k.dram["wu3"]).then_inc(k.l3f_loaded, 16)
            sp.dma_start(k.RC[:, 8192:8256], k.dram["wgs3"]).then_inc(k.l3f_loaded, 16)
            sp.dma_start(k.RC[:, 8256:8320], k.dram["wus3"]).then_inc(k.l3f_loaded, 16)
            sp.dma_start(k.RC[0:FH, 8320:8448], k.dram["wds3"]).then_inc(k.l3f_loaded, 16)
            sp.wait_ge(k.l2f_loaded, 96)
            sp.wait_ge(ex.acc_read, NB)
            for n, m in enumerate("qkvo"):
                sp.dma_start(k.RA[:, bass.ts(n, 1024)], k.dram[f"w{m}3"]).then_inc(k.l3x_loaded, 16)

        @block.gpsimd
        def _(pool):
            k.clear_last(pool)

        @block.vector
        def _(dve):
            own = Tally(dve, vec)
            norm_vector(dve, k, nm, own)
            route_top2(dve, k, r, own, None, renormalise=False)
            experts_vector(dve, ex)

        @block.scalar
        def _(act):
            norm_scalar(act, k, nm)
            route_exp(act, r)
            route_store(act, k, r)
            experts_scalar(act, ex)

        @block.tensor
        def _(pe):
            norm_tensor(pe, k, nm)
            route_logits(pe, k, r, nm, k.gates[:, 0:2 * E2])
            route_turn(pe, k, r)
            pe.wait_ge(r.wt_ready, r.NWT)
            pe.wait_ge(k.l2f_loaded, 96)
            experts_tensor(pe, ex, r.WT)



class PostNorm:

    def __init__(self, k):
        self.k, self.nm, self.shifted = k, Norm(k, "l3y", k.XN, turn=False), k.sem("l3y_shifted")

    def vector(self, dve, own, out_added):
        k = self.k
        dve.wait_ge(out_added, NT)
        norm_vector(dve, k, self.nm, own)
        dve.wait_ge(self.nm.xn_ready, NT)
        own.settle(dve.tensor_tensor(k.XN[:], k.XN[:], over(k.row("ln_gamma"), 1, NT), ALU.mult))
        dve.wait_ge(self.shifted, 1)
        dve.tensor_tensor(k.X[:], k.X[:], k.XN[:], ALU.add)

    def scalar(self, act):
        norm_scalar(act, self.k, self.nm)

    def gpsimd(self, pool):
        k = self.k
        pool.tensor_tensor(k.X[:], k.X[:], over(k.row("ln_beta"), 1, NT), ALU.add).then_inc(self.shifted, 1)


def attention_3(k):
    w = [k.RA[:, bass.ts(n, 1024)] for n in range(4)]
    chunk = lambda a: lambda c: a[:, bass.ts(c, P)]
    QT = [k.RA[:, bass.ts(2 + r, 2048)].rearrange("p (c q) -> p c q", c=8) for r in range(2)]
    VT = k.RA[:, 8192:12288].rearrange("p (c n) -> p c n", c=8)
    hd = Heads("l3x", 8, chunk(w[0]), chunk(w[1]), chunk(w[2]), chunk(w[3]),
               lambda c: k.col("bq3", c), lambda c: k.col("bk3", c), lambda c: k.col("bv3", c),
               64 ** -0.5, k.head2[:], QT, VT)
    heads_attention(k, hd, "bo3", [(k.l3x_loaded, 64)], after=PostNorm(k))



def route_grouped(dve, k, r, own):
    BIG = -FAR
    full = lambda a: a.rearrange("p r e -> p (r e)")
    tokens = lambda a: full(a).rearrange("p (t e) -> p t e", e=E3)
    groups = lambda a: full(a).rearrange("p (g e) -> p g e", e=GE)
    four = lambda a: full(a).rearrange("p (t g h) -> p t g h", g=G3, h=G3)
    small = k.RB[:, 8320:8320 + 8 * NT * G3].rearrange("p (n g) -> p n g", n=8)
    best, count, second, other, total, rank, keep, low = (small[:, n, :] for n in range(8))
    pg = lambda a: a.rearrange("p (t g) -> p t g", g=G3)

    dve.wait_ge(r.exped, 1)
    own.settle(dve.tensor_tensor(tokens(r.L), tokens(r.W), over(k.row("gate_bias"), 1, NT), ALU.add))
    own.settle(dve.tensor_reduce(best, groups(r.L), AX.X, ALU.max))
    own.settle(dve.tensor_tensor(groups(r.T1), groups(r.L), over(best, 2, GE), ALU.is_equal))
    own.mark(dve.tensor_reduce(count, groups(r.T1), AX.X, ALU.add))
    own.settle(dve.scalar_tensor_tensor(full(r.T2), full(r.T1), FAR, full(r.L), ALU.mult, ALU.add))
    own.mark(dve.tensor_reduce(second, groups(r.T2), AX.X, ALU.max))
    own.settle(dve.tensor_scalar(other, count, 1.5, None, ALU.is_lt))
    own.settle(dve.scalar_tensor_tensor(other, other, FAR, best, ALU.mult, ALU.add))
    own.settle(dve.tensor_tensor(second, second, other, ALU.max))
    own.settle(dve.tensor_tensor(total, best, second, ALU.add))
    mine, others = over(pg(total), 3, G3), over(pg(total), 2, G3)
    own.mark(dve.tensor_tensor(four(r.T1), others, mine, ALU.is_gt))
    own.settle(dve.tensor_tensor(four(r.T2), others, mine, ALU.is_equal))
    own.settle(dve.tensor_tensor(full(r.T2).rearrange("p (t n) -> p t n", t=NT),
                                 full(r.T2).rearrange("p (t n) -> p t n", t=NT), over(k.before[:], 1, NT), ALU.mult))
    own.settle(dve.tensor_tensor(full(r.T1), full(r.T1), full(r.T2), ALU.add))
    own.settle(dve.tensor_reduce(rank, groups(r.T1), AX.X, ALU.add))
    own.settle(dve.tensor_scalar(low, rank, TG - 0.5, FAR, ALU.is_gt, ALU.mult))
    own.settle(dve.tensor_tensor(groups(r.T1), groups(r.L), over(low, 2, GE), ALU.add))
    for t in range(NT):
        own.mark(dve.max(r.top[:, t, :], tokens(r.T1)[:, t, :]))
    own.wait()
    for t in range(NT):
        own.mark(dve.match_replace(tokens(r.T2)[:, t, :], r.top[:, t, :], tokens(r.T1)[:, t, :], -3.0e38))
    own.wait()
    own.settle(dve.tensor_tensor(full(r.T1), full(r.T1), full(r.T2), ALU.not_equal))
    own.settle(dve.tensor_tensor(full(r.W), full(r.W), full(r.T1), ALU.mult))
    z, rz = r.z[:, 0:NT], r.rz[:, 0:NT]
    own.settle(dve.tensor_reduce(z, tokens(r.W), AX.X, ALU.add))
    own.settle(dve.tensor_scalar(z, z, 1e-20, None, ALU.add))
    own.settle(dve.reciprocal(rz, z))
    own.settle(dve.tensor_scalar(rz, rz, 2.5, None, ALU.mult))
    own.settle(dve.tensor_tensor(tokens(r.W), tokens(r.W), over(rz, 2, E3), ALU.mult))
    route_parts(dve, r, own)


def grouped_experts(k):
    nm, r = Norm(k, "l3f", k.X), Route(k, "l3f", E2, 2)
    gate, up, down = k.RC[:, 0:4096], k.RC[:, 4096:8192], k.RB[:, 12288:16384]
    steps = [Step(gate[:, bass.ts(c, P)], up[:, bass.ts(c, P)], down[:, bass.ts(c, D)],
                  spread=(k.pair_sel[:, c % PAIRS, :], c // PAIRS)) for c in range(2 * PAIRS)]
    steps.append(Step(k.RC[:, 8192:8256], k.RC[:, 8256:8320], k.RC[0:FH, 8320:8448]))
    ex = Experts(k, "l3f", [steps], ACT.Silu, (k.l3f_loaded, 80))
    vec = k.sem("l3f_vector")

    with k.nc.Block() as block:

        @block.sync
        def _(sp):
            sp.dma_start(down, k.dram["wd3"]).then_inc(k.l3d_loaded, 16)

        @block.gpsimd
        def _(pool):
            k.clear_last(pool)

        @block.vector
        def _(dve):
            own = Tally(dve, vec)
            norm_vector(dve, k, nm, own)
            route_grouped(dve, k, r, own)
            experts_vector(dve, ex)

        @block.scalar
        def _(act):
            norm_scalar(act, k, nm)
            act.wait_ge(r.logits_ready, 1)
            act.activation(r.W.rearrange("p r e -> p (r e)"), r.logits, ACT.Sigmoid).then_inc(r.exped, 1)
            route_store(act, k, r)
            experts_scalar(act, ex)

        @block.tensor
        def _(pe):
            norm_tensor(pe, k, nm)
            route_logits(pe, k, r, nm, k.gates[:, 2 * E2:2 * E2 + E3])
            route_turn(pe, k, r)
            pe.wait_ge(r.wt_ready, r.NWT)
            pe.wait_ge(k.l3f_loaded, 80)
            pe.wait_ge(k.l3d_loaded, 16)
            experts_tensor(pe, ex, r.WT)



def store(k, out, src):
    done = k.lasting_sem("out_stored")
    with k.nc.Block() as block:

        @block.sync
        def _(sp):
            ov = out.rearrange("b (j p) d -> p (b j) d", p=P)
            for q in range(4):
                sp.dma_start(ov[:, 4 * q:4 * q + 4, :], src[:, 4 * q:4 * q + 4, :]).then_inc(done, 16)
            sp.wait_ge(done, 64)


LAYERS = [similarity_attention, gelu_experts, attention_1, product_keys, attention_2, silu_experts,
          attention_3, grouped_experts]


def program(nc, dram, out):
    with ExitStack() as ctx:
        k = Core(nc, ctx, dram)
        setup(k)
        for layer in LAYERS:
            layer(k)
        store(k, out, k.X)



def layouts(v):
    import numpy as np
    a = {}
    c = lambda z: np.ascontiguousarray(z)
    ctx = v["ctx_1024"]
    a["x"] = c(v["x"].reshape(T, D))
    a["ctxT"] = c(ctx.reshape(B * C, D).T)
    a["ctxK"] = c(ctx.transpose(1, 0, 2))
    a["Wqv"] = c(v["L0_xattn_W_qv"].reshape(4, D, D).transpose(1, 0, 2))
    a["w1_0"] = c(v["L0_ffn_w1"].transpose(1, 0, 2))
    a["w2_0"] = c(v["L0_ffn_w2"].reshape(E0, K0, P, D).transpose(2, 0, 1, 3))
    a["b2_0"] = c(v["L0_ffn_b2"])
    a["gw0"] = c(v["L0_ffn_gate_w"])
    a["wa1"] = c(np.stack([v[f"L1_xattn_W{m}"].T for m in "qkvo"], axis=1))
    kv = v["L2_xattn_kv_w"]
    a["wa2"] = c(np.stack([v["L2_xattn_q_w"], kv[:, :D], kv[:, D:], v["L2_xattn_proj_w"]], axis=1))
    a["mask1"] = c(v["mask_SxS2_if1"].reshape(2, P, C).transpose(1, 0, 2))
    a["mask2"] = c(v["mask_BxS2_bk0"].reshape(1, B * C)).view(np.int32)
    a["w_q"] = c(v["L1_ffn_w_q"].reshape(2 * NH, P, D).transpose(1, 0, 2).reshape(P, 2 * NH * D))
    a["keysT"] = c(v["L1_ffn_keys_p"].transpose(3, 2, 0, 1).reshape(P, 2 * NH * NK))
    a["downT"] = c(v["L1_ffn_down"][:NE].T)
    a["up"] = c(v["L1_ffn_up"][:NE].reshape(NE // P, P, D).transpose(1, 0, 2).reshape(P, NE // P * D))
    for g in range(2):
        a[f"wg2_{g}"] = c(v[f"L2_ffn_wg{g}"].transpose(1, 0, 2).reshape(D, E2 * FH))
        a[f"wu2_{g}"] = c(v[f"L2_ffn_wu{g}"].transpose(1, 0, 2).reshape(D, E2 * FH))
        a[f"wd2_{g}"] = c(v[f"L2_ffn_wd{g}"].reshape(PAIRS, P, D).transpose(1, 0, 2).reshape(P, PAIRS * D))
    a["router2"] = c(np.concatenate([v["L2_ffn_router_w0"], v["L2_ffn_router_w1"]], axis=1))
    for m in "qkv":
        a[f"w{m}3"] = c(v[f"L3_xattn_W{m}"])
    a["wo3"] = c(v["L3_xattn_Wo"].reshape(8, P, D).transpose(1, 0, 2).reshape(P, 8 * D))
    a["wg3"] = c(v["L3_ffn_We_gate"].transpose(1, 0, 2).reshape(D, E3 * FH))
    a["wu3"] = c(v["L3_ffn_We_up"].transpose(1, 0, 2).reshape(D, E3 * FH))
    a["wd3"] = c(v["L3_ffn_We_down"].reshape(2 * PAIRS, P, D).transpose(1, 0, 2).reshape(P, 2 * PAIRS * D))
    a["gw3"] = c(v["L3_ffn_gate_w"].T)
    a["wgs3"] = c(v["L3_ffn_Ws_gate"])
    a["wus3"] = c(v["L3_ffn_Ws_up"])
    a["wds3"] = c(v["L3_ffn_Ws_down"])
    col = lambda z: z.reshape(-1, P).T
    kb = v["L2_xattn_kv_b"]
    a["cols"] = c(np.concatenate([col(z) for z in (
        v["L0_xattn_w_sim"], v["L0_ffn_b1"].reshape(-1), v["L1_xattn_bq"], v["L1_xattn_bk"], v["L1_xattn_bv"],
        v["L1_ffn_bn_gamma"], v["L1_ffn_bn_beta"], v["L2_xattn_q_b"], kb[:D], kb[D:], v["L3_xattn_bq"],
        v["L3_xattn_bk"], v["L3_xattn_bv"])], axis=1))
    a["rows"] = c(np.concatenate([v["L0_xattn_b_qv"], v["L1_xattn_bo"], v["L2_xattn_proj_b"], v["L3_xattn_bo"],
                                  v["L3_xattn_ln_gamma"], v["L3_xattn_ln_beta"], v["L0_ffn_gate_b"],
                                  v["L3_ffn_gate_bias"], v["L0_xattn_b_sim"]])[None, :])
    return a


def kernel(**inputs):
    import numpy as _np
    import concourse.bacc as _bacc
    from concourse import mybir as _mybir
    from concourse.bass_utils import run_bass_kernel_spmd as _run

    arrays = layouts({name: _np.asarray(a) for name, a in inputs.items()})
    nc = _bacc.Bacc("TRN2", target_bir_lowering=False, num_devices=1)
    dram = {}
    for name, a in arrays.items():
        dram[name] = nc.dram_tensor(f"in_{name}", a.shape, _mybir.dt.from_np(a.dtype), kind="ExternalInput").ap()
    out = nc.dram_tensor("out_x", (B, S, D), _mybir.dt.float32, kind="ExternalOutput").ap()
    program(nc, dram, out)
    r = _run(nc, [{f"in_{name}": a for name, a in arrays.items()}], core_ids=[0])
    return r.results[0]["out_x"]
```

```python
from contextlib import ExitStack

import concourse.bass as bass
from concourse import mybir

F32 = mybir.dt.float32
F32R = mybir.dt.float32r
BF16 = mybir.dt.bfloat16
I32 = mybir.dt.int32
U32 = mybir.dt.uint32
U8 = mybir.dt.uint8
ALU = mybir.AluOpType
ACT = mybir.ActivationFunctionType
AX = mybir.AxisListType

P = 128
D = 128
B, S, C = 8, 256, 64
T = B * S
NT = T // P
BLK = 512
NB = T // BLK
TPB = BLK // P
H = 16
HC = H * C
EPS = 1e-5
FAR = -1.0e30
PARTS = 3
E0, F0, K0 = 8, 512, 4
E2, E3, FH = 32, 64, 64
PAIRS = 16
NH, NK, KT8 = 8, 32, 8
NE = NK * NK
G3, GE, TG = 8, 8, 4


class Tally:

    def __init__(self, eng, sem):
        self.eng, self.sem, self.n = eng, sem, 0

    def mark(self, ins):
        ins.then_inc(self.sem, 1)
        self.n = self.n + 1
        return ins

    def wait(self):
        self.eng.wait_ge(self.sem, self.n)

    def settle(self, ins):
        self.mark(ins)
        self.wait()

    def enter(self, i, per):
        self.base, self.per = self.n, per
        self.n = self.base + i * per

    def leave(self, times):
        self.n = self.base + times * self.per


def known(n, least):
    return not isinstance(n, int) or n >= least


def rolled(eng, total, unroll, step):
    for n in range(unroll):
        step(n, n)
    with eng.Fori(1, total // unroll) as i:
        for r in range(unroll):
            step(i * unroll + r, r)


def run_tiles(eng, step):
    for n in range(TPB):
        step(n, n, 0)
    with eng.Fori(1, NB - 1) as i:
        for r in range(TPB):
            step(i * TPB + r, r, i)
    for n in range(NT - TPB, NT):
        step(n, n % TPB, NB - 1)


COLS = {}
ROWS = {}


def _place(table, names):
    at = 0
    for name, width in names:
        table[name] = (at, width)
        at += width
    return at


NCOLS = _place(COLS, [("w_sim", 3), ("b1_0", E0 * K0), ("bq1", 1), ("bk1", 1), ("bv1", 1), ("gamma", 1), ("beta", 1),
                      ("bq2", 1), ("bk2", 1), ("bv2", 1), ("bq3", 8), ("bk3", 8), ("bv3", 8)])
NROWS = _place(ROWS, [("b_qv", D), ("bo1", D), ("bo2", D), ("bo3", D), ("ln_gamma", D), ("ln_beta", D),
                      ("gate_b", E0), ("gate_bias", E3), ("b_sim", 1)])


class Core:

    def __init__(self, nc, ctx, dram):
        self.nc, self.ctx, self.dram = nc, ctx, dram
        self.own_sems, self.last_sems = [], []

        self.offset = {}

        def sb(name, shape, dt=F32):
            self.offset[name] = nc.sbuf_base
            return ctx.enter_context(nc.sbuf_tensor(name, shape, dt))

        self.X = sb("X", [P, NT, D])
        self.XN = sb("XN", [P, NT, D])
        self.XT = sb("XT", [P, T])
        self.RA = sb("RA", [P, 12288])
        self.RB = sb("RB", [P, 16384])
        self.RC = sb("RC", [P, 8448])
        self.RW = sb("RW", [P, 4096])
        self.identf = sb("identf", [P, P])
        self.identb = sb("identb", [P, P], BF16)
        self.pair_sel = sb("pair_sel", [PARTS * E2, PAIRS, P], BF16)
        self.one_sel = sb("one_sel", [PARTS * E0, E0, P], BF16)
        self.head16 = sb("head16", [P, H])
        self.head2 = sb("head2", [P, 2])
        self.iota = sb("iota", [P, E2])
        self.before = sb("before", [P, G3 * G3])
        self.gates = sb("gates", [P, 2 * E2 + E3])
        self.eps = sb("eps", [P, 1])
        self.cols = sb("cols", [P, NCOLS])
        self.rows = sb("rows", [P, NROWS])
        self.ctxT = sb("ctxT", [P, B * C])
        self.stats = sb("stats", [P, NT, 6])
        self.mom = sb("mom", [P, 8, NT])
        self.region = {"RA": self.RA, "RB": self.RB, "RC": self.RC, "XT": self.XT}
        self.PS = ctx.enter_context(nc.psum_tensor("PS", [P, 8, BLK], F32))
        self.PB = self.PS[:].bitcast(BF16)

    def rounded(self, name, region, at, width, partitions=P):
        return self.nc.alloc_sbuf_tensor_at(name, [partitions, width], F32R, offset=self.offset[region] + 4 * at)[:]

    def sem(self, name):
        self.own_sems.append(self.nc.alloc_semaphore(name=name))
        return self.own_sems[-1]

    def lasting_sem(self, name):
        return self.ctx.enter_context(self.nc.semaphore(name))

    def clear_last(self, pool):
        if self.last_sems:
            self.nc.clear_and_free_semaphores(self.last_sems)
        self.last_sems, self.own_sems = self.own_sems, []

    def col(self, name, k=0):
        at, _ = COLS[name]
        return self.cols[:, at + k:at + k + 1]

    def row(self, name):
        at, width = ROWS[name]
        return self.rows[:, at:at + width]


def over(ap, axis, n):
    ap = ap.unsqueeze(axis)
    shape = list(ap.shape)
    shape[axis] = n
    return ap.broadcast_to(shape)



class Norm:

    def __init__(self, k, name, src, turn=True):
        self.k, self.src, self.turn = k, src, turn
        self.var_ready = k.sem(f"{name}_var_ready")
        self.std_ready = k.sem(f"{name}_std_ready")
        self.xn_ready = k.sem(f"{name}_xn_ready")
        self.xt_turned = k.sem(f"{name}_xt_turned")
        self.xt_ready = k.sem(f"{name}_xt_ready")


def norm_vector(dve, k, nm, own, loaded=None):
    st, mom = k.stats, k.mom
    mean2, dif, m2, difsq, var, mean, std, rstd = (mom[:, j, :] for j in range(8))
    if loaded:
        for t in range(NT):
            if t % TPB == 0:
                dve.wait_ge(loaded[t // TPB], 16)
            own.mark(dve.bn_stats(st[:, t, :], nm.src[:, t, :]))
    else:
        with dve.Fori(0, NT // 4) as i:
            own.enter(i, 4)
            for r in range(4):
                own.mark(dve.bn_stats(st[:, i * 4 + r, :], nm.src[:, i * 4 + r, :]))
        own.leave(NT // 4)
    own.wait()
    own.mark(dve.tensor_tensor(mean2, st[:, :, 1], st[:, :, 4], ALU.add))
    own.mark(dve.tensor_tensor(dif, st[:, :, 1], st[:, :, 4], ALU.subtract))
    own.settle(dve.tensor_tensor(m2, st[:, :, 2], st[:, :, 5], ALU.add))
    own.mark(dve.tensor_scalar(mean, mean2, 0.5, None, ALU.mult))
    own.settle(dve.scalar_tensor_tensor(difsq, dif, D / 4.0, dif, ALU.mult, ALU.mult))
    dve.tensor_tensor(var, difsq, m2, ALU.add).then_inc(nm.var_ready, 1)
    dve.wait_ge(nm.std_ready, 1)
    own.settle(dve.reciprocal(rstd, std))
    for t in range(NT):
        dve.tensor_scalar(k.XN[:, t, :], nm.src[:, t, :], mean[:, t:t + 1], rstd[:, t:t + 1],
                          ALU.subtract, ALU.mult).then_inc(nm.xn_ready, 1)


def norm_scalar(act, k, nm, between=None):
    act.wait_ge(nm.var_ready, 1)
    act.activation(k.mom[:, 6, :], k.mom[:, 4, :], ACT.Sqrt, bias=k.eps[:, 0:1],
                   scale=1.0 / D).then_inc(nm.std_ready, 1)
    if nm.turn:
        for b in range(NB):
            if between:
                between(b)
            act.wait_ge(nm.xt_turned, b + 1)
            act.activation(k.XT[:, bass.ts(b, BLK)], k.PS[:, b, :], ACT.Copy).then_inc(nm.xt_ready, 1)


def norm_tensor(pe, k, nm, between=None):
    for t in range(NT):
        pe.wait_ge(nm.xn_ready, t + 1)
        mm = pe.transpose(k.PS[:, t // TPB, bass.ts(t % TPB, P)], k.XN[:, t, :], k.identf[:])
        if t % TPB == TPB - 1:
            mm.then_inc(nm.xt_turned, 1)
            if between:
                between(t // TPB)



def setup(k):
    nc, dram = k.nc, k.dram
    k.made, k.zeroed = k.lasting_sem("constants_made"), k.lasting_sem("zeroed")
    k.x_loaded = [k.lasting_sem(f"x_loaded{q}") for q in range(NB)]
    k.small_loaded, k.ctx_loaded = k.lasting_sem("small_loaded"), k.lasting_sem("ctx_loaded")
    k.l0x_loaded, k.l0f_loaded = k.lasting_sem("l0x_loaded"), k.lasting_sem("l0f_loaded")
    k.att_loaded, k.keys_loaded = k.lasting_sem("att_loaded"), k.lasting_sem("keys_loaded")
    k.l2f_loaded, k.l3x_loaded = k.lasting_sem("l2f_loaded"), k.lasting_sem("l3x_loaded")
    k.l3f_loaded, k.l3d_loaded = k.lasting_sem("l3f_loaded"), k.lasting_sem("l3d_loaded")

    k.ctxK = k.RB[0:C, 0:B * D].rearrange("p (b d) -> p b d", b=B)
    k.Wqv = k.RB[:, 1024:1536].rearrange("p (c n) -> p c n", c=4)
    k.W1_0 = k.RA[:, 0:4096].rearrange("p (e f) -> p e f", e=E0)
    k.W2_0 = k.RA[:, 4096:8192].rearrange("p (e f n) -> p e f n", e=E0, f=K0)
    k.b2_0 = k.RA[0:E0, 8192:8320]
    k.gw0 = k.RA[:, 8320:8328]
    k.Wa = [k.RC[:, at:at + 512].rearrange("p (m n) -> p m n", m=4) for at in (5120, 5632)]
    k.mask1 = k.RC[:, 6144:6272].bitcast(I32).rearrange("p (j c) -> p j c", j=2)
    k.mask2 = k.RC[:, 6272:6400].bitcast(U8).rearrange("p (b c) -> p b c", b=B)
    k.masks = k.RC[:, 6400:6784].bitcast(BF16)
    k.mask1_add = k.masks[:, 0:2 * C].rearrange("p (j c) -> p j c", j=2)
    k.mask2_add = k.masks[:, 2 * C:(2 + B) * C].rearrange("p (b c) -> p b c", b=B)
    k.masks_made = k.lasting_sem("masks_made")

    with nc.Block() as block:

        @block.sync
        def _(sp):
            xv = dram["x"].rearrange("(t p) d -> p t d", p=P)
            for q in range(NB):
                sp.dma_start(k.X[:, 4 * q:4 * q + 4, :], xv[:, 4 * q:4 * q + 4, :]).then_inc(k.x_loaded[q], 16)

        @block.gpsimd
        def _(pool):
            own = Tally(pool, k.made)
            own.settle(pool.memset(k.identf[:], 0.0))
            own.settle(pool.affine_select(out=k.identf[:], in_=k.identf[:], compare_op=ALU.not_equal, fill=1.0, base=0,
                                          pattern=[[-1, P]], channel_multiplier=1))


def loads(sp, k):
    dram = k.dram
    sp.dma_start(k.ctxT[:], dram["ctxT"]).then_inc(k.ctx_loaded, 16)
    sp.dma_start(k.cols[:], dram["cols"]).then_inc(k.small_loaded, 16)
    sp.dma_start(k.rows[:], dram["rows"].broadcast_to([P, NROWS])).then_inc(k.small_loaded, 16)
    sp.dma_start(k.gates[:, 0:2 * E2], dram["router2"]).then_inc(k.small_loaded, 16)
    sp.dma_start(k.gates[:, 2 * E2:], dram["gw3"]).then_inc(k.small_loaded, 16)
    sp.dma_start(k.ctxK, dram["ctxK"]).then_inc(k.l0x_loaded, 16)
    sp.dma_start(k.Wqv, dram["Wqv"]).then_inc(k.l0x_loaded, 16)
    sp.dma_start(k.W1_0, dram["w1_0"]).then_inc(k.l0f_loaded, 16)
    sp.dma_start(k.W2_0, dram["w2_0"]).then_inc(k.l0f_loaded, 16)
    sp.dma_start(k.b2_0, dram["b2_0"]).then_inc(k.l0f_loaded, 16)
    sp.dma_start(k.gw0, dram["gw0"]).then_inc(k.l0f_loaded, 16)
    for n in range(2):
        sp.dma_start(k.Wa[n], dram[f"wa{n + 1}"]).then_inc(k.att_loaded, 16)
    sp.dma_start(k.mask1, dram["mask1"]).then_inc(k.att_loaded, 16)
    sp.dma_start(k.RC[:, 6272:6400].bitcast(I32),
                 dram["mask2"].broadcast_to([P, B * C // 4])).then_inc(k.att_loaded, 16)
    sp.dma_start(k.RC[:, 0:2048], dram["w_q"]).then_inc(k.keys_loaded, 16)
    sp.dma_start(k.RC[:, 2048:2560], dram["keysT"]).then_inc(k.keys_loaded, 16)
    sp.dma_start(k.RC[:, 2560:3584], dram["downT"]).then_inc(k.keys_loaded, 16)
    sp.dma_start(k.RC[:, 3584:4608], dram["up"]).then_inc(k.keys_loaded, 16)


def fills(dve, k):
    dve.memset(k.eps[:], EPS).then_inc(k.zeroed, 1)
    dve.memset(k.head16[:], 1.0).then_inc(k.zeroed, 1)
    dve.memset(k.head2[:], 0.0).then_inc(k.zeroed, 1)
    dve.memset(k.pair_sel[:], 0.0).then_inc(k.zeroed, 1)
    dve.memset(k.one_sel[:], 0.0).then_inc(k.zeroed, 1)


def additive_masks(dve, k):
    dve.wait_ge(k.att_loaded, 64)
    dve.tensor_scalar(k.mask1_add, k.mask1, 0, FAR, ALU.is_equal, ALU.mult).then_inc(k.masks_made, 1)
    dve.tensor_scalar(k.mask2_add, k.mask2, 0, FAR, ALU.not_equal, ALU.mult).then_inc(k.masks_made, 1)


def constants(pool, k, own):
    own.settle(pool.iota(k.iota[:], pattern=[[1, E2]], base=0, channel_multiplier=0,
                         allow_small_or_imprecise_dtypes=True))
    own.settle(pool.memset(k.identb[:], 0.0))
    own.settle(pool.affine_select(out=k.identb[:], in_=k.identb[:], compare_op=ALU.not_equal, fill=1.0, base=0,
                                  pattern=[[-1, P]], channel_multiplier=1))
    pool.wait_ge(k.zeroed, 5)
    own.settle(pool.affine_select(out=k.head16[:], in_=k.head16[:], compare_op=ALU.is_ge, fill=0.0, base=0,
                                  pattern=[[-(P // H), H]], channel_multiplier=1))
    own.settle(pool.affine_select(out=k.head16[:], in_=k.head16[:], compare_op=ALU.is_ge, fill=0.0,
                                  base=P // H - 1, pattern=[[P // H, H]], channel_multiplier=-1))
    own.settle(pool.memset(k.head2[0:64, 0:1], 1.0))
    own.settle(pool.memset(k.head2[64:P, 1:2], 1.0))
    own.settle(pool.memset(k.before[:], 1.0))
    own.settle(pool.affine_select(out=k.before[:], in_=k.before[:], compare_op=ALU.is_gt, fill=0.0, base=0,
                                  pattern=[[1, G3], [-1, G3]], channel_multiplier=0))
    for part in range(PARTS):
        own.settle(pool.affine_select(out=k.pair_sel[:], in_=k.pair_sel[:], compare_op=ALU.not_equal,
                                      fill=1.0, base=-part * E2, pattern=[[-2, PAIRS], [-1, 2], [0, FH]],
                                      channel_multiplier=1))
        own.settle(pool.affine_select(out=k.one_sel[:], in_=k.one_sel[:], compare_op=ALU.not_equal,
                                      fill=1.0, base=-part * E0, pattern=[[-1, E0], [0, P]],
                                      channel_multiplier=1))



def similarity_attention(k):
    nc, PS, RB = k.nc, k.PS, k.RB
    nm = Norm(k, "l0x", k.X)
    vec, gps = k.sem("l0x_vector"), k.sem("l0x_gpsimd")
    w_ready, sim_ready = k.sem("l0x_w_ready"), k.sem("l0x_sim_ready")
    max_ready, shifted, exped = k.sem("l0x_max_ready"), k.sem("l0x_shifted"), k.sem("l0x_exped")
    a_ready, at_turned, at_ready = k.sem("l0x_a_ready"), k.sem("l0x_at_turned"), k.sem("l0x_at_ready")
    mt_ready, bshift, bexp = k.sem("l0x_mt_ready"), k.sem("l0x_bshift"), k.sem("l0x_bexp")
    batt_ready, bc_turned, bc_ready = k.sem("l0x_batt_ready"), k.sem("l0x_bc_turned"), k.sem("l0x_bc_ready")
    hc_done, w14_ready = k.sem("l0x_hc_done"), k.sem("l0x_w14_ready")
    hq_done, hq_ready, f3_ready = k.sem("l0x_hq_done"), k.sem("l0x_hq_ready"), k.sem("l0x_f3_ready")
    out_done, biased = k.sem("l0x_out_done"), k.sem("l0x_biased")

    R = RB[:, 1536:2048]
    w2b = RB[:, 2048:2176]
    sim = RB[:, 2304:3328].rearrange("p (t c) -> p t c", t=NT)
    w14 = RB[:, 3328:4352].rearrange("p (b n) -> p b n", b=B)
    AT = RB[0:C, 4352:6400]
    HQ = RB[:, 6400:8448]
    F3 = RB[:, 8448:10496]
    qmax = k.RW[:, 0:NT]
    qsum = k.RW[:, 16:32]
    qrec = k.RW[:, 32:48]
    batt = k.RW[0:B, 64:64 + S]
    bsum = k.RW[0:B, 400:401]
    brec = k.RW[0:B, 401:402]
    bmax = k.RW[0:B, 402:403]
    bcol = k.RW[:, 416:432].rearrange("p (j b) -> p j b", j=2)
    hc = k.RW[:, 432:440]
    ones = k.RB[:, 2176:2304]
    SIM, MT, BC, HC = 4, 6, 6, 7
    sim_ps = PS[:, SIM:SIM + 2, :].rearrange("p a (t c) -> p (a t) c", c=C)
    q2 = qmax.rearrange("p (b j) -> p j b", j=2)

    with nc.Block() as block:

        @block.sync
        def _(sp):
            loads(sp, k)

        @block.gpsimd
        def _(pool):
            k.clear_last(pool)
            own = Tally(pool, gps)
            constants(pool, k, own)
            pool.wait_ge(nm.xn_ready, NT)
            pool.wait_ge(k.small_loaded, 64)
            pool.tensor_tensor(k.X[:], k.X[:], over(k.row("b_qv"), 1, NT), ALU.add).then_inc(biased, 1)

        @block.vector
        def _(dve):
            own = Tally(dve, vec)
            fills(dve, k)
            norm_vector(dve, k, nm, own, loaded=k.x_loaded)
            own.mark(dve.memset(ones, 1.0))
            dve.wait_ge(k.ctx_loaded, 16)
            dve.wait_ge(k.small_loaded, 64)
            own.settle(dve.tensor_scalar(R, k.ctxT[:], k.col("w_sim", 2), k.col("w_sim", 0), ALU.mult, ALU.add))
            dve.tensor_scalar(w2b, ones, k.col("w_sim", 1), None, ALU.mult).then_inc(w_ready, 1)
            dve.wait_ge(sim_ready, 1)
            own.settle(dve.tensor_scalar(sim, sim_ps, k.row("b_sim"), None, ALU.add))
            dve.tensor_reduce(qmax, sim, AX.X, ALU.max).then_inc(max_ready, 1)
            dve.wait_ge(max_ready, 1)
            dve.tensor_tensor(sim, sim, over(qmax, 2, C), ALU.subtract).then_inc(shifted, 1)
            dve.wait_ge(mt_ready, 1)
            own.settle(dve.tensor_reduce(bmax, PS[0:B, MT, 0:S], AX.X, ALU.max))
            dve.tensor_scalar(batt, PS[0:B, MT, 0:S], bmax, None, ALU.subtract).then_inc(bshift, 1)
            dve.wait_ge(exped, 1)
            own.settle(dve.tensor_reduce(qsum, sim, AX.X, ALU.add))
            own.settle(dve.reciprocal(qrec, qsum))
            dve.tensor_tensor(sim, sim, over(qrec, 2, C), ALU.mult).then_inc(a_ready, 1)
            dve.wait_ge(bexp, 1)
            own.settle(dve.reciprocal(brec, bsum))
            dve.tensor_scalar(batt, batt, brec, None, ALU.mult).then_inc(batt_ready, 1)
            dve.wait_ge(bc_turned, 1)
            dve.tensor_copy(bcol, PS[:, BC, 0:2 * B].rearrange("p (j b) -> p j b", j=2)).then_inc(bc_ready, 1)
            dve.wait_ge(hc_done, 1)
            own.settle(dve.tensor_copy(hc, PS[:, HC, 0:B]))
            dve.wait_ge(k.l0x_loaded, 32)
            for b in range(B):
                ins = dve.scalar_tensor_tensor(w14[:, b, :], k.Wqv[:, 3, :], hc[:, b:b + 1], k.Wqv[:, 0, :],
                                               ALU.mult, ALU.add)
            ins.then_inc(w14_ready, 1)
            for q in range(NB):
                dve.wait_ge(hq_done, q + 1)
                dve.tensor_tensor(F3[:, bass.ts(q, BLK)], k.XT[:, bass.ts(q, BLK)], PS[:, q, :],
                                  ALU.mult).then_inc(f3_ready, 1)
            dve.wait_ge(biased, 1)
            for q in range(NB):
                dve.wait_ge(out_done, q + 1)
                xq = k.X[:, TPB * q:TPB * (q + 1), :].rearrange("p t d -> p (t d)")
                dve.tensor_tensor(xq, xq, PS[:, 4 + q, :], ALU.add)
            additive_masks(dve, k)

        @block.scalar
        def _(act):
            norm_scalar(act, k, nm)
            act.wait_ge(shifted, 1)
            act.activation(sim, sim, ACT.Exp).then_inc(exped, 1)
            act.wait_ge(bshift, 1)
            act.activation(batt, batt, ACT.Exp, accum_out=bsum).then_inc(bexp, 1)
            act.wait_ge(at_turned, 1)
            for q in range(NB):
                act.activation(AT[:, bass.ts(q, BLK)], PS[0:C, q, :], ACT.Copy).then_inc(at_ready, 1)
            for q in range(NB):
                act.wait_ge(hq_done, q + 1)
                act.wait_ge(f3_ready, q + 1)
                act.activation(HQ[:, bass.ts(q, BLK)], PS[:, q, :], ACT.Copy).then_inc(hq_ready, 1)

        @block.tensor
        def _(pe):
            norm_tensor(pe, k, nm)
            pe.wait_ge(w_ready, 1)
            pe.wait_ge(nm.xt_ready, NB)
            for t in range(NT):
                b = t // 2
                pe.matmul(sim_ps[:, t, :], k.XT[:, bass.ts(t, P)], R[:, bass.ts(b, C)], start=True, stop=False)
                mm = pe.matmul(sim_ps[:, t, :], w2b, k.ctxT[:, bass.ts(b, C)], start=False, stop=True)
            mm.then_inc(sim_ready, 1)
            pe.wait_ge(max_ready, 1)
            for j in range(2):
                mm = pe.transpose(PS[0:B, MT, bass.ts(j, P)], q2[:, j, :], k.identf[:])
            mm.then_inc(mt_ready, 1)
            pe.wait_ge(a_ready, 1)
            for t in range(NT):
                mm = pe.transpose(PS[0:C, t // TPB, bass.ts(t % TPB, P)], sim[:, t, :], k.identf[:])
            mm.then_inc(at_turned, 1)
            pe.wait_ge(batt_ready, 1)
            for j in range(2):
                mm = pe.transpose(PS[:, BC, bass.ts(j, B)], batt[:, bass.ts(j, P)], k.identf[0:B, 0:B])
            mm.then_inc(bc_turned, 1)
            pe.wait_ge(bc_ready, 1)
            for b in range(B):
                for j in range(2):
                    mm = pe.matmul(PS[:, HC, b:b + 1], k.XN[:, 2 * b + j, :], bcol[:, j, b:b + 1],
                                   start=(j == 0), stop=(j == 1))
            mm.then_inc(hc_done, 1)
            pe.wait_ge(k.l0x_loaded, 32)
            for b in range(B):
                pe.wait_ge(at_ready, NB)
                mm = pe.matmul(PS[:, b // 2, bass.ts(b % 2, S)], k.ctxK[:, b, :], AT[:, bass.ts(b, S)],
                               start=True, stop=True)
                if b % 2:
                    mm.then_inc(hq_done, 1)
            pe.wait_ge(w14_ready, 1)
            pe.wait_ge(hq_ready, NB)
            for t in range(NT):
                o = PS[:, 4 + t // TPB, bass.ts(t % TPB, P)]
                pe.matmul(o, k.XT[:, bass.ts(t, P)], w14[:, t // 2, :], start=True, stop=False)
                pe.matmul(o, HQ[:, bass.ts(t, P)], k.Wqv[:, 1, :], start=False, stop=False)
                mm = pe.matmul(o, F3[:, bass.ts(t, P)], k.Wqv[:, 2, :], start=False, stop=True)
                if t % TPB == TPB - 1:
                    mm.then_inc(out_done, 1)



class Step:

    def __init__(self, gate, up, down, bias=0.0, spread=None, fresh=True):
        self.gate, self.up, self.down, self.bias = gate, up, down, bias
        self.spread, self.fresh = spread, fresh
        self.rows = gate[0].shape[1]


def product3(pe, out, w, x, start, stop):
    (wh, wl), (xh, xl) = w, x
    pe.matmul(out, wh, xh, start=start, stop=False)
    pe.matmul(out, wh, xl, start=False, stop=False)
    return pe.matmul(out, wl, xh, start=False, stop=stop)


class Rests:

    def __init__(self, k, name, parts):
        self.parts = []
        for n, (region, at, width, rest_region, rest_at, rows) in enumerate(parts):
            whole = k.region[region][0:rows, at:at + width]
            high = k.rounded(f"{name}_high{n}", region, at, width, rows)
            rest = k.rounded(f"{name}_rest{n}", rest_region, rest_at, width, rows)
            self.parts.append((whole, high, rest))
        self.rounded = k.sem(f"{name}_rounded")
        self.subtracted = k.sem(f"{name}_subtracted")
        self.ready = k.sem(f"{name}_parts_split")

    def vector(self, dve, first, last):
        for whole, high, rest in self.parts[first:last]:
            dve.tensor_copy(rest, whole).then_inc(self.rounded, 1)

    def gpsimd(self, pool):
        for n, (whole, high, rest) in enumerate(self.parts):
            pool.wait_ge(self.rounded, n + 1)
            pool.tensor_tensor(rest, whole, rest, ALU.subtract).then_inc(self.subtracted, 1)

    def scalar(self, act, used, xt_part):
        for n, (whole, high, rest) in enumerate(self.parts):
            act.wait_ge(self.subtracted, n + 1)
            if n == xt_part:
                act.wait_ge(used, 1)
            act.activation(high, whole, ACT.Copy).then_inc(self.ready, 1)


class Experts:

    GATE, UP, SPREAD, ACC, TURN = 0, 2, 4, 6, 7

    def __init__(self, k, name, passes, func, rests, need):
        self.k, self.passes, self.func = k, passes, func
        self.rests, self.need = rests, need
        _, self.XH, self.XL = rests.parts[need[0] - 1]
        self.gate_ready = k.sem(f"{name}_gate_ready")
        self.acted = k.sem(f"{name}_acted")
        self.up_ready = k.sem(f"{name}_up_ready")
        self.multiplied = k.sem(f"{name}_multiplied")
        self.spread_ready = k.sem(f"{name}_spread_ready")
        self.weighted = k.sem(f"{name}_weighted")
        self.rounded = k.sem(f"{name}_hid_rounded")
        self.hidden_ready = k.sem(f"{name}_hidden_ready")
        self.down_done = k.sem(f"{name}_down_done")
        self.acc_read = k.sem(f"{name}_acc_read")
        self.out_turned = k.sem(f"{name}_out_turned")
        self.out_added = k.sem(f"{name}_out_added")
        self.paced = k.sem(f"{name}_paced")
        self.K = len(passes[0])
        self.A = [k.RW[:, bass.ts(n, BLK)] for n in range(2)]
        self.M = k.RW[:, bass.ts(2, BLK)]
        self.OT = k.RW[:, bass.ts(3, BLK)]
        self.lag = 3
        self.even = self.K // 4 * 4
        self.HID, self.HIGH, self.REST = [], [], []
        high, rest = (k.rounded(f"{name}_hid_{what}", "RB", at, 5 * BLK) for what, at in (("high", 0), ("rest", 5 * BLK)))
        for c in range(self.K):
            slot = c % 4 if c < self.even else 4
            self.HID.append(k.RW[:, bass.ts(4 + c % 2, BLK)])
            self.HIGH.append(high[:, bass.ts(slot, BLK)])
            self.REST.append(rest[:, bass.ts(slot, BLK)])
        self.no, self.last, n = [], {}, -1
        for c, st in enumerate(passes[0]):
            n += st.spread is not None and st.fresh
            self.no.append(n)
            if st.spread is not None:
                self.last[n] = c
        self.KS = n + 1

    def vector_rests(self, dve, nm):
        at = self.need[0] - 1
        self.rests.vector(dve, 0, at)
        dve.wait_ge(nm.xt_ready, NB)
        self.rests.vector(dve, at, len(self.rests.parts))

    def bank_user(self, j, c):
        if c >= 2 or known(j, 1):
            odd = self.K % 2 and c == 0
            return j * self.K + (0 if odd else c - 1)
        return None

    def slot_user(self, j, c):
        if 4 <= c < self.even:
            return j * self.K + c - 3
        if known(j, 1):
            return j * self.K - self.K + (self.even - 3 + c if c < 4 else c + 1)
        return None

    def spread_user(self, j, n):
        if n >= 2:
            return j * self.K + self.last[n - 2] + 1
        if known(j, 1):
            return j * self.K - self.K + self.last[self.KS - 2 + n] + 1
        return None

    def blocks(self, eng, block):
        for g, steps in enumerate(self.passes):
            before = self.passes[max(g - 1, 0)]
            block(g * NB, 0, g, steps, before)
            with eng.Fori(1, NB) as i:
                block(i + g * NB, i, g, steps, steps)


def wait_user(eng, sem, count):
    if count is not None:
        eng.wait_ge(sem, count)


def experts_tensor(pe, e, WT, extra=None):
    k, K, PS = e.k, e.K, e.k.PS

    def down(j, c, st):
        pe.wait_ge(e.hidden_ready, j * K + c + 1)
        rows = slice(0, st.rows)
        product3(pe, PS[:, e.ACC, :], st.down, (e.HIGH[c][rows, :], e.REST[c][rows, :]),
                 start=(c == 0 and extra is None), stop=(c == K - 1)).then_inc(e.down_done, 1)

    def turn():
        for r in range(TPB):
            mm = pe.transpose(PS[:, e.TURN, bass.ts(r, P)], e.OT[:, bass.ts(r, P)], k.identf[:])
        mm.then_inc(e.out_turned, 1)

    def block(j, i, g, steps, before):
        if isinstance(i, int) and i == 0:
            pe.wait_ge(e.rests.ready, e.need[g])
        x = (e.XH[:, bass.ts(i, BLK)], e.XL[:, bass.ts(i, BLK)])
        for c, st in enumerate(steps):
            wait_user(pe, e.acted, e.bank_user(j, c))
            if st.rows < P:
                pe.sem_inc(e.paced, 1)
            product3(pe, PS[0:st.rows, e.GATE + c % 2, :], st.gate, x, True, True).then_inc(e.gate_ready, 1)
            if st.up is not None:
                wait_user(pe, e.multiplied, e.bank_user(j, c))
                if st.rows < P:
                    pe.sem_inc(e.paced, 1)
                product3(pe, PS[0:st.rows, e.UP + c % 2, :], st.up, x, True, True).then_inc(e.up_ready, 1)
            if st.spread is not None and st.fresh:
                n = e.no[c]
                sel, group = st.spread
                wait_user(pe, e.weighted, e.spread_user(j, n))
                if e.spread_user(j, n) is not None and sel.shape[0] <= 32:
                    pe.sem_inc(e.paced, 1)
                pe.matmul(PS[:, e.SPREAD + n % 2, :], sel, WT[:, group, bass.ts(i, BLK)], start=True,
                          stop=True).then_inc(e.spread_ready, 1)
            if c >= e.lag:
                if c == e.lag and known(j, 1):
                    pe.wait_ge(e.acc_read, j)
                if c == e.lag and extra is not None:
                    pe.sem_inc(e.paced, 1)
                    extra(pe, i)
                down(j, c - e.lag, steps[c - e.lag])
            elif known(j, 1):
                down(j - 1, K - e.lag + c, before[K - e.lag + c])
            if c == e.lag + 1 and known(j, 1):
                turn()

    e.blocks(pe, block)
    last = len(e.passes) * NB - 1
    for c in range(K - e.lag, K):
        down(last, c, e.passes[-1][c])
    pe.wait_ge(e.acc_read, last + 1)
    turn()


def experts_scalar(act, e):
    PS, K = e.k.PS, e.K

    def copy_sum(blocks):
        act.wait_ge(e.down_done, blocks * K)
        act.activation(e.OT, PS[:, e.ACC, :], ACT.Copy).then_inc(e.acc_read, 1)

    def block(j, i, g, steps, before):
        for c, st in enumerate(steps):
            act.wait_ge(e.gate_ready, j * K + c + 1)
            wait_user(act, e.multiplied if st.up is not None else e.weighted, e.bank_user(j, c))
            act.activation(e.A[c % 2][0:st.rows, :], PS[0:st.rows, e.GATE + c % 2, :], e.func,
                           bias=st.bias).then_inc(e.acted, 1)
            if c == e.lag and known(j, 1):
                copy_sum(j)

    act.preload_act_table(e.func)
    e.blocks(act, block)
    copy_sum(len(e.passes) * NB)


def experts_vector(dve, e):
    k, PS, K = e.k, e.k.PS, e.K
    place = lambda slots, c, st: slots[c][0:st.rows, :]

    def round_hidden(j, c, st):
        dve.wait_ge(e.weighted, j * K + c + 1)
        wait_user(dve, e.down_done, e.slot_user(j, c))
        dve.tensor_copy(place(e.HIGH, c, st), place(e.HID, c, st)).then_inc(e.rounded, 1)

    def round_before(j, c, steps, before):
        if c >= 1:
            round_hidden(j, c - 1, steps[c - 1])
        elif known(j, 1):
            round_hidden(j - 1, K - 1, before[K - 1])

    def add_sum(block, i):
        dve.wait_ge(e.out_turned, block)
        x = k.X[:, bass.ts(i, TPB), :].rearrange("p t d -> p (t d)")
        dve.tensor_tensor(x, x, PS[:, e.TURN, :], ALU.add).then_inc(e.out_added, 1)

    def block(j, i, g, steps, before):
        for c, st in enumerate(steps):
            m = j * K + c
            rows = slice(0, st.rows)
            a = e.A[c % 2][rows, :]
            if st.up is None:
                round_before(j, c, steps, before)
            dve.wait_ge(e.acted, m + 1)
            if st.up is not None:
                dve.wait_ge(e.up_ready, m + 1)
                if known(j, 1) or c >= 1:
                    dve.wait_ge(e.weighted, m)
                dve.tensor_tensor(e.M[rows, :], a, PS[rows, e.UP + c % 2, :], ALU.mult).then_inc(e.multiplied, 1)
                round_before(j, c, steps, before)
                dve.wait_ge(e.multiplied, m + 1)
                a = e.M[rows, :]
            wait_user(dve, e.hidden_ready, e.bank_user(j, c))
            hid = place(e.HID, c, st)
            if st.spread is None:
                dve.tensor_copy(hid, a).then_inc(e.weighted, 1)
            else:
                dve.wait_ge(e.spread_ready, j * e.KS + e.no[c] + 1)
                dve.tensor_tensor(hid, a, PS[:, e.SPREAD + e.no[c] % 2, :], ALU.mult).then_inc(e.weighted, 1)
            if c == e.lag + 2 and known(j, 1):
                add_sum(j, (NB - 1) if isinstance(i, int) else i - 1)

    e.blocks(dve, block)
    last = len(e.passes) * NB - 1
    round_hidden(last, K - 1, e.passes[-1][K - 1])
    add_sum(last + 1, NB - 1)


def experts_gpsimd(pool, e):
    def block(j, i, g, steps, before):
        for c, st in enumerate(steps):
            pool.wait_ge(e.rounded, j * e.K + c + 1)
            wait_user(pool, e.down_done, e.slot_user(j, c))
            hid, high, rest = (slots[c][0:st.rows, :] for slots in (e.HID, e.HIGH, e.REST))
            pool.tensor_tensor(rest, hid, high, ALU.subtract).then_inc(e.hidden_ready, 1)

    e.blocks(pool, block)



class Route:

    LOGITS = 4

    def __init__(self, k, name, experts, groups):
        self.k, self.E, self.G, self.R = k, experts, groups, NT * groups
        n = NT * groups * experts
        RB = k.RB
        self.rows = lambda at: RB[:, at:at + n].rearrange("p (r e) -> p r e", e=experts)
        self.L, self.W, self.T1, self.T2 = (self.rows(at) for at in (0, 1024, 2048, 3072))
        self.parts = RB[:, 4096:4096 + n * PARTS // 2].bitcast(BF16).rearrange(
            "p (r a e) -> p r a e", a=PARTS, e=experts)
        self.top = RB[:, 5632:5632 + 8 * self.R].rearrange("p (r j) -> p r j", j=8)
        self.at = RB[:, 5888:5888 + 8 * self.R].bitcast(U32).rearrange("p (r j) -> p r j", j=8)
        self.z = RB[:, 6144:6144 + self.R]
        self.rz = RB[:, 6208:6208 + self.R]
        self.WT = RB[0:PARTS * experts, 6272:6272 + groups * T // 2].bitcast(BF16).rearrange(
            "p (g t) -> p g t", g=groups)
        self.WT32 = RB[0:experts, 8320:8320 + T]
        self.logits_ready = k.sem(f"{name}_logits_ready")
        self.shifted = k.sem(f"{name}_route_shifted")
        self.exped = k.sem(f"{name}_route_exped")
        self.parts_ready = k.sem(f"{name}_parts_ready")
        self.parts_turned = k.sem(f"{name}_parts_turned")
        self.wt_ready = k.sem(f"{name}_wt_ready")
        self.logits = k.PS[:, self.LOGITS:self.LOGITS + 2, :].rearrange("p a f -> p (a f)")[:, 0:n]
        self.NWT = 2 * groups


def route_logits(pe, k, r, nm, gate):
    pe.wait_ge(nm.xt_ready, NB)
    w = r.G * r.E
    for t in range(NT):
        mm = pe.matmul(r.logits[:, bass.ts(t, w)], k.XT[:, bass.ts(t, P)], gate, start=True, stop=True)
    mm.then_inc(r.logits_ready, 1)


def route_top2(dve, k, r, own, bias, renormalise):
    dve.wait_ge(r.logits_ready, 1)
    lg = r.logits.rearrange("p (r e) -> p r e", e=r.E)
    if bias is None:
        own.settle(dve.tensor_copy(r.L, lg))
    else:
        own.settle(dve.tensor_tensor(r.L, lg, over(bias, 1, r.R), ALU.add))
    for j in range(r.R):
        own.mark(dve.max(r.top[:, j, :], r.L[:, j, :]))
    own.wait()
    dve.tensor_tensor(r.W, r.L, r.top[:, :, 0:1].broadcast_to([P, r.R, r.E]), ALU.subtract).then_inc(r.shifted, 1)
    for j in range(r.R):
        own.mark(dve.max_index(r.at[:, j, :], r.top[:, j, :], r.L[:, j, :]))
    own.wait()
    iota = over(k.iota[:, 0:r.E], 1, r.R)
    own.mark(dve.tensor_tensor(r.T1, iota, r.at[:, :, 0:1].broadcast_to([P, r.R, r.E]), ALU.is_equal))
    own.settle(dve.tensor_tensor(r.T2, iota, r.at[:, :, 1:2].broadcast_to([P, r.R, r.E]), ALU.is_equal))
    own.settle(dve.tensor_tensor(r.T1, r.T1, r.T2, ALU.add))
    dve.wait_ge(r.exped, 1)
    if not renormalise:
        own.settle(dve.tensor_reduce(r.z, r.W, AX.X, ALU.add))
    own.settle(dve.tensor_tensor(r.W, r.W, r.T1, ALU.mult))
    if renormalise:
        own.settle(dve.tensor_reduce(r.z, r.W, AX.X, ALU.add))
    own.settle(dve.reciprocal(r.rz, r.z))
    if not renormalise:
        own.settle(dve.tensor_scalar(r.rz, r.rz, 0.5, None, ALU.mult))
    own.settle(dve.tensor_tensor(r.W, r.W, over(r.rz, 2, r.E), ALU.mult))
    route_parts(dve, r, own)


def route_parts(dve, r, own):
    own.settle(dve.tensor_copy(r.parts[:, :, 0, :], r.W))
    own.settle(dve.tensor_tensor(r.T1, r.W, r.parts[:, :, 0, :], ALU.subtract))
    own.settle(dve.tensor_copy(r.parts[:, :, 1, :], r.T1))
    own.settle(dve.tensor_tensor(r.T1, r.T1, r.parts[:, :, 1, :], ALU.subtract))
    dve.tensor_copy(r.parts[:, :, 2, :], r.T1).then_inc(r.parts_ready, 1)


def route_exp(act, r):
    act.wait_ge(r.shifted, 1)
    act.activation(r.W, r.W, ACT.Exp).then_inc(r.exped, 1)


def route_turn(pe, k, r, whole=False):
    pe.wait_ge(r.parts_ready, 1)
    n = PARTS * r.E
    for g in range(r.G):
        for t in range(NT):
            mm = pe.transpose(k.PB[0:n, 2 * g + t // 8, bass.ts(t % 8, P)],
                              r.parts[:, t * r.G + g, :, :].rearrange("p a e -> p (a e)"), k.identb[:])
    if whole:
        for t in range(NT):
            mm = pe.transpose(k.PS[0:r.E, 4 + t // TPB, bass.ts(t % TPB, P)], r.W[:, t, :], k.identf[:])
    mm.then_inc(r.parts_turned, 1)


def route_store(act, k, r, whole=False):
    act.wait_ge(r.parts_turned, 1)
    n = PARTS * r.E
    for g in range(r.G):
        for h in range(2):
            act.activation(r.WT[:, g, bass.ts(h, T // 2)], k.PB[0:n, 2 * g + h, :], ACT.Copy).then_inc(r.wt_ready, 1)
    if whole:
        for q in range(NB):
            act.activation(r.WT32[:, bass.ts(q, BLK)], k.PS[0:r.E, 4 + q, :], ACT.Copy).then_inc(r.wt_ready, 1)



def gelu_experts(k):
    nm, r = Norm(k, "l0f", k.X), Route(k, "l0f", E0, 1)
    n, fit = E0 * F0, (E0 - 1) * F0
    rests = Rests(k, "l0f", [("RA", 0, n, "RB", 10368, P), ("RA", n, fit, "RA", 8448, P),
                             ("RA", n + fit, F0, "RB", 14464, P), ("XT", 0, T, "XN", 0, P)])
    w1, w2, w2_last = (part[1:] for part in rests.parts[:3])
    chunk = lambda pair, c: tuple(a[:, bass.ts(c, P)] for a in pair)
    last = fit // P
    steps = [Step(chunk(w1, c), None, chunk(w2, c) if c < last else chunk(w2_last, c - last),
                  bias=k.col("b1_0", c), spread=(k.one_sel[:, c // K0, :], 0), fresh=(c % K0 == 0))
             for c in range(E0 * K0)]
    ex = Experts(k, "l0f", [steps], ACT.Gelu, rests, [4])
    vec = k.sem("l0f_vector")

    def bias2(pe, i):
        pe.matmul(k.PS[:, ex.ACC, :], k.b2_0, r.WT32[:, bass.ts(i, BLK)], start=True, stop=False)

    with k.nc.Block() as block:

        @block.gpsimd
        def _(pool):
            k.clear_last(pool)
            ex.rests.gpsimd(pool)
            experts_gpsimd(pool, ex)

        @block.vector
        def _(dve):
            own = Tally(dve, vec)
            norm_vector(dve, k, nm, own)
            dve.wait_ge(k.l0f_loaded, 64)
            ex.vector_rests(dve, nm)
            route_top2(dve, k, r, own, k.row("gate_b"), renormalise=True)
            experts_vector(dve, ex)

        @block.scalar
        def _(act):
            norm_scalar(act, k, nm)
            route_exp(act, r)
            ex.rests.scalar(act, r.logits_ready, ex.need[0] - 1)
            route_store(act, k, r, whole=True)
            experts_scalar(act, ex)

        @block.tensor
        def _(pe):
            norm_tensor(pe, k, nm)
            pe.wait_ge(k.l0f_loaded, 64)
            route_logits(pe, k, r, nm, k.gw0)
            route_turn(pe, k, r, whole=True)
            pe.wait_ge(r.wt_ready, r.NWT + NB)
            experts_tensor(pe, ex, r.WT, extra=bias2)



class Heads:

    def __init__(self, name, chunks, wq, wk, wv, wo, bq, bk, bv, scale, head_mask, QT, VT,
                 spare, bk_all, mask=None, per_tile=False):
        self.name, self.chunks, self.spare, self.bk_all = name, chunks, spare, bk_all
        self.wq, self.wk, self.wv, self.wo = wq, wk, wv, wo
        self.bq, self.bk, self.bv, self.scale = bq, bk, bv, scale
        self.head_mask, self.QT, self.VT = head_mask, QT, VT
        self.mask, self.per_tile = mask, per_tile


def heads_attention(k, hd, bias_row, weights_loaded, before=None, after=None):
    nc, PS = k.nc, k.PS
    nm = Norm(k, hd.name, k.X)
    target = k.XN if after else k.X
    s = lambda what: k.sem(f"{hd.name}_{what}")
    vec = s("vector")
    k_ready, v_ready, v_biased, bk_masked = s("k_ready"), s("v_ready"), s("v_biased"), s("bk_masked")
    k_masked = s("k_masked_vector"), s("k_masked_scalar")
    v_spread, vw_ready, vw_stored = s("v_spread"), s("vw_ready"), s("vw_stored")
    q_ready, q_stored, score_ready, shifted = s("q_ready"), s("q_stored"), s("score_ready"), s("shifted")
    exped, summed, normed, p_turned, p_stored = s("exped"), s("summed"), s("normed"), s("p_turned"), s("p_stored")
    out_ready, out_added, biased = s("out_ready"), s("out_added"), s("biased")

    NC, HPC = hd.chunks, H // hd.chunks
    Kall = k.RB[:, 0:8192].rearrange("p (b h c) -> p b h c", b=B, h=H)
    Kflat = k.RB[:, 0:8192].rearrange("p (b n) -> p b n", b=B)
    VW = k.RB[:, 8192:16384].rearrange("p (b c n) -> p b c n", b=B, n=D)
    VWflat = k.RB[:, 8192:16384].rearrange("p (b n) -> p b n", b=B)
    SS = hd.spare + [k.RW[:, bass.ts(r, HC)] for r in range(2)]
    PT = k.RW[:, 2 * HC:3 * HC]
    VM = SS[2:4]
    small = k.RW[:, 3 * HC:]
    top, tot, rec = ([small[:, at + H * r:at + H * (r + 1)] for r in range(4)] for at in (512, 576, 640))
    PTB, OUT, Q = 4, 6, 7
    score = [PS[:, 2 * r:2 * r + 2, :].rearrange("p a f -> p (a f)") for r in range(2)]
    vw_ps = [PS[:, 4 + 2 * r:6 + 2 * r, :].rearrange("p a f -> p (a f)") for r in range(2)]
    turn_ps = PS[:, PTB:PTB + 2, :].rearrange("p a f -> p (a f)")
    masked_bk = small[:, 704:704 + H]
    key_jobs = [(c, range(HPC)) for c in range(NC)] if NC > 1 else [(0, range(0, H // 2)), (0, range(H // 2, H))]
    key_bank = lambda n: PS[:, n % 2, :].rearrange("p (b c) -> p b c", b=B)
    JOBS = max(1, NC // 2)
    CPJ = NC // JOBS

    with nc.Block() as block:

        if before is not None:
            @block.sync
            def _(sp):
                before(sp)

        @block.vector
        def _(dve):
            own = Tally(dve, vec)
            dve.tensor_tensor(masked_bk.rearrange("p (n h) -> p n h", n=NC), over(hd.bk_all, 2, HPC),
                              over(hd.head_mask, 1, NC), ALU.mult).then_inc(bk_masked, 1)
            norm_vector(dve, k, nm, own)
            for n, (c, heads) in enumerate(key_jobs):
                if n % 2 == 0:
                    dve.wait_ge(k_ready, n + 1)
                    for h in heads:
                        ins = dve.tensor_scalar(Kall[:, :, c * HPC + h, :], key_bank(n), hd.bk(c),
                                                hd.head_mask[:, h:h + 1], ALU.add, ALU.mult)
                    ins.then_inc(k_masked[0], 1)

            def add_out(n):
                dve.wait_ge(out_ready, n + 1)
                x = target[:, n, :]
                dve.tensor_tensor(x, x, PS[:, OUT, 0:D], ALU.add).then_inc(out_added, 1)

            def total(n, r):
                dve.wait_ge(exped, n + 1)
                own.settle(dve.tensor_reduce(tot[r], SS[r].rearrange("p (h c) -> p h c", c=C), AX.X, ALU.add))
                dve.reciprocal(rec[r], tot[r]).then_inc(summed, 1)

            def step(n, r):
                dve.wait_ge(score_ready, n + 1)
                if isinstance(n, int) and n == 2:
                    dve.wait_ge(vw_ready, B)
                if known(n, 4):
                    dve.wait_ge(p_turned, n - 3)
                sv = score[r % 2].rearrange("p (h c) -> p h c", c=C)
                own.settle(dve.tensor_reduce(top[r], sv, AX.X, ALU.max))
                dve.tensor_tensor(SS[r].rearrange("p (h c) -> p h c", c=C), sv, over(top[r], 2, C),
                                  ALU.subtract).then_inc(shifted, 1)
                if known(n, 1):
                    total(n - 1, (r - 1) % 4)
                if isinstance(n, int) and n == 3:
                    dve.wait_ge(biased, 1)
                if known(n, 3):
                    add_out(n - 3)

            for n in range(4):
                step(n, n)
            with dve.Fori(1, NT // 4) as i:
                own.enter(i - 1, 8)
                for r in range(4):
                    step(i * 4 + r, r)
            own.leave(NT // 4 - 1)
            total(NT - 1, 3)
            for n in range(NT - 3, NT):
                add_out(n)
            if after:
                after.vector(dve, own, out_added)

        @block.scalar
        def _(act):
            for c in range(NC):
                act.wait_ge(v_ready, c + 1)
                act.activation(hd.VT[:, c, :], PS[:, 6 + c % 2, :], ACT.Identity, bias=hd.bv(c)).then_inc(v_biased, 1)

            def store_vw(b):
                act.wait_ge(vw_ready, b + 1)
                act.activation(VWflat[:, b, :], vw_ps[b % 2], ACT.Copy).then_inc(vw_stored, 1)

            store_vw(0)
            norm_scalar(act, k, nm, between=lambda b: store_vw(b + 1))
            store_vw(5)
            act.wait_ge(bk_masked, 1)
            for n, (c, heads) in enumerate(key_jobs):
                if n % 2:
                    act.wait_ge(k_ready, n + 1)
                    for h in heads:
                        at = c * HPC + h
                        ins = act.activation(Kall[:, :, at, :], key_bank(n), ACT.Identity,
                                             bias=masked_bk[:, at:at + 1], scale=hd.head_mask[:, h:h + 1])
                    ins.then_inc(k_masked[1], 1)
            store_vw(6)
            store_vw(7)

            def store_q(b, slot, j):
                act.wait_ge(q_ready, b * JOBS + j + 1)
                for c in range(CPJ):
                    ins = act.activation(hd.QT[slot][:, j * CPJ + c, :], PS[:, Q, bass.ts(c, S)], ACT.Identity,
                                         bias=hd.bq(j * CPJ + c))
                ins.then_inc(q_stored, 1)

            def exp(n, r):
                act.wait_ge(shifted, n + 1)
                act.activation(SS[r], SS[r], ACT.Exp, scale=hd.scale).then_inc(exped, 1)

            def step(n, r, ahead):
                if not isinstance(n, int) or n + 2 < NT:
                    exp(n + 2, (r + 2) % 4)
                act.wait_ge(p_turned, n + 1)
                if known(n, 1):
                    act.wait_ge(out_ready, n)
                act.activation(PT, turn_ps, ACT.Copy).then_inc(p_stored, 1)
                for b, slot, j in ahead:
                    store_q(b, slot, j)

            for b in range(2):
                for j in range(JOBS):
                    store_q(b, b, j)
            exp(0, 0)
            exp(1, 1)
            attention_steps(act, step, JOBS)
            if after:
                after.scalar(act)

        @block.gpsimd
        def _(pool):
            k.clear_last(pool)
            pool.wait_ge(v_biased, NC)

            def spread_values(b, r):
                if known(b, 2):
                    pool.wait_ge(vw_ready, b - 1)
                if NC == 1:
                    v = over(hd.VT[:, 0, bass.ts(b, C)], 1, H)
                    m = over(hd.head_mask, 2, C)
                    o = VM[r].rearrange("p (h c) -> p h c", c=C)
                else:
                    v = over(hd.VT[:, :, bass.ts(b, C)], 2, HPC)
                    m = over(over(hd.head_mask, 1, NC), 3, C)
                    o = VM[r].rearrange("p (n h c) -> p n h c", h=HPC, c=C)
                pool.tensor_tensor(o, v, m, ALU.mult).then_inc(v_spread, 1)

            rolled(pool, B, 2, spread_values)
            pool.wait_ge(nm.xn_ready, NT)
            if after:
                pool.wait_ge(nm.xt_turned, NB)
            pool.tensor_tensor(target[:], target[:], over(k.row(bias_row), 1, NT), ALU.add).then_inc(biased, 1)
            with pool.Fori(0, NT // 4) as i:
                for r in range(4):
                    pool.wait_ge(summed, i * 4 + r + 1)
                    sv = SS[r].rearrange("p (h c) -> p h c", c=C)
                    pool.tensor_tensor(sv, sv, over(rec[r], 2, C), ALU.mult).then_inc(normed, 1)
            if after:
                after.gpsimd(pool)

        @block.tensor
        def _(pe):
            for sm, n in weights_loaded:
                pe.wait_ge(sm, n)
            for c in range(NC):
                if c >= 2:
                    pe.wait_ge(v_biased, c - 1)
                pe.matmul(PS[:, 6 + c % 2, :], hd.wv(c), k.ctxT[:], start=True, stop=True).then_inc(v_ready, 1)
            pe.wait_ge(v_biased, NC)

            def value_products(b, r):
                pe.wait_ge(v_spread, b + 1)
                if known(b, 2):
                    pe.wait_ge(vw_stored, b - 1)
                for c in range(8):
                    mm = pe.matmul(vw_ps[r][:, bass.ts(c, D)], VM[r][:, bass.ts(c, P)], hd.wo(c),
                                   start=True, stop=True)
                mm.then_inc(vw_ready, 1)

            for b in range(2):
                value_products(b, b)
            norm_tensor(pe, k, nm, between=lambda b: value_products(b + 2, b % 2))
            pe.wait_ge(nm.xt_ready, 2)
            for n, (c, heads) in enumerate(key_jobs):
                if n >= 2:
                    pe.wait_ge(k_masked[n % 2], n // 2)
                pe.matmul(PS[:, n % 2, :], hd.wk(c), k.ctxT[:], start=True, stop=True).then_inc(k_ready, 1)
            for b in range(6, B):
                value_products(b, b % 2)
            pe.wait_ge(vw_stored, B)
            pe.wait_ge(nm.xt_ready, NB)
            for sm in k_masked:
                pe.wait_ge(sm, len(key_jobs) // 2)

            def make_q(b, slot, j):
                pe.wait_ge(q_stored, b * JOBS + j)
                for c in range(CPJ):
                    mm = pe.matmul(PS[:, Q, bass.ts(c, S)], hd.wq(j * CPJ + c), k.XT[:, bass.ts(b, S)],
                                   start=True, stop=True)
                mm.then_inc(q_ready, 1)

            def scores(n, b, r):
                pe.wait_ge(q_stored, (b + 1) * JOBS)
                q = lambda c, slot=r // 2: hd.QT[slot][:, c, bass.ts(r % 2, P)]
                to = score[r % 2]
                if known(n, 2):
                    pe.wait_ge(shifted, n - 1)
                masked = hd.mask is not None
                if NC == 1:
                    for half in range(2):
                        mm = pe.matmul(to[:, bass.ts(half, BLK)], q(0), Kflat[:, b, bass.ts(half, BLK)],
                                       start=True, stop=not masked)
                        if masked:
                            m = hd.mask[:, r % 2, :] if hd.per_tile else hd.mask[:, b, :]
                            mm = pe.matmul(to[:, bass.ts(half, BLK)].rearrange("p (h c) -> p h c", c=C),
                                           k.identb[:], over(m, 1, H // 2), start=False, stop=True)
                else:
                    for c in range(NC):
                        mm = pe.matmul(to[:, bass.ts(c, P)], q(c), Kflat[:, b, bass.ts(c, P)], start=True, stop=True)
                mm.then_inc(score_ready, 1)

            def turn(n, r):
                pe.wait_ge(normed, n + 1)
                if known(n, 1):
                    pe.wait_ge(p_stored, n)
                for c in range(8):
                    mm = pe.transpose(turn_ps[:, bass.ts(c, P)], SS[r][:, bass.ts(c, P)], k.identf[:])
                mm.then_inc(p_turned, 1)

            def output(n, b):
                pe.wait_ge(p_stored, n + 1)
                if known(n, 1):
                    pe.wait_ge(out_added, n)
                for c in range(8):
                    mm = pe.matmul(PS[:, OUT, 0:D], PT[:, bass.ts(c, P)], VW[:, b, c, :], start=(c == 0), stop=(c == 7))
                mm.then_inc(out_ready, 1)

            def step(n, r, ahead):
                if not isinstance(n, int) or n + 2 < NT:
                    scores(n + 2, step.b0 + (r + 2) // 2, (r + 2) % 4)
                turn(n, r)
                ahead = list(ahead)
                if ahead:
                    make_q(*ahead[0])
                if known(n, 1):
                    output(n - 1, step.b0 + (r - 1) // 2)
                for job in ahead[1:]:
                    make_q(*job)

            for b in range(2):
                for j in range(JOBS):
                    make_q(b, b, j)
            scores(0, 0, 0)
            scores(1, 0, 1)
            attention_steps(pe, step, JOBS)
            output(NT - 1, B - 1)


def attention_steps(eng, step, jobs):
    def ahead(b, r):
        share = range(0, (jobs + 1) // 2) if r % 2 == 0 else range((jobs + 1) // 2, jobs)
        return [(b + 2 + r // 2, r // 2, j) for j in share]

    for n in range(4):
        step.b0 = 0
        step(n, n, ahead(0, n))
    with eng.Fori(1, NT // 4 - 1) as i:
        step.b0 = i * 2
        for r in range(4):
            step(i * 4 + r, r, ahead(i * 2, r))
    for r in range(4):
        step.b0 = B - 2
        step(NT - 4 + r, r, [])


def narrow_attention(k, n, wa, mask, per_tile, before=None):
    place = k.RW[:, 3 * HC:3 * HC + 512]
    QT = [place[:, bass.ts(r, S)].rearrange("p (c q) -> p c q", c=1) for r in range(2)]
    VT = k.RW[:, 2 * HC:2 * HC + B * C].rearrange("p (c n) -> p c n", c=1)
    spare = [k.XN[:, bass.ts(r, NT // 2), :].rearrange("p t d -> p (t d)") for r in range(2)]
    hd = Heads(f"l{n}x", 1, lambda c: wa[:, 0, :], lambda c: wa[:, 1, :], lambda c: wa[:, 2, :], lambda c: wa[:, 3, :],
               lambda c: k.col(f"bq{n}"), lambda c: k.col(f"bk{n}"), lambda c: k.col(f"bv{n}"),
               (D // H) ** -0.5, k.head16[:], QT, VT, spare, k.col(f"bk{n}"), mask, per_tile)
    heads_attention(k, hd, f"bo{n}", [(k.att_loaded, 64), (k.masks_made, 2)], before)


def attention_1(k):
    narrow_attention(k, 1, k.Wa[0], k.mask1_add, True)



def product_keys(k):
    nc, PS, RA, RB, RC = k.nc, k.PS, k.RA, k.RB, k.RC
    nm = Norm(k, "l1f", k.X)
    s = lambda what: k.sem(f"l1f_{what}")
    vec, paced = s("vector"), s("paced")
    wf_ready, wf_stored, bn_var, bn_std, bn_ready = s("wf_ready"), s("wf_stored"), s("bn_var"), s("bn_std"), s("bn_ready")
    z_ready, z_stored = s("z_ready"), s("z_stored")
    xb_ready, s_ready, s_stored, top_done = s("xb_ready"), s("s_ready"), s("s_stored"), s("top_done")
    a_pool, a_vector, sig_ready, g_ready, g_turned = s("a_pool"), s("a_vector"), s("sig_ready"), s("g_ready"), s("g_turned")
    m_ready, out_ready, out_added = s("m_ready"), s("out_ready"), s("out_added")

    w_q = RC[:, 0:2048].rearrange("p (n d) -> p n d", n=2 * NH)
    keysT = RC[:, 2048:2560].rearrange("p (n c) -> p n c", n=2 * NH)
    downT = RC[:, 2560:3584].rearrange("p (n c) -> p n c", n=8)
    up = RC[:, 3584:4608].rearrange("p (n c) -> p n c", n=8)
    Wf = RC[:, 4608:5120]
    zT = RB[:, :].rearrange("p (n t) -> p n t", n=8)
    A = [RA[:, bass.ts(h, NE)] for h in range(NH)]
    Ssb = [k.RW[:, bass.ts(r, 512)] for r in range(2)]
    M = [k.RW[:, bass.ts(1 + r, 1024)] for r in range(2)]
    xb = [k.RW[:, bass.ts(24 + r, P)] for r in range(2)]
    cand = k.RW[:, 3328:3840]
    t8 = k.RW[:, 3840:3968].rearrange("p (n j) -> p n j", j=8)
    v8 = k.RW[:, 3968:4032].rearrange("p (n j) -> p n j", j=8)
    bn = k.stats[:].rearrange("p t s -> p (t s)")
    mv, bstd, brstd, scale, shift, tmp = (k.mom[:, j, 0:2] for j in range(6))
    OUT, SP, Z, WF = 6, 7, 6, 7
    gt, *SG = (PS[:, 2 * n:2 * n + 2, :].rearrange("p a f -> p (a f)") for n in range(3))
    ON_VECTOR = 0
    ON_POOL = NH - ON_VECTOR

    def pair_scores(r, h):
        s0 = over(Ssb[r][:, bass.ts(h, NK)], 2, NK)
        s1 = over(Ssb[r][:, bass.ts(NH + h, NK)], 1, NK)
        return A[h].rearrange("p (a b) -> p a b", a=NK), s0, s1

    with nc.Block() as block:

        @block.vector
        def _(dve):
            own = Tally(dve, vec)
            norm_vector(dve, k, nm, own)
            for q in range(NB):
                dve.wait_ge(nm.xt_ready, q + 1)
                own.mark(dve.bn_stats(bn[:, bass.ts(q, 6)], k.XT[:, bass.ts(q, BLK)]))
            own.wait()
            dve.bn_aggr(mv, bn[:, 0:24]).then_inc(bn_var, 1)
            dve.wait_ge(bn_std, 1)
            own.settle(dve.reciprocal(brstd[:, 0:1], bstd[:, 0:1]))
            own.settle(dve.tensor_tensor(scale[:, 0:1], brstd[:, 0:1], k.col("gamma"), ALU.mult))
            own.settle(dve.tensor_tensor(tmp[:, 0:1], scale[:, 0:1], mv[:, 0:1], ALU.mult))
            dve.tensor_tensor(shift[:, 0:1], k.col("beta"), tmp[:, 0:1], ALU.subtract).then_inc(bn_ready, 1)

            def picks(n, r):
                dve.wait_ge(s_stored, n + 1)
                dve.sem_inc(paced, 1)
                for j in range(2 * NH):
                    own.mark(dve.max(t8[:, j, :], Ssb[r][:, bass.ts(j, NK)]))
                own.wait()
                own.settle(dve.tensor_tensor(cand.rearrange("p (h a b) -> p h a b", h=NH, a=8),
                                             over(t8[:, 0:NH, :], 3, 8), over(t8[:, NH:, :], 2, 8), ALU.add))
                dve.sem_inc(paced, 1)
                for h in range(NH):
                    own.mark(dve.max(v8[:, h, :], cand[:, bass.ts(h, 64)]))
                own.wait()
                for h in range(ON_POOL, NH):
                    if known(n, 1):
                        dve.wait_ge(g_turned, n * NH)
                    dve.tensor_tensor(*pair_scores(r, h), ALU.add).then_inc(a_vector, 1)

            def weigh(n, r, q):
                dve.wait_ge(g_turned, (n + 1) * NH)
                dve.wait_ge(z_stored, (q + 1) * 8)
                if known(n, 2):
                    dve.wait_ge(out_ready, n - 1)
                dve.tensor_tensor(M[r].rearrange("p (c t) -> p c t", c=8), gt.rearrange("p (c t) -> p c t", c=8),
                                  zT[:, :, bass.ts(n, P)], ALU.mult).then_inc(m_ready, 1)

            def add_out(n):
                dve.wait_ge(out_ready, n + 1)
                dve.tensor_tensor(k.X[:, n, :], k.X[:, n, :], PS[:, OUT, 0:D], ALU.add).then_inc(out_added, 1)

            def step(n, t, q):
                r = t % 2
                picks(n, r)
                if known(n, 2):
                    add_out(n - 2)
                if known(n, 1):
                    weigh(n - 1, 1 - r, q if t else q - 1)
                for h in range(NH):
                    dve.wait_ge(sig_ready, n * NH + h + 1)
                    if h >= ON_POOL:
                        dve.wait_ge(a_vector, n * ON_VECTOR + h - ON_POOL + 1)
                    dve.scalar_tensor_tensor(A[h], A[h], v8[:, h, 7:8], SG[h % 2], ALU.is_ge,
                                             ALU.mult).then_inc(g_ready, 1)

            per = 2 * NH + 1 + NH
            for n in range(TPB):
                step(n, n, 0)
            with dve.Fori(1, NB) as i:
                own.enter(i - 1, TPB * per)
                for t in range(TPB):
                    step(i * TPB + t, t, i)
            own.leave(NB - 1)
            add_out(NT - 2)
            weigh(NT - 1, 1, NB - 1)
            add_out(NT - 1)

        @block.scalar
        def _(act):
            act.wait_ge(wf_ready, 1)
            act.activation(Wf, PS[:, WF, :], ACT.Copy).then_inc(wf_stored, 1)
            norm_scalar(act, k, nm)
            act.wait_ge(bn_var, 1)
            act.activation(bstd[:, 0:1], mv[:, 1:2], ACT.Sqrt, bias=k.eps[:, 0:1]).then_inc(bn_std, 1)
            act.wait_ge(bn_ready, 1)

            def gelu(m, c, q):
                act.wait_ge(z_ready, m + 1)
                act.activation(zT[:, c, bass.ts(q, BLK)], PS[:, Z + c % 2, :], ACT.Gelu).then_inc(z_stored, 1)

            def batch_normed(n, r):
                if known(n, 2):
                    act.wait_ge(s_ready, n - 1)
                act.activation(xb[r], k.XT[:, bass.ts(n, P)], ACT.Identity, bias=shift[:, 0:1],
                               scale=scale[:, 0:1]).then_inc(xb_ready, 1)

            def store_s(n, r):
                act.wait_ge(s_ready, n + 1)
                if known(n, 2):
                    act.wait_ge(a_pool, (n - 1) * ON_POOL)
                    if ON_VECTOR:
                        act.wait_ge(a_vector, (n - 1) * ON_VECTOR)
                act.activation(Ssb[r], PS[:, SP, :], ACT.Copy).then_inc(s_stored, 1)

            def sigmoid(n, h):
                if h < ON_POOL:
                    act.wait_ge(a_pool, n * ON_POOL + h + 1)
                else:
                    act.wait_ge(a_vector, n * ON_VECTOR + h - ON_POOL + 1)
                if known(n, 1) or h >= 2:
                    act.wait_ge(g_ready, n * NH + h - 1)
                act.activation(SG[h % 2], A[h], ACT.Sigmoid).then_inc(sig_ready, 1)

            def step(n, t, q):
                r = t % 2
                for h in range(4):
                    sigmoid(n, h)
                if not isinstance(n, int) or n + 1 < NT:
                    store_s(n + 1, 1 - r)
                for h in range(4, NH):
                    sigmoid(n, h)
                if not isinstance(n, int) or n + 2 < NT:
                    batch_normed(n + 2, r)
                if not isinstance(n, int) or n + TPB < NT:
                    for c in (2 * t, 2 * t + 1):
                        gelu(n * 2 + 8 + c % 2, c, q + 1)

            batch_normed(0, 0)
            batch_normed(1, 1)
            store_s(0, 0)
            for c in range(8):
                gelu(c, c, 0)
            run_tiles(act, step)

        @block.gpsimd
        def _(pool):
            k.clear_last(pool)

            def step(n, t, q):
                r = t % 2
                pool.wait_ge(s_stored, n + 1)
                for h in range(ON_POOL):
                    if known(n, 1):
                        pool.wait_ge(g_turned, (n - 1) * NH + h + 1)
                    pool.tensor_tensor(*pair_scores(r, h), ALU.add).then_inc(a_pool, 1)
            run_tiles(pool, step)

        @block.tensor
        def _(pe):
            pe.wait_ge(k.keys_loaded, 64)
            for n in range(2 * NH):
                mm = pe.matmul(PS[:, WF, bass.ts(n, NK)], w_q[:, n, :], keysT[:, n, :], start=True, stop=True)
            mm.then_inc(wf_ready, 1)
            norm_tensor(pe, k, nm)
            pe.wait_ge(wf_stored, 1)
            pe.wait_ge(nm.xt_ready, NB)

            def project(m, c, q):
                if known(m, 2):
                    pe.wait_ge(z_stored, m - 1)
                pe.matmul(PS[:, Z + c % 2, :], downT[:, c, :], k.XT[:, bass.ts(q, BLK)], start=True,
                          stop=True).then_inc(z_ready, 1)

            def halves(n, r, z=None):
                pe.wait_ge(xb_ready, n + 1)
                if z is not None:
                    pe.wait_ge(z_stored, z)
                pe.matmul(PS[:, SP, :], xb[r], Wf, start=True, stop=True).then_inc(s_ready, 1)

            def turn(n, r, h):
                pe.wait_ge(g_ready, n * NH + h + 1)
                for c in range(8):
                    mm = pe.matmul(gt[:, bass.ts(c, P)], A[h][:, bass.ts(c, P)], k.identf[:],
                                   start=(h == 0 and c % 4 == 0), stop=(h == NH - 1), is_transpose=True,
                                   skip_group_check=True)
                mm.then_inc(g_turned, 1)

            def output(n, r):
                pe.wait_ge(m_ready, n + 1)
                if known(n, 1):
                    pe.wait_ge(out_added, n)
                for c in range(8):
                    mm = pe.matmul(PS[:, OUT, 0:D], M[r][:, bass.ts(c, P)], up[:, c, :], start=(c == 0), stop=(c == 7))
                mm.then_inc(out_ready, 1)

            def step(n, t, q):
                r = t % 2
                last = isinstance(n, int) and n + TPB >= NT
                if not isinstance(n, int) or n + 1 < NT:
                    halves(n + 1, 1 - r, 8 * NB if last else n * 2 + 8)
                if not last:
                    if known(n, 2):
                        pe.wait_ge(out_added, n - 1)
                    project(n * 2 + 8, 2 * t, q + 1)
                for h in range(4):
                    turn(n, r, h)
                if not last:
                    pe.wait_ge(s_stored, n + 2)
                    project(n * 2 + 9, 2 * t + 1, q + 1)
                for h in range(4, NH):
                    turn(n, r, h)
                if not last:
                    pe.wait_ge(z_stored, n * 2 + 10)
                if known(n, 1):
                    output(n - 1, 1 - r)

            halves(0, 0)
            pe.wait_ge(s_stored, 1)
            for c in range(8):
                project(c, c, 0)
            run_tiles(pe, step)
            output(NT - 1, 1)


def attention_2(k):
    def load(sp):
        sp.wait_ge(k.l0f_loaded, 64)
        for g in range(2):
            for n, m in enumerate("gud"):
                sp.dma_start(k.RA[:, 6144 * g + 2048 * n:6144 * g + 2048 * (n + 1)],
                             k.dram[f"w{m}2_{g}"]).then_inc(k.l2f_loaded, 16)
    narrow_attention(k, 2, k.Wa[1], k.mask2_add, False, before=load)



def silu_experts(k):
    nm, r = Norm(k, "l2f", k.X), Route(k, "l2f", E2, 2)
    n = E2 * FH
    rests = Rests(k, "l2f", [("RA", 0, 3 * n, "RB", 8320, P), ("XT", 0, T, "XN", 0, P),
                             ("RA", 3 * n, 3 * n, "RC", 0, P)])
    passes = []
    for g in range(2):
        w = [tuple(a[:, bass.ts(m, n)] for a in rests.parts[2 * g][1:]) for m in range(3)]
        chunk = lambda pair, c: tuple(a[:, bass.ts(c, P)] for a in pair)
        passes.append([Step(chunk(w[0], c), chunk(w[1], c), chunk(w[2], c), spread=(k.pair_sel[:, c, :], g))
                       for c in range(PAIRS)])
    ex = Experts(k, "l2f", passes, ACT.Silu, rests, [2, 3])
    vec = k.sem("l2f_vector")

    with k.nc.Block() as block:

        @block.sync
        def _(sp):
            sp.wait_ge(k.l2f_loaded, 96)
            sp.wait_ge(ex.acc_read, NB)
            for n, m in enumerate("qkvo"):
                sp.dma_start(k.RA[:, bass.ts(n, 1024)], k.dram[f"w{m}3"]).then_inc(k.l3x_loaded, 16)

        @block.gpsimd
        def _(pool):
            k.clear_last(pool)
            ex.rests.gpsimd(pool)
            experts_gpsimd(pool, ex)

        @block.vector
        def _(dve):
            own = Tally(dve, vec)
            norm_vector(dve, k, nm, own)
            dve.wait_ge(k.l2f_loaded, 96)
            ex.vector_rests(dve, nm)
            route_top2(dve, k, r, own, None, renormalise=False)
            experts_vector(dve, ex)

        @block.scalar
        def _(act):
            norm_scalar(act, k, nm)
            route_exp(act, r)
            ex.rests.scalar(act, r.logits_ready, ex.need[0] - 1)
            route_store(act, k, r)
            experts_scalar(act, ex)

        @block.tensor
        def _(pe):
            norm_tensor(pe, k, nm)
            route_logits(pe, k, r, nm, k.gates[:, 0:2 * E2])
            route_turn(pe, k, r)
            pe.wait_ge(r.wt_ready, r.NWT)
            experts_tensor(pe, ex, r.WT)



class PostNorm:

    def __init__(self, k):
        self.k, self.nm, self.shifted = k, Norm(k, "l3y", k.XN, turn=False), k.sem("l3y_shifted")

    def vector(self, dve, own, out_added):
        k = self.k
        dve.wait_ge(out_added, NT)
        norm_vector(dve, k, self.nm, own)
        dve.wait_ge(self.nm.xn_ready, NT)
        own.settle(dve.tensor_tensor(k.XN[:], k.XN[:], over(k.row("ln_gamma"), 1, NT), ALU.mult))
        dve.wait_ge(self.shifted, 1)
        dve.tensor_tensor(k.X[:], k.X[:], k.XN[:], ALU.add)

    def scalar(self, act):
        norm_scalar(act, self.k, self.nm)

    def gpsimd(self, pool):
        k = self.k
        pool.tensor_tensor(k.X[:], k.X[:], over(k.row("ln_beta"), 1, NT), ALU.add).then_inc(self.shifted, 1)


def attention_3(k):
    def load(sp):
        sp.wait_ge(k.keys_loaded, 64)
        sp.wait_ge(k.att_loaded, 64)
        sp.dma_start(k.RC[:, 0:4096], k.dram["wg3"]).then_inc(k.l3f_loaded, 16)
        sp.dma_start(k.RC[:, 4096:8192], k.dram["wu3"]).then_inc(k.l3f_loaded, 16)
        sp.dma_start(k.RC[:, 8192:8256], k.dram["wgs3"]).then_inc(k.l3f_loaded, 16)
        sp.dma_start(k.RC[:, 8256:8320], k.dram["wus3"]).then_inc(k.l3f_loaded, 16)
        sp.dma_start(k.RC[0:FH, 8320:8448], k.dram["wds3"]).then_inc(k.l3f_loaded, 16)
    w = [k.RA[:, bass.ts(n, 1024)] for n in range(4)]
    chunk = lambda a: lambda c: a[:, bass.ts(c, P)]
    QT = [k.RA[:, bass.ts(2 + r, 2048)].rearrange("p (c q) -> p c q", c=8) for r in range(2)]
    VT = k.RA[:, 8192:12288].rearrange("p (c n) -> p c n", c=8)
    hd = Heads("l3x", 8, chunk(w[0]), chunk(w[1]), chunk(w[2]), chunk(w[3]),
               lambda c: k.col("bq3", c), lambda c: k.col("bk3", c), lambda c: k.col("bv3", c),
               64 ** -0.5, k.head2[:], QT, VT, w[1:3],
               k.cols[:, COLS["bk3"][0]:COLS["bk3"][0] + 8])
    heads_attention(k, hd, "bo3", [(k.l3x_loaded, 64)], before=load, after=PostNorm(k))



def route_grouped(dve, k, r, own):
    BIG = -FAR
    full = lambda a: a.rearrange("p r e -> p (r e)")
    tokens = lambda a: full(a).rearrange("p (t e) -> p t e", e=E3)
    groups = lambda a: full(a).rearrange("p (g e) -> p g e", e=GE)
    four = lambda a: full(a).rearrange("p (t g h) -> p t g h", g=G3, h=G3)
    small = k.RB[:, 8320:8320 + 8 * NT * G3].rearrange("p (n g) -> p n g", n=8)
    best, count, second, other, total, rank, keep, low = (small[:, n, :] for n in range(8))
    pg = lambda a: a.rearrange("p (t g) -> p t g", g=G3)

    dve.wait_ge(r.exped, 1)
    own.settle(dve.tensor_tensor(tokens(r.L), tokens(r.W), over(k.row("gate_bias"), 1, NT), ALU.add))
    own.settle(dve.tensor_reduce(best, groups(r.L), AX.X, ALU.max))
    own.settle(dve.tensor_tensor(groups(r.T1), groups(r.L), over(best, 2, GE), ALU.is_equal))
    own.mark(dve.tensor_reduce(count, groups(r.T1), AX.X, ALU.add))
    own.settle(dve.scalar_tensor_tensor(full(r.T2), full(r.T1), FAR, full(r.L), ALU.mult, ALU.add))
    own.mark(dve.tensor_reduce(second, groups(r.T2), AX.X, ALU.max))
    own.settle(dve.tensor_scalar(other, count, 1.5, None, ALU.is_lt))
    own.settle(dve.scalar_tensor_tensor(other, other, FAR, best, ALU.mult, ALU.add))
    own.settle(dve.tensor_tensor(second, second, other, ALU.max))
    own.settle(dve.tensor_tensor(total, best, second, ALU.add))
    mine, others = over(pg(total), 3, G3), over(pg(total), 2, G3)
    own.mark(dve.tensor_tensor(four(r.T1), others, mine, ALU.is_gt))
    own.settle(dve.tensor_tensor(four(r.T2), others, mine, ALU.is_equal))
    own.settle(dve.tensor_tensor(full(r.T2).rearrange("p (t n) -> p t n", t=NT),
                                 full(r.T2).rearrange("p (t n) -> p t n", t=NT), over(k.before[:], 1, NT), ALU.mult))
    own.settle(dve.tensor_tensor(full(r.T1), full(r.T1), full(r.T2), ALU.add))
    own.settle(dve.tensor_reduce(rank, groups(r.T1), AX.X, ALU.add))
    own.settle(dve.tensor_scalar(low, rank, TG - 0.5, FAR, ALU.is_gt, ALU.mult))
    own.settle(dve.tensor_tensor(groups(r.T1), groups(r.L), over(low, 2, GE), ALU.add))
    for t in range(NT):
        own.mark(dve.max(r.top[:, t, :], tokens(r.T1)[:, t, :]))
    own.wait()
    for t in range(NT):
        own.mark(dve.match_replace(tokens(r.T2)[:, t, :], r.top[:, t, :], tokens(r.T1)[:, t, :], -3.0e38))
    own.wait()
    own.settle(dve.tensor_tensor(full(r.T1), full(r.T1), full(r.T2), ALU.not_equal))
    own.settle(dve.tensor_tensor(full(r.W), full(r.W), full(r.T1), ALU.mult))
    z, rz = r.z[:, 0:NT], r.rz[:, 0:NT]
    own.settle(dve.tensor_reduce(z, tokens(r.W), AX.X, ALU.add))
    own.settle(dve.tensor_scalar(z, z, 1e-20, None, ALU.add))
    own.settle(dve.reciprocal(rz, z))
    own.settle(dve.tensor_scalar(rz, rz, 2.5, None, ALU.mult))
    own.settle(dve.tensor_tensor(tokens(r.W), tokens(r.W), over(rz, 2, E3), ALU.mult))
    route_parts(dve, r, own)


def grouped_experts(k):
    nm, r = Norm(k, "l3f", k.X), Route(k, "l3f", E2, 2)
    n = E3 * FH
    down = k.RB[:, 12288:16384]
    rests = Rests(k, "l3f", [("RC", 0, n, "RA", 0, P), ("RC", n, n, "RA", n, P), ("RB", 12288, n, "RA", 2 * n, P),
                             ("RC", 2 * n, 2 * FH, "RB", 9600, P), ("RC", 2 * n + 2 * FH, D, "RB", 9728, FH),
                             ("XT", 0, T, "XN", 0, P)])
    weights = [part[1:] for part in rests.parts[:3]]
    chunk = lambda pair, c: tuple(a[:, bass.ts(c, P)] for a in pair)
    steps = [Step(*(chunk(pair, c) for pair in weights), spread=(k.pair_sel[:, c % PAIRS, :], c // PAIRS))
             for c in range(2 * PAIRS)]
    own_in, own_down = (part[1:] for part in rests.parts[3:5])
    steps.append(Step(tuple(a[:, 0:FH] for a in own_in), tuple(a[:, FH:2 * FH] for a in own_in), own_down))
    ex = Experts(k, "l3f", [steps], ACT.Silu, rests, [6])
    vec = k.sem("l3f_vector")

    with k.nc.Block() as block:

        @block.sync
        def _(sp):
            sp.dma_start(down, k.dram["wd3"]).then_inc(k.l3d_loaded, 16)

        @block.gpsimd
        def _(pool):
            k.clear_last(pool)
            ex.rests.gpsimd(pool)
            experts_gpsimd(pool, ex)

        @block.vector
        def _(dve):
            own = Tally(dve, vec)
            norm_vector(dve, k, nm, own)
            dve.wait_ge(k.l3f_loaded, 80)
            dve.wait_ge(k.l3d_loaded, 16)
            ex.vector_rests(dve, nm)
            route_grouped(dve, k, r, own)
            experts_vector(dve, ex)

        @block.scalar
        def _(act):
            norm_scalar(act, k, nm)
            act.wait_ge(r.logits_ready, 1)
            act.activation(r.W.rearrange("p r e -> p (r e)"), r.logits, ACT.Sigmoid).then_inc(r.exped, 1)
            ex.rests.scalar(act, r.logits_ready, ex.need[0] - 1)
            route_store(act, k, r)
            experts_scalar(act, ex)

        @block.tensor
        def _(pe):
            norm_tensor(pe, k, nm)
            route_logits(pe, k, r, nm, k.gates[:, 2 * E2:2 * E2 + E3])
            route_turn(pe, k, r)
            pe.wait_ge(r.wt_ready, r.NWT)
            experts_tensor(pe, ex, r.WT)



def store(k, out, src):
    done = k.lasting_sem("out_stored")
    with k.nc.Block() as block:

        @block.sync
        def _(sp):
            ov = out.rearrange("b (j p) d -> p (b j) d", p=P)
            for q in range(4):
                sp.dma_start(ov[:, 4 * q:4 * q + 4, :], src[:, 4 * q:4 * q + 4, :]).then_inc(done, 16)
            sp.wait_ge(done, 64)


LAYERS = [similarity_attention, gelu_experts, attention_1, product_keys, attention_2, silu_experts,
          attention_3, grouped_experts]


def program(nc, dram, out):
    with ExitStack() as ctx:
        k = Core(nc, ctx, dram)
        setup(k)
        for layer in LAYERS:
            layer(k)
        store(k, out, k.X)



def layouts(v):
    import numpy as np
    a = {}
    c = lambda z: np.ascontiguousarray(z)
    ctx = v["ctx_1024"]
    a["x"] = c(v["x"].reshape(T, D))
    a["ctxT"] = c(ctx.reshape(B * C, D).T)
    a["ctxK"] = c(ctx.transpose(1, 0, 2))
    a["Wqv"] = c(v["L0_xattn_W_qv"].reshape(4, D, D).transpose(1, 0, 2))
    a["w1_0"] = c(v["L0_ffn_w1"].transpose(1, 0, 2))
    a["w2_0"] = c(v["L0_ffn_w2"].reshape(E0, K0, P, D).transpose(2, 0, 1, 3))
    a["b2_0"] = c(v["L0_ffn_b2"])
    a["gw0"] = c(v["L0_ffn_gate_w"])
    a["wa1"] = c(np.stack([v[f"L1_xattn_W{m}"].T for m in "qkvo"], axis=1))
    kv = v["L2_xattn_kv_w"]
    a["wa2"] = c(np.stack([v["L2_xattn_q_w"], kv[:, :D], kv[:, D:], v["L2_xattn_proj_w"]], axis=1))
    a["mask1"] = c(v["mask_SxS2_if1"].reshape(2, P, C).transpose(1, 0, 2))
    a["mask2"] = c(v["mask_BxS2_bk0"].reshape(1, B * C)).view(np.int32)
    a["w_q"] = c(v["L1_ffn_w_q"].reshape(2 * NH, P, D).transpose(1, 0, 2).reshape(P, 2 * NH * D))
    a["keysT"] = c(v["L1_ffn_keys_p"].transpose(3, 2, 0, 1).reshape(P, 2 * NH * NK))
    a["downT"] = c(v["L1_ffn_down"][:NE].T)
    a["up"] = c(v["L1_ffn_up"][:NE].reshape(NE // P, P, D).transpose(1, 0, 2).reshape(P, NE // P * D))
    for g in range(2):
        a[f"wg2_{g}"] = c(v[f"L2_ffn_wg{g}"].transpose(1, 0, 2).reshape(D, E2 * FH))
        a[f"wu2_{g}"] = c(v[f"L2_ffn_wu{g}"].transpose(1, 0, 2).reshape(D, E2 * FH))
        a[f"wd2_{g}"] = c(v[f"L2_ffn_wd{g}"].reshape(PAIRS, P, D).transpose(1, 0, 2).reshape(P, PAIRS * D))
    a["router2"] = c(np.concatenate([v["L2_ffn_router_w0"], v["L2_ffn_router_w1"]], axis=1))
    for m in "qkv":
        a[f"w{m}3"] = c(v[f"L3_xattn_W{m}"])
    a["wo3"] = c(v["L3_xattn_Wo"].reshape(8, P, D).transpose(1, 0, 2).reshape(P, 8 * D))
    a["wg3"] = c(v["L3_ffn_We_gate"].transpose(1, 0, 2).reshape(D, E3 * FH))
    a["wu3"] = c(v["L3_ffn_We_up"].transpose(1, 0, 2).reshape(D, E3 * FH))
    a["wd3"] = c(v["L3_ffn_We_down"].reshape(2 * PAIRS, P, D).transpose(1, 0, 2).reshape(P, 2 * PAIRS * D))
    a["gw3"] = c(v["L3_ffn_gate_w"].T)
    a["wgs3"] = c(v["L3_ffn_Ws_gate"])
    a["wus3"] = c(v["L3_ffn_Ws_up"])
    a["wds3"] = c(v["L3_ffn_Ws_down"])
    col = lambda z: z.reshape(-1, P).T
    kb = v["L2_xattn_kv_b"]
    a["cols"] = c(np.concatenate([col(z) for z in (
        v["L0_xattn_w_sim"], v["L0_ffn_b1"].reshape(-1), v["L1_xattn_bq"], v["L1_xattn_bk"], v["L1_xattn_bv"],
        v["L1_ffn_bn_gamma"], v["L1_ffn_bn_beta"], v["L2_xattn_q_b"], kb[:D], kb[D:], v["L3_xattn_bq"],
        v["L3_xattn_bk"], v["L3_xattn_bv"])], axis=1))
    a["rows"] = c(np.concatenate([v["L0_xattn_b_qv"], v["L1_xattn_bo"], v["L2_xattn_proj_b"], v["L3_xattn_bo"],
                                  v["L3_xattn_ln_gamma"], v["L3_xattn_ln_beta"], v["L0_ffn_gate_b"],
                                  v["L3_ffn_gate_bias"], v["L0_xattn_b_sim"]])[None, :])
    return a


def kernel(**inputs):
    import numpy as _np
    import concourse.bacc as _bacc
    from concourse import mybir as _mybir
    from concourse.bass_utils import run_bass_kernel_spmd as _run

    arrays = layouts({name: _np.asarray(a) for name, a in inputs.items()})
    nc = _bacc.Bacc("TRN2", target_bir_lowering=False, num_devices=1)
    dram = {}
    for name, a in arrays.items():
        dram[name] = nc.dram_tensor(f"in_{name}", a.shape, _mybir.dt.from_np(a.dtype), kind="ExternalInput").ap()
    out = nc.dram_tensor("out_x", (B, S, D), _mybir.dt.float32, kind="ExternalOutput").ap()
    program(nc, dram, out)
    r = _run(nc, [{f"in_{name}": a for name, a in arrays.items()}], core_ids=[0])
    return r.results[0]["out_x"]
```

```python
from contextlib import ExitStack

import concourse.bass as bass
from concourse import mybir

F32 = mybir.dt.float32
F32R = mybir.dt.float32r
BF16 = mybir.dt.bfloat16
I32 = mybir.dt.int32
U32 = mybir.dt.uint32
U8 = mybir.dt.uint8
ALU = mybir.AluOpType
ACT = mybir.ActivationFunctionType
AX = mybir.AxisListType

P = 128
D = 128
B, S, C = 8, 256, 64
T = B * S
NT = T // P
BLK = 512
NB = T // BLK
TPB = BLK // P
H = 16
HC = H * C
EPS = 1e-5
FAR = -1.0e30
PARTS = 3
E0, F0, K0 = 8, 512, 4
E2, E3, FH = 32, 64, 64
PAIRS = 16
NH, NK = 8, 32
NE = NK * NK
G3, GE, TG = 8, 8, 4


class Tally:

    def __init__(self, eng, sem):
        self.eng, self.sem, self.n = eng, sem, 0

    def mark(self, ins):
        ins.then_inc(self.sem, 1)
        self.n = self.n + 1
        return ins

    def wait(self):
        self.eng.wait_ge(self.sem, self.n)

    def settle(self, ins):
        self.mark(ins)
        self.wait()

    def enter(self, i, per):
        self.base, self.per = self.n, per
        self.n = self.base + i * per

    def leave(self, times):
        self.n = self.base + times * self.per


def known(n, least):
    return not isinstance(n, int) or n >= least


def rolled(eng, total, unroll, step):
    for n in range(unroll):
        step(n, n)
    with eng.Fori(1, total // unroll) as i:
        for r in range(unroll):
            step(i * unroll + r, r)


def run_tiles(eng, step):
    for n in range(TPB):
        step(n, n, 0)
    with eng.Fori(1, NB - 1) as i:
        for r in range(TPB):
            step(i * TPB + r, r, i)
    for n in range(NT - TPB, NT):
        step(n, n % TPB, NB - 1)


COLS = {}
ROWS = {}


def _place(table, names):
    at = 0
    for name, width in names:
        table[name] = (at, width)
        at += width
    return at


NCOLS = _place(COLS, [("w_sim", 3), ("b1_0", E0 * K0), ("bq1", 1), ("bk1", 1), ("bv1", 1), ("gamma", 1), ("beta", 1),
                      ("bq2", 1), ("bk2", 1), ("bv2", 1), ("bq3", 8), ("bk3", 8), ("bv3", 8)])
NROWS = _place(ROWS, [("b_qv", D), ("bo1", D), ("bo2", D), ("bo3", D), ("ln_gamma", D), ("ln_beta", D),
                      ("gate_b", E0), ("gate_bias", E3), ("b_sim", 1)])


class Core:

    def __init__(self, nc, ctx, dram):
        self.nc, self.ctx, self.dram = nc, ctx, dram
        self.own_sems, self.last_sems = [], []

        self.offset = {}

        def sb(name, shape, dt=F32):
            self.offset[name] = nc.sbuf_base
            return ctx.enter_context(nc.sbuf_tensor(name, shape, dt))

        self.X = sb("X", [P, NT, D])
        self.XN = sb("XN", [P, NT, D])
        self.XT = sb("XT", [P, T])
        self.RA = sb("RA", [P, 12288])
        self.RB = sb("RB", [P, 16384])
        self.RC = sb("RC", [P, 8448])
        self.RW = sb("RW", [P, 4096])
        self.identf = sb("identf", [P, P])
        self.identb = sb("identb", [P, P], BF16)
        self.pair_sel = sb("pair_sel", [PARTS * E2, PAIRS, P], BF16)
        self.one_sel = sb("one_sel", [PARTS * E0, E0, P], BF16)
        self.head16 = sb("head16", [P, H])
        self.head2 = sb("head2", [P, 2])
        self.iota = sb("iota", [P, E2])
        self.before = sb("before", [P, G3 * G3])
        self.gates = sb("gates", [P, 2 * E2 + E3])
        self.eps = sb("eps", [P, 1])
        self.cols = sb("cols", [P, NCOLS])
        self.rows = sb("rows", [P, NROWS])
        self.ctxT = sb("ctxT", [P, B * C])
        self.stats = sb("stats", [P, NT, 6])
        self.mom = sb("mom", [P, 8, NT])
        self.region = {"RA": self.RA, "RB": self.RB, "RC": self.RC, "XT": self.XT}
        self.PS = ctx.enter_context(nc.psum_tensor("PS", [P, 8, BLK], F32))
        self.PB = self.PS[:].bitcast(BF16)

    def rounded(self, name, region, at, width, partitions=P):
        return self.nc.alloc_sbuf_tensor_at(name, [partitions, width], F32R, offset=self.offset[region] + 4 * at)[:]

    def sem(self, name):
        self.own_sems.append(self.nc.alloc_semaphore(name=name))
        return self.own_sems[-1]

    def lasting_sem(self, name):
        return self.ctx.enter_context(self.nc.semaphore(name))

    def clear_last(self, pool):
        if self.last_sems:
            self.nc.clear_and_free_semaphores(self.last_sems)
        self.last_sems, self.own_sems = self.own_sems, []

    def col(self, name, k=0):
        at, _ = COLS[name]
        return self.cols[:, at + k:at + k + 1]

    def row(self, name):
        at, width = ROWS[name]
        return self.rows[:, at:at + width]


def over(ap, axis, n):
    ap = ap.unsqueeze(axis)
    shape = list(ap.shape)
    shape[axis] = n
    return ap.broadcast_to(shape)



class Norm:

    def __init__(self, k, name, src, turn=True, counted=False):
        self.k, self.src, self.turn = k, src, turn
        self.counted = counted
        self.var_ready = k.sem(f"{name}_var_ready")
        self.std_ready = k.sem(f"{name}_std_ready")
        self.xn_ready = k.sem(f"{name}_xn_ready")
        self.xt_turned = k.sem(f"{name}_xt_turned")
        self.xt_ready = k.sem(f"{name}_xt_ready")


def count_tile(dve, k, src, t, added, n, paced):
    dve.wait_ge(added, n)
    if not isinstance(n, int):
        dve.sem_inc(paced, 1)
    return dve.bn_stats(k.stats[:, t, :], src[:, t, :])


def norm_vector(dve, k, nm, own, loaded=None):
    st, mom = k.stats, k.mom
    mean2, dif, m2, difsq, var, mean, std, rstd = (mom[:, j, :] for j in range(8))
    if not nm.counted:
        for t in range(NT):
            if loaded and t % TPB == 0:
                dve.wait_ge(loaded[t // TPB], 16)
            own.mark(dve.bn_stats(st[:, t, :], nm.src[:, t, :]))
        own.wait()
    own.mark(dve.tensor_tensor(mean2, st[:, :, 1], st[:, :, 4], ALU.add))
    own.mark(dve.tensor_tensor(dif, st[:, :, 1], st[:, :, 4], ALU.subtract))
    own.settle(dve.tensor_tensor(m2, st[:, :, 2], st[:, :, 5], ALU.add))
    own.mark(dve.tensor_scalar(mean, mean2, 0.5, None, ALU.mult))
    own.settle(dve.scalar_tensor_tensor(difsq, dif, D / 4.0, dif, ALU.mult, ALU.mult))
    dve.tensor_tensor(var, difsq, m2, ALU.add).then_inc(nm.var_ready, 1)
    dve.wait_ge(nm.std_ready, 1)
    own.settle(dve.reciprocal(rstd, std))
    for t in range(NT):
        dve.tensor_scalar(k.XN[:, t, :], nm.src[:, t, :], mean[:, t:t + 1], rstd[:, t:t + 1],
                          ALU.subtract, ALU.mult).then_inc(nm.xn_ready, 1)


def norm_scalar(act, k, nm, first=None):
    act.wait_ge(nm.var_ready, 1)
    act.activation(k.mom[:, 6, :], k.mom[:, 4, :], ACT.Sqrt, bias=k.eps[:, 0:1],
                   scale=1.0 / D).then_inc(nm.std_ready, 1)
    if nm.turn:
        if first:
            first()
        for b in range(NB):
            act.wait_ge(nm.xt_turned, b + 1)
            act.activation(k.XT[:, bass.ts(b, BLK)], k.PS[:, b, :], ACT.Copy).then_inc(nm.xt_ready, 1)


def norm_tensor(pe, k, nm, behind=None):
    for t in range(NT):
        pe.wait_ge(nm.xn_ready, t + 1)
        mm = pe.transpose(k.PS[:, t // TPB, bass.ts(t % TPB, P)], k.XN[:, t, :], k.identf[:])
        if t % TPB == TPB - 1:
            mm.then_inc(nm.xt_turned, 1)
            if behind and t >= TPB:
                behind(t // TPB - 1)
    if behind:
        behind(NB - 1)



def setup(k):
    nc, dram = k.nc, k.dram
    k.made, k.zeroed = k.lasting_sem("constants_made"), k.lasting_sem("zeroed")
    k.x_loaded = [k.lasting_sem(f"x_loaded{q}") for q in range(NB)]
    k.small_loaded, k.ctx_loaded = k.lasting_sem("small_loaded"), k.lasting_sem("ctx_loaded")
    k.l0x_loaded, k.l0f_loaded = k.lasting_sem("l0x_loaded"), k.lasting_sem("l0f_loaded")
    k.att_loaded, k.keys_loaded = k.lasting_sem("att_loaded"), k.lasting_sem("keys_loaded")
    k.l2f_loaded, k.l3x_loaded = k.lasting_sem("l2f_loaded"), k.lasting_sem("l3x_loaded")
    k.l3f_loaded, k.l3d_loaded = k.lasting_sem("l3f_loaded"), k.lasting_sem("l3d_loaded")

    k.ctxK = k.RB[0:C, 0:B * D].rearrange("p (b d) -> p b d", b=B)
    k.Wqv = k.RB[:, 1024:1536].rearrange("p (c n) -> p c n", c=4)
    k.W1_0 = k.RA[:, 0:4096].rearrange("p (e f) -> p e f", e=E0)
    k.W2_0 = k.RA[:, 4096:8192].rearrange("p (e f n) -> p e f n", e=E0, f=K0)
    k.b2_0 = k.RA[0:E0, 8192:8320]
    k.gw0 = k.RA[:, 8320:8328]
    k.Wa = [k.RC[:, at:at + 512].rearrange("p (m n) -> p m n", m=4) for at in (5120, 5632)]
    k.mask1 = k.RC[:, 6144:6272].bitcast(I32).rearrange("p (j c) -> p j c", j=2)
    k.mask2 = k.RC[:, 6272:6400].bitcast(U8).rearrange("p (b c) -> p b c", b=B)
    k.masks = k.RC[:, 6400:6784].bitcast(BF16)
    k.mask1_add = k.masks[:, 0:2 * C].rearrange("p (j c) -> p j c", j=2)
    k.mask2_add = k.masks[:, 2 * C:(2 + B) * C].rearrange("p (b c) -> p b c", b=B)
    k.masks_made = k.lasting_sem("masks_made")

    with nc.Block() as block:

        @block.sync
        def _(sp):
            xv = dram["x"].rearrange("(t p) d -> p t d", p=P)
            for q in range(NB):
                sp.dma_start(k.X[:, 4 * q:4 * q + 4, :], xv[:, 4 * q:4 * q + 4, :]).then_inc(k.x_loaded[q], 16)

        @block.gpsimd
        def _(pool):
            own = Tally(pool, k.made)
            own.settle(pool.memset(k.identf[:], 0.0))
            own.settle(pool.affine_select(out=k.identf[:], in_=k.identf[:], compare_op=ALU.not_equal, fill=1.0,
                                          base=0, pattern=[[-1, P]], channel_multiplier=1))


def loads(sp, k):
    dram = k.dram
    sp.dma_start(k.ctxT[:], dram["ctxT"]).then_inc(k.ctx_loaded, 16)
    sp.dma_start(k.cols[:], dram["cols"]).then_inc(k.small_loaded, 16)
    sp.dma_start(k.rows[:], dram["rows"].broadcast_to([P, NROWS])).then_inc(k.small_loaded, 16)
    sp.dma_start(k.gates[:, 0:2 * E2], dram["router2"]).then_inc(k.small_loaded, 16)
    sp.dma_start(k.gates[:, 2 * E2:], dram["gw3"]).then_inc(k.small_loaded, 16)
    sp.dma_start(k.ctxK, dram["ctxK"]).then_inc(k.l0x_loaded, 16)
    sp.dma_start(k.Wqv, dram["Wqv"]).then_inc(k.l0x_loaded, 16)
    sp.dma_start(k.W1_0, dram["w1_0"]).then_inc(k.l0f_loaded, 16)
    sp.dma_start(k.W2_0, dram["w2_0"]).then_inc(k.l0f_loaded, 16)
    sp.dma_start(k.b2_0, dram["b2_0"]).then_inc(k.l0f_loaded, 16)
    sp.dma_start(k.gw0, dram["gw0"]).then_inc(k.l0f_loaded, 16)
    for n in range(2):
        sp.dma_start(k.Wa[n], dram[f"wa{n + 1}"]).then_inc(k.att_loaded, 16)
    sp.dma_start(k.mask1, dram["mask1"]).then_inc(k.att_loaded, 16)
    sp.dma_start(k.RC[:, 6272:6400].bitcast(I32),
                 dram["mask2"].broadcast_to([P, B * C // 4])).then_inc(k.att_loaded, 16)
    sp.dma_start(k.RC[:, 0:2048], dram["w_q"]).then_inc(k.keys_loaded, 16)
    sp.dma_start(k.RC[:, 2048:2560], dram["keysT"]).then_inc(k.keys_loaded, 16)
    sp.dma_start(k.RC[:, 2560:3584], dram["downT"]).then_inc(k.keys_loaded, 16)
    sp.dma_start(k.RC[:, 3584:4608], dram["up"]).then_inc(k.keys_loaded, 16)


def fills(dve, k):
    dve.memset(k.eps[:], EPS).then_inc(k.zeroed, 1)
    dve.memset(k.head16[:], 1.0).then_inc(k.zeroed, 1)
    dve.memset(k.head2[:], 0.0).then_inc(k.zeroed, 1)
    dve.memset(k.pair_sel[:], 0.0).then_inc(k.zeroed, 1)
    dve.memset(k.one_sel[:], 0.0).then_inc(k.zeroed, 1)


def additive_masks(dve, k):
    dve.wait_ge(k.att_loaded, 64)
    dve.tensor_scalar(k.mask1_add, k.mask1, 0, FAR, ALU.is_equal, ALU.mult).then_inc(k.masks_made, 1)
    dve.tensor_scalar(k.mask2_add, k.mask2, 0, FAR, ALU.not_equal, ALU.mult).then_inc(k.masks_made, 1)


def constants(pool, k, own):
    own.settle(pool.iota(k.iota[:], pattern=[[1, E2]], base=0, channel_multiplier=0,
                         allow_small_or_imprecise_dtypes=True))
    own.settle(pool.memset(k.identb[:], 0.0))
    own.settle(pool.affine_select(out=k.identb[:], in_=k.identb[:], compare_op=ALU.not_equal, fill=1.0, base=0,
                                  pattern=[[-1, P]], channel_multiplier=1))
    pool.wait_ge(k.zeroed, 5)
    own.settle(pool.affine_select(out=k.head16[:], in_=k.head16[:], compare_op=ALU.is_ge, fill=0.0, base=0,
                                  pattern=[[-(P // H), H]], channel_multiplier=1))
    own.settle(pool.affine_select(out=k.head16[:], in_=k.head16[:], compare_op=ALU.is_ge, fill=0.0,
                                  base=P // H - 1, pattern=[[P // H, H]], channel_multiplier=-1))
    own.settle(pool.memset(k.head2[0:64, 0:1], 1.0))
    own.settle(pool.memset(k.head2[64:P, 1:2], 1.0))
    own.settle(pool.memset(k.before[:], 1.0))
    own.settle(pool.affine_select(out=k.before[:], in_=k.before[:], compare_op=ALU.is_gt, fill=0.0, base=0,
                                  pattern=[[1, G3], [-1, G3]], channel_multiplier=0))
    for part in range(PARTS):
        own.settle(pool.affine_select(out=k.pair_sel[:], in_=k.pair_sel[:], compare_op=ALU.not_equal,
                                      fill=1.0, base=-part * E2, pattern=[[-2, PAIRS], [-1, 2], [0, FH]],
                                      channel_multiplier=1))
        own.settle(pool.affine_select(out=k.one_sel[:], in_=k.one_sel[:], compare_op=ALU.not_equal,
                                      fill=1.0, base=-part * E0, pattern=[[-1, E0], [0, P]],
                                      channel_multiplier=1))



def similarity_attention(k):
    nc, PS, RB = k.nc, k.PS, k.RB
    nm = Norm(k, "l0x", k.X)
    n, fit = E0 * F0, (E0 - 1) * F0
    split = k.l0f_split = Rests(k, "l0f_w", [("RA", 0, n, "RB", 10496, P), ("RA", n, fit, "RA", 8448, P),
                                             ("RA", n + fit, F0, "RB", 10496 + n, P)])
    vec, gps = k.sem("l0x_vector"), k.sem("l0x_gpsimd")
    w_ready, sim_ready = k.sem("l0x_w_ready"), k.sem("l0x_sim_ready")
    max_ready, shifted, exped = k.sem("l0x_max_ready"), k.sem("l0x_shifted"), k.sem("l0x_exped")
    a_ready, at_turned, at_ready = k.sem("l0x_a_ready"), k.sem("l0x_at_turned"), k.sem("l0x_at_ready")
    mt_ready, bshift, bexp = k.sem("l0x_mt_ready"), k.sem("l0x_bshift"), k.sem("l0x_bexp")
    batt_ready, bc_turned, bc_ready = k.sem("l0x_batt_ready"), k.sem("l0x_bc_turned"), k.sem("l0x_bc_ready")
    hc_done, w14_ready = k.sem("l0x_hc_done"), k.sem("l0x_w14_ready")
    hq_done, hq_ready, f3_ready = k.sem("l0x_hq_done"), k.sem("l0x_hq_ready"), k.sem("l0x_f3_ready")
    out_done, biased, x_added = k.sem("l0x_out_done"), k.sem("l0x_biased"), k.sem("l0x_x_added")

    R = RB[:, 1536:2048]
    w2b = RB[:, 2048:2176]
    sim = RB[:, 2304:3328].rearrange("p (t c) -> p t c", t=NT)
    w14 = RB[:, 3328:4352].rearrange("p (b n) -> p b n", b=B)
    AT = RB[0:C, 4352:6400]
    HQ = RB[:, 6400:8448]
    F3 = RB[:, 8448:10496]
    qmax = k.RW[:, 0:NT]
    qsum = k.RW[:, 16:32]
    qrec = k.RW[:, 32:48]
    batt = k.RW[0:B, 64:64 + S]
    bsum = k.RW[0:B, 400:401]
    brec = k.RW[0:B, 401:402]
    bmax = k.RW[0:B, 402:403]
    bcol = k.RW[:, 416:432].rearrange("p (j b) -> p j b", j=2)
    hc = k.RW[:, 432:440]
    ones = k.RB[:, 2176:2304]
    SIM, MT, BC, HC = 4, 6, 6, 7
    sim_ps = PS[:, SIM:SIM + 2, :].rearrange("p a (t c) -> p (a t) c", c=C)
    q2 = qmax.rearrange("p (b j) -> p j b", j=2)

    with nc.Block() as block:

        @block.sync
        def _(sp):
            loads(sp, k)

        @block.gpsimd
        def _(pool):
            k.clear_last(pool)
            own = Tally(pool, gps)
            constants(pool, k, own)
            pool.wait_ge(nm.xn_ready, NT)
            pool.wait_ge(k.small_loaded, 64)
            pool.tensor_tensor(k.X[:], k.X[:], over(k.row("b_qv"), 1, NT), ALU.add).then_inc(biased, 1)
            split.gpsimd(pool)

        @block.vector
        def _(dve):
            own = Tally(dve, vec)
            fills(dve, k)
            norm_vector(dve, k, nm, own, loaded=k.x_loaded)
            own.mark(dve.memset(ones, 1.0))
            dve.wait_ge(k.ctx_loaded, 16)
            dve.wait_ge(k.small_loaded, 64)
            own.settle(dve.tensor_scalar(R, k.ctxT[:], k.col("w_sim", 2), k.col("w_sim", 0), ALU.mult, ALU.add))
            dve.tensor_scalar(w2b, ones, k.col("w_sim", 1), None, ALU.mult).then_inc(w_ready, 1)
            dve.wait_ge(sim_ready, 1)
            own.settle(dve.tensor_scalar(sim, sim_ps, k.row("b_sim"), None, ALU.add))
            dve.tensor_reduce(qmax, sim, AX.X, ALU.max).then_inc(max_ready, 1)
            dve.wait_ge(max_ready, 1)
            dve.tensor_tensor(sim, sim, over(qmax, 2, C), ALU.subtract).then_inc(shifted, 1)
            dve.wait_ge(mt_ready, 1)
            own.settle(dve.tensor_reduce(bmax, PS[0:B, MT, 0:S], AX.X, ALU.max))
            dve.tensor_scalar(batt, PS[0:B, MT, 0:S], bmax, None, ALU.subtract).then_inc(bshift, 1)
            dve.wait_ge(exped, 1)
            own.settle(dve.tensor_reduce(qsum, sim, AX.X, ALU.add))
            own.settle(dve.reciprocal(qrec, qsum))
            dve.tensor_tensor(sim, sim, over(qrec, 2, C), ALU.mult).then_inc(a_ready, 1)
            dve.wait_ge(bexp, 1)
            own.settle(dve.reciprocal(brec, bsum))
            dve.tensor_scalar(batt, batt, brec, None, ALU.mult).then_inc(batt_ready, 1)
            dve.wait_ge(k.l0f_loaded, 64)
            split.vector(dve, 0, 3)
            dve.wait_ge(bc_turned, 1)
            dve.tensor_copy(bcol, PS[:, BC, 0:2 * B].rearrange("p (j b) -> p j b", j=2)).then_inc(bc_ready, 1)
            dve.wait_ge(hc_done, 1)
            own.settle(dve.tensor_copy(hc, PS[:, HC, 0:B]))
            dve.wait_ge(k.l0x_loaded, 32)
            for b in range(B):
                ins = dve.scalar_tensor_tensor(w14[:, b, :], k.Wqv[:, 3, :], hc[:, b:b + 1], k.Wqv[:, 0, :],
                                               ALU.mult, ALU.add)
            ins.then_inc(w14_ready, 1)
            for q in range(NB):
                dve.wait_ge(hq_done, q + 1)
                dve.tensor_tensor(F3[:, bass.ts(q, BLK)], k.XT[:, bass.ts(q, BLK)], PS[:, q, :],
                                  ALU.mult).then_inc(f3_ready, 1)
            dve.wait_ge(biased, 1)

            def count_block(q):
                for t in range(TPB * q, TPB * (q + 1)):
                    count_tile(dve, k, k.X, t, x_added, q + 1, None)

            for q in range(NB):
                dve.wait_ge(out_done, q + 1)
                xq = k.X[:, TPB * q:TPB * (q + 1), :].rearrange("p t d -> p (t d)")
                dve.tensor_tensor(xq, xq, PS[:, 4 + q, :], ALU.add).then_inc(x_added, 1)
                if q >= 1:
                    count_block(q - 1)
            count_block(NB - 1)
            additive_masks(dve, k)

        @block.scalar
        def _(act):
            norm_scalar(act, k, nm)
            act.wait_ge(shifted, 1)
            act.activation(sim, sim, ACT.Exp).then_inc(exped, 1)
            act.wait_ge(bshift, 1)
            act.activation(batt, batt, ACT.Exp, accum_out=bsum).then_inc(bexp, 1)
            act.wait_ge(at_turned, 1)
            for q in range(NB):
                act.activation(AT[:, bass.ts(q, BLK)], PS[0:C, q, :], ACT.Copy).then_inc(at_ready, 1)
            for q in range(NB):
                act.wait_ge(hq_done, q + 1)
                act.wait_ge(f3_ready, q + 1)
                act.activation(HQ[:, bass.ts(q, BLK)], PS[:, q, :], ACT.Copy).then_inc(hq_ready, 1)
            split.scalar(act)

        @block.tensor
        def _(pe):
            norm_tensor(pe, k, nm)
            pe.wait_ge(w_ready, 1)
            pe.wait_ge(nm.xt_ready, NB)
            for t in range(NT):
                b = t // 2
                pe.matmul(sim_ps[:, t, :], k.XT[:, bass.ts(t, P)], R[:, bass.ts(b, C)], start=True, stop=False)
                mm = pe.matmul(sim_ps[:, t, :], w2b, k.ctxT[:, bass.ts(b, C)], start=False, stop=True)
            mm.then_inc(sim_ready, 1)
            pe.wait_ge(max_ready, 1)
            for j in range(2):
                mm = pe.transpose(PS[0:B, MT, bass.ts(j, P)], q2[:, j, :], k.identf[:])
            mm.then_inc(mt_ready, 1)
            pe.wait_ge(a_ready, 1)
            for t in range(NT):
                mm = pe.transpose(PS[0:C, t // TPB, bass.ts(t % TPB, P)], sim[:, t, :], k.identf[:])
            mm.then_inc(at_turned, 1)
            pe.wait_ge(batt_ready, 1)
            for j in range(2):
                mm = pe.transpose(PS[:, BC, bass.ts(j, B)], batt[:, bass.ts(j, P)], k.identf[0:B, 0:B])
            mm.then_inc(bc_turned, 1)
            pe.wait_ge(bc_ready, 1)
            for b in range(B):
                for j in range(2):
                    mm = pe.matmul(PS[:, HC, b:b + 1], k.XN[:, 2 * b + j, :], bcol[:, j, b:b + 1],
                                   start=(j == 0), stop=(j == 1))
            mm.then_inc(hc_done, 1)
            pe.wait_ge(k.l0x_loaded, 32)
            for b in range(B):
                pe.wait_ge(at_ready, NB)
                mm = pe.matmul(PS[:, b // 2, bass.ts(b % 2, S)], k.ctxK[:, b, :], AT[:, bass.ts(b, S)],
                               start=True, stop=True)
                if b % 2:
                    mm.then_inc(hq_done, 1)
            pe.wait_ge(w14_ready, 1)
            pe.wait_ge(hq_ready, NB)
            for t in range(NT):
                o = PS[:, 4 + t // TPB, bass.ts(t % TPB, P)]
                pe.matmul(o, k.XT[:, bass.ts(t, P)], w14[:, t // 2, :], start=True, stop=False)
                pe.matmul(o, HQ[:, bass.ts(t, P)], k.Wqv[:, 1, :], start=False, stop=False)
                mm = pe.matmul(o, F3[:, bass.ts(t, P)], k.Wqv[:, 2, :], start=False, stop=True)
                if t % TPB == TPB - 1:
                    mm.then_inc(out_done, 1)



class Step:

    def __init__(self, gate, up, down, bias=0.0, spread=None, fresh=True):
        self.gate, self.up, self.down, self.bias = gate, up, down, bias
        self.spread, self.fresh = spread, fresh
        self.rows = gate[0].shape[1]


def product3(pe, out, w, x, start, stop):
    (wh, wl), (xh, xl) = w, x
    pe.matmul(out, wh, xh, start=start, stop=False)
    pe.matmul(out, wh, xl, start=False, stop=False)
    return pe.matmul(out, wl, xh, start=False, stop=stop)


class Rests:

    def __init__(self, k, name, parts):
        self.parts = []
        for n, (region, at, width, rest_region, rest_at, rows) in enumerate(parts):
            whole = k.region[region][0:rows, at:at + width]
            high = k.rounded(f"{name}_high{n}", region, at, width, rows)
            rest = k.rounded(f"{name}_rest{n}", rest_region, rest_at, width, rows)
            self.parts.append((whole, high, rest))
        self.rounded = k.sem(f"{name}_rounded")
        self.subtracted = k.sem(f"{name}_subtracted")
        self.ready = k.sem(f"{name}_parts_split")

    def vector(self, dve, first, last):
        for whole, high, rest in self.parts[first:last]:
            dve.tensor_copy(rest, whole).then_inc(self.rounded, 1)

    def gpsimd(self, pool):
        for n, (whole, high, rest) in enumerate(self.parts):
            pool.wait_ge(self.rounded, n + 1)
            pool.tensor_tensor(rest, whole, rest, ALU.subtract).then_inc(self.subtracted, 1)

    def scalar(self, act, first=0, last=None):
        for n, (whole, high, rest) in enumerate(self.parts[first:last], first):
            act.wait_ge(self.subtracted, n + 1)
            act.activation(high, whole, ACT.Copy).then_inc(self.ready, 1)


class Experts:

    GATE, UP, SPREAD, ACC, TURN = 0, 2, 4, 6, 7

    def __init__(self, k, name, passes, func, rests, xt, now):
        self.k, self.passes, self.func = k, passes, func
        self.rests, self.xt, self.now = rests, xt, now
        _, self.XH, self.XL = rests.parts[xt]
        self.gate_ready = k.sem(f"{name}_gate_ready")
        self.acted = k.sem(f"{name}_acted")
        self.up_ready = k.sem(f"{name}_up_ready")
        self.multiplied = k.sem(f"{name}_multiplied")
        self.spread_ready = k.sem(f"{name}_spread_ready")
        self.weighted = k.sem(f"{name}_weighted")
        self.rounded = k.sem(f"{name}_hid_rounded")
        self.hidden_ready = k.sem(f"{name}_hidden_ready")
        self.down_done = k.sem(f"{name}_down_done")
        self.acc_read = k.sem(f"{name}_acc_read")
        self.out_turned = k.sem(f"{name}_out_turned")
        self.out_added = k.sem(f"{name}_out_added")
        self.paced, self.paced_count = k.sem(f"{name}_paced"), k.sem(f"{name}_paced_count")
        self.K = len(passes[0])
        self.A = [k.RW[:, bass.ts(n, BLK)] for n in range(2)]
        self.M = k.RW[:, bass.ts(2, BLK)]
        self.OT = k.RW[:, bass.ts(3, BLK)]
        self.lag = 3
        self.even = self.K // 4 * 4
        self.HID, self.HIGH, self.REST = [], [], []
        high = k.rounded(f"{name}_hid_high", "RB", 0, 5 * BLK)
        rest = k.rounded(f"{name}_hid_rest", "RB", 5 * BLK, 5 * BLK)
        for c in range(self.K):
            slot = c % 4 if c < self.even else 4
            self.HID.append(k.RW[:, bass.ts(4 + c % 2, BLK)])
            self.HIGH.append(high[:, bass.ts(slot, BLK)])
            self.REST.append(rest[:, bass.ts(slot, BLK)])
        self.no, self.last, n = [], {}, -1
        for c, st in enumerate(passes[0]):
            n += st.spread is not None and st.fresh
            self.no.append(n)
            if st.spread is not None:
                self.last[n] = c
        self.KS = n + 1

    def vector_rests(self, dve, nm):
        self.rests.vector(dve, 0, self.xt)
        dve.wait_ge(nm.xt_ready, NB)
        self.rests.vector(dve, self.xt, len(self.rests.parts))

    def scalar_rests(self, act, xt_used):
        self.rests.scalar(act, 0, self.xt)
        act.wait_ge(xt_used, 1)
        self.rests.scalar(act, self.xt, self.now)
        act.preload_act_table(self.func)

    def bank_user(self, j, c):
        if c >= 2 or known(j, 1):
            odd = self.K % 2 and c == 0
            return j * self.K + (0 if odd else c - 1)
        return None

    def slot_user(self, j, c):
        if 4 <= c < self.even:
            return j * self.K + c - 3
        if known(j, 1):
            return j * self.K - self.K + (self.even - 3 + c if c < 4 else c + 1)
        return None

    def spread_user(self, j, n):
        if n >= 2:
            return j * self.K + self.last[n - 2] + 1
        if known(j, 1):
            return j * self.K - self.K + self.last[self.KS - 2 + n] + 1
        return None

    def blocks(self, eng, block):
        for g, steps in enumerate(self.passes):
            before = self.passes[max(g - 1, 0)]
            block(g * NB, 0, g, steps, before)
            with eng.Fori(1, NB) as i:
                block(i + g * NB, i, g, steps, steps)


def wait_user(eng, sem, count):
    if count is not None:
        eng.wait_ge(sem, count)


def experts_tensor(pe, e, r, extra=None):
    k, K, PS = e.k, e.K, e.k.PS

    def down(j, c, st):
        pe.wait_ge(e.hidden_ready, j * K + c + 1)
        rows = slice(0, st.rows)
        product3(pe, PS[:, e.ACC, :], st.down, (e.HIGH[c][rows, :], e.REST[c][rows, :]),
                 start=(c == 0 and extra is None), stop=(c == K - 1)).then_inc(e.down_done, 1)

    def turn():
        for r in range(TPB):
            mm = pe.transpose(PS[:, e.TURN, bass.ts(r, P)], e.OT[:, bass.ts(r, P)], k.identf[:])
        mm.then_inc(e.out_turned, 1)

    def block(j, i, g, steps, before):
        if isinstance(i, int):
            pe.wait_ge(e.rests.ready, e.now if g == 0 else len(e.rests.parts))
        if isinstance(j, int) and j == 0:
            pe.wait_ge(r.wt_ready, r.G)
        x = (e.XH[:, bass.ts(i, BLK)], e.XL[:, bass.ts(i, BLK)])
        for c, st in enumerate(steps):
            wait_user(pe, e.acted, e.bank_user(j, c))
            if st.rows < P:
                pe.sem_inc(e.paced, 1)
            product3(pe, PS[0:st.rows, e.GATE + c % 2, :], st.gate, x, True, True).then_inc(e.gate_ready, 1)
            if st.up is not None:
                wait_user(pe, e.multiplied, e.bank_user(j, c))
                if st.rows < P:
                    pe.sem_inc(e.paced, 1)
                product3(pe, PS[0:st.rows, e.UP + c % 2, :], st.up, x, True, True).then_inc(e.up_ready, 1)
            if isinstance(j, int) and j == 0 and c == 0:
                pe.wait_ge(r.wt_ready, r.stores)
            if st.spread is not None and st.fresh:
                n = e.no[c]
                sel, group = st.spread
                wait_user(pe, e.weighted, e.spread_user(j, n))
                if e.spread_user(j, n) is not None and sel.shape[0] <= 32:
                    pe.sem_inc(e.paced, 1)
                pe.matmul(PS[:, e.SPREAD + n % 2, :], sel, r.WT[:, group, bass.ts(i, BLK)], start=True,
                          stop=True).then_inc(e.spread_ready, 1)
            if c >= e.lag:
                if c == e.lag and known(j, 1):
                    pe.wait_ge(e.acc_read, j)
                if c == e.lag and extra is not None:
                    pe.sem_inc(e.paced, 1)
                    extra(pe, i)
                down(j, c - e.lag, steps[c - e.lag])
            elif known(j, 1):
                down(j - 1, K - e.lag + c, before[K - e.lag + c])
            if c == e.lag + 1 and known(j, 1):
                turn()

    e.blocks(pe, block)
    last = len(e.passes) * NB - 1
    for c in range(K - e.lag, K):
        down(last, c, e.passes[-1][c])
    pe.wait_ge(e.acc_read, last + 1)
    turn()


def experts_scalar(act, e):
    PS, K = e.k.PS, e.K

    def copy_sum(blocks):
        act.wait_ge(e.down_done, blocks * K)
        act.activation(e.OT, PS[:, e.ACC, :], ACT.Copy).then_inc(e.acc_read, 1)

    def block(j, i, g, steps, before):
        for c, st in enumerate(steps):
            act.wait_ge(e.gate_ready, j * K + c + 1)
            wait_user(act, e.multiplied if st.up is not None else e.weighted, e.bank_user(j, c))
            act.activation(e.A[c % 2][0:st.rows, :], PS[0:st.rows, e.GATE + c % 2, :], e.func,
                           bias=st.bias).then_inc(e.acted, 1)
            if c == e.lag and known(j, 1):
                copy_sum(j)
            later = e.now + c // 2 - 3
            if isinstance(j, int) and j == 0 and c % 2 == 0 and e.now <= later < len(e.rests.parts):
                e.rests.scalar(act, later, later + 1)

    e.blocks(act, block)
    copy_sum(len(e.passes) * NB)


def experts_vector(dve, e, count=True):
    k, PS, K = e.k, e.k.PS, e.K
    place = lambda slots, c, st: slots[c][0:st.rows, :]

    def round_hidden(j, c, st):
        dve.wait_ge(e.weighted, j * K + c + 1)
        wait_user(dve, e.down_done, e.slot_user(j, c))
        dve.tensor_copy(place(e.HIGH, c, st), place(e.HID, c, st)).then_inc(e.rounded, 1)

    def round_before(j, c, steps, before):
        if c >= 1:
            round_hidden(j, c - 1, steps[c - 1])
        elif known(j, 1):
            round_hidden(j - 1, K - 1, before[K - 1])

    def add_sum(block, i):
        dve.wait_ge(e.out_turned, block)
        x = k.X[:, bass.ts(i, TPB), :].rearrange("p t d -> p (t d)")
        dve.tensor_tensor(x, x, PS[:, e.TURN, :], ALU.add).then_inc(e.out_added, 1)

    def count_block(blocks, i):
        if count:
            for r in range(TPB):
                count_tile(dve, k, k.X, i * TPB + r, e.out_added, blocks, e.paced_count)

    def block(j, i, g, steps, before):
        for c, st in enumerate(steps):
            m = j * K + c
            rows = slice(0, st.rows)
            a = e.A[c % 2][rows, :]
            if st.up is None:
                round_before(j, c, steps, before)
            dve.wait_ge(e.acted, m + 1)
            if st.up is not None:
                dve.wait_ge(e.up_ready, m + 1)
                if known(j, 1) or c >= 1:
                    dve.wait_ge(e.weighted, m)
                dve.tensor_tensor(e.M[rows, :], a, PS[rows, e.UP + c % 2, :], ALU.mult).then_inc(e.multiplied, 1)
                round_before(j, c, steps, before)
                dve.wait_ge(e.multiplied, m + 1)
                a = e.M[rows, :]
            wait_user(dve, e.hidden_ready, e.bank_user(j, c))
            hid = place(e.HID, c, st)
            if st.spread is None:
                dve.tensor_copy(hid, a).then_inc(e.weighted, 1)
            else:
                dve.wait_ge(e.spread_ready, j * e.KS + e.no[c] + 1)
                dve.tensor_tensor(hid, a, PS[:, e.SPREAD + e.no[c] % 2, :], ALU.mult).then_inc(e.weighted, 1)
            if c == e.lag + 2 and known(j, 1):
                add_sum(j, (NB - 1) if isinstance(i, int) else i - 1)
            if c == e.lag + 3 and g == len(e.passes) - 1 and not isinstance(i, int):
                count_block(j, i - 1)

    e.blocks(dve, block)
    last = len(e.passes) * NB - 1
    round_hidden(last, K - 1, e.passes[-1][K - 1])
    add_sum(last + 1, NB - 1)
    count_block(last + 1, NB - 1)


def experts_gpsimd(pool, e):
    def block(j, i, g, steps, before):
        for c, st in enumerate(steps):
            pool.wait_ge(e.rounded, j * e.K + c + 1)
            wait_user(pool, e.down_done, e.slot_user(j, c))
            hid, high, rest = (slots[c][0:st.rows, :] for slots in (e.HID, e.HIGH, e.REST))
            pool.tensor_tensor(rest, hid, high, ALU.subtract).then_inc(e.hidden_ready, 1)

    e.blocks(pool, block)



class Route:

    LOGITS = 4

    def __init__(self, k, name, experts, groups, whole=False):
        self.k, self.E, self.G, self.R, self.whole = k, experts, groups, NT * groups, whole
        n = NT * groups * experts
        RB = k.RB
        self.rows = lambda at: RB[:, at:at + n].rearrange("p (r e) -> p r e", e=experts)
        self.L, self.W, self.T1, self.T2 = (self.rows(at) for at in (0, 1024, 2048, 3072))
        self.parts = RB[:, 4096:4096 + n * PARTS // 2].bitcast(BF16).rearrange(
            "p (r a e) -> p r a e", a=PARTS, e=experts)
        self.top = RB[:, 5632:5632 + 8 * self.R].rearrange("p (r j) -> p r j", j=8)
        self.at = RB[:, 5888:5888 + 8 * self.R].bitcast(U32).rearrange("p (r j) -> p r j", j=8)
        self.z = RB[:, 6144:6144 + self.R]
        self.rz = RB[:, 6208:6208 + self.R]
        self.WT = RB[0:PARTS * experts, 6272:6272 + groups * T // 2].bitcast(BF16).rearrange(
            "p (g t) -> p g t", g=groups)
        self.WT32 = RB[0:experts, 8320:8320 + T]
        self.logits_ready = k.sem(f"{name}_logits_ready")
        self.shifted = k.sem(f"{name}_route_shifted")
        self.exped = k.sem(f"{name}_route_exped")
        self.parts_ready = k.sem(f"{name}_parts_ready")
        self.parts_turned = k.sem(f"{name}_parts_turned")
        self.wt_ready = k.sem(f"{name}_wt_ready")
        self.logits = k.PS[:, self.LOGITS:self.LOGITS + 2, :].rearrange("p a f -> p (a f)")[:, 0:n]
        self.stores = 2 * groups + (NB if whole else 0)


def route_logits(pe, k, r, nm, gate, b):
    w = r.G * r.E
    pe.wait_ge(nm.xt_ready, b + 1)
    for t in range(TPB * b, TPB * (b + 1)):
        mm = pe.matmul(r.logits[:, bass.ts(t, w)], k.XT[:, bass.ts(t, P)], gate, start=True, stop=True)
    if b == NB - 1:
        mm.then_inc(r.logits_ready, 1)


def route_top2(dve, k, r, own, bias, renormalise):
    dve.wait_ge(r.logits_ready, 1)
    lg = r.logits.rearrange("p (r e) -> p r e", e=r.E)
    if bias is None:
        own.settle(dve.tensor_copy(r.L, lg))
    else:
        own.settle(dve.tensor_tensor(r.L, lg, over(bias, 1, r.R), ALU.add))
    for j in range(r.R):
        own.mark(dve.max(r.top[:, j, :], r.L[:, j, :]))
    own.wait()
    dve.tensor_tensor(r.W, r.L, r.top[:, :, 0:1].broadcast_to([P, r.R, r.E]), ALU.subtract).then_inc(r.shifted, 1)
    for j in range(r.R):
        own.mark(dve.max_index(r.at[:, j, :], r.top[:, j, :], r.L[:, j, :]))
    own.wait()
    iota = over(k.iota[:, 0:r.E], 1, r.R)
    own.mark(dve.tensor_tensor(r.T1, iota, r.at[:, :, 0:1].broadcast_to([P, r.R, r.E]), ALU.is_equal))
    own.settle(dve.tensor_tensor(r.T2, iota, r.at[:, :, 1:2].broadcast_to([P, r.R, r.E]), ALU.is_equal))
    own.settle(dve.tensor_tensor(r.T1, r.T1, r.T2, ALU.add))
    dve.wait_ge(r.exped, 1)
    if not renormalise:
        own.settle(dve.tensor_reduce(r.z, r.W, AX.X, ALU.add))
    own.settle(dve.tensor_tensor(r.W, r.W, r.T1, ALU.mult))
    if renormalise:
        own.settle(dve.tensor_reduce(r.z, r.W, AX.X, ALU.add))
    own.settle(dve.reciprocal(r.rz, r.z))
    if not renormalise:
        own.settle(dve.tensor_scalar(r.rz, r.rz, 0.5, None, ALU.mult))
    own.settle(dve.tensor_tensor(r.W, r.W, over(r.rz, 2, r.E), ALU.mult))
    route_parts(dve, r, own)


def route_parts(dve, r, own):
    for h in range(2):
        rows = slice(h * r.R // 2, (h + 1) * r.R // 2)
        w, left, parts = r.W[:, rows, :], r.T1[:, rows, :], r.parts[:, rows, :, :]
        own.settle(dve.tensor_copy(parts[:, :, 0, :], w))
        own.settle(dve.tensor_tensor(left, w, parts[:, :, 0, :], ALU.subtract))
        own.settle(dve.tensor_copy(parts[:, :, 1, :], left))
        own.settle(dve.tensor_tensor(left, left, parts[:, :, 1, :], ALU.subtract))
        dve.tensor_copy(parts[:, :, 2, :], left).then_inc(r.parts_ready, 1)


def route_exp(act, r):
    act.wait_ge(r.shifted, 1)
    act.activation(r.W, r.W, ACT.Exp).then_inc(r.exped, 1)


def route_turn(pe, k, r):
    n = PARTS * r.E
    for h in range(2):
        pe.wait_ge(r.parts_ready, h + 1)
        for g in range(r.G):
            for t in range(h * NT // 2, (h + 1) * NT // 2):
                mm = pe.transpose(k.PB[0:n, 2 * g + h, bass.ts(t % 8, P)],
                                  r.parts[:, t * r.G + g, :, :].rearrange("p a e -> p (a e)"), k.identb[:])
            mm.then_inc(r.parts_turned, 1)
    if r.whole:
        for t in range(NT):
            mm = pe.transpose(k.PS[0:r.E, 4 + t // TPB, bass.ts(t % TPB, P)], r.W[:, t, :], k.identf[:])
        mm.then_inc(r.parts_turned, 1)


def route_store(act, k, r):
    n, m = PARTS * r.E, 0
    for h in range(2):
        for g in range(r.G):
            m += 1
            act.wait_ge(r.parts_turned, m)
            act.activation(r.WT[:, g, bass.ts(h, T // 2)], k.PB[0:n, 2 * g + h, :], ACT.Copy).then_inc(r.wt_ready, 1)
    if r.whole:
        act.wait_ge(r.parts_turned, m + 1)
        for q in range(NB):
            act.activation(r.WT32[:, bass.ts(q, BLK)], k.PS[0:r.E, 4 + q, :], ACT.Copy).then_inc(r.wt_ready, 1)



def gelu_experts(k):
    nm, r = Norm(k, "l0f", k.X, counted=True), Route(k, "l0f", E0, 1, whole=True)
    rests = Rests(k, "l0f", [("XT", 0, T, "XN", 0, P)])
    w1, w2, w2_last = (part[1:] for part in k.l0f_split.parts)
    fit = (E0 - 1) * F0
    chunk = lambda pair, c: tuple(a[:, bass.ts(c, P)] for a in pair)
    last = fit // P
    steps = [Step(chunk(w1, c), None, chunk(w2, c) if c < last else chunk(w2_last, c - last),
                  bias=k.col("b1_0", c), spread=(k.one_sel[:, c // K0, :], 0), fresh=(c % K0 == 0))
             for c in range(E0 * K0)]
    ex = Experts(k, "l0f", [steps], ACT.Gelu, rests, xt=0, now=1)
    vec = k.sem("l0f_vector")

    def bias2(pe, i):
        pe.matmul(k.PS[:, ex.ACC, :], k.b2_0, r.WT32[:, bass.ts(i, BLK)], start=True, stop=False)

    with k.nc.Block() as block:

        @block.gpsimd
        def _(pool):
            k.clear_last(pool)
            ex.rests.gpsimd(pool)
            experts_gpsimd(pool, ex)

        @block.vector
        def _(dve):
            own = Tally(dve, vec)
            norm_vector(dve, k, nm, own)
            ex.vector_rests(dve, nm)
            route_top2(dve, k, r, own, k.row("gate_b"), renormalise=True)
            experts_vector(dve, ex)

        @block.scalar
        def _(act):
            norm_scalar(act, k, nm)
            route_exp(act, r)
            ex.scalar_rests(act, r.logits_ready)
            route_store(act, k, r)
            experts_scalar(act, ex)

        @block.tensor
        def _(pe):
            pe.wait_ge(k.l0f_loaded, 64)
            norm_tensor(pe, k, nm, behind=lambda b: route_logits(pe, k, r, nm, k.gw0, b))
            route_turn(pe, k, r)
            experts_tensor(pe, ex, r, extra=bias2)



class Heads:

    def __init__(self, name, chunks, wq, wk, wv, wo, bq, bk, bv, scale, head_mask, QT, VT,
                 spare, bk_all, counted, mask=None, per_tile=False):
        self.counted = counted
        self.name, self.chunks, self.spare, self.bk_all = name, chunks, spare, bk_all
        self.wq, self.wk, self.wv, self.wo = wq, wk, wv, wo
        self.bq, self.bk, self.bv, self.scale = bq, bk, bv, scale
        self.head_mask, self.QT, self.VT = head_mask, QT, VT
        self.mask, self.per_tile = mask, per_tile


def heads_attention(k, hd, bias_row, weights_loaded, before=None, after=None):
    nc, PS = k.nc, k.PS
    nm = Norm(k, hd.name, k.X, counted=hd.counted)
    target = k.XN if after else k.X
    s = lambda what: k.sem(f"{hd.name}_{what}")
    vec = s("vector")
    k_ready, v_ready, v_biased, bk_masked = s("k_ready"), s("v_ready"), s("v_biased"), s("bk_masked")
    k_masked, paced = (s("k_masked_vector"), s("k_masked_scalar")), s("paced")
    v_spread, vw_ready, vw_stored = s("v_spread"), s("vw_ready"), s("vw_stored")
    q_ready, q_stored, score_ready, shifted = s("q_ready"), s("q_stored"), s("score_ready"), s("shifted")
    exped, summed, normed, p_turned, p_stored = s("exped"), s("summed"), s("normed"), s("p_turned"), s("p_stored")
    out_ready, out_added, biased = s("out_ready"), s("out_added"), s("biased")

    NC, HPC = hd.chunks, H // hd.chunks
    Kall = k.RB[:, 0:8192].rearrange("p (b h c) -> p b h c", b=B, h=H)
    Kflat = k.RB[:, 0:8192].rearrange("p (b n) -> p b n", b=B)
    VW = k.RB[:, 8192:16384].rearrange("p (b c n) -> p b c n", b=B, n=D)
    VWflat = k.RB[:, 8192:16384].rearrange("p (b n) -> p b n", b=B)
    SS = hd.spare + [k.RW[:, bass.ts(r, HC)] for r in range(2)]
    PT = k.RW[:, 2 * HC:3 * HC]
    VM = SS[2:4]
    small = k.RW[:, 3 * HC:]
    top, tot, rec = ([small[:, at + H * r:at + H * (r + 1)] for r in range(4)] for at in (512, 576, 640))
    PTB, OUT, Q = 4, 6, 7
    score = [PS[:, 2 * r:2 * r + 2, :].rearrange("p a f -> p (a f)") for r in range(2)]
    vw_ps = [PS[:, 4 + 2 * r:6 + 2 * r, :].rearrange("p a f -> p (a f)") for r in range(2)]
    turn_ps = PS[:, PTB:PTB + 2, :].rearrange("p a f -> p (a f)")
    masked_bk = small[:, 704:704 + H]
    key_jobs = [(c, range(HPC)) for c in range(NC)] if NC > 1 else [(0, range(0, H // 2)), (0, range(H // 2, H))]
    key_bank = lambda n: PS[:, n % 2, :].rearrange("p (b c) -> p b c", b=B)
    JOBS = max(1, NC // 2)
    CPJ = NC // JOBS

    def query_bank(b, j, ahead):
        return Q if not ahead else 2 + j % 2 if b == 0 else Q - j % 2

    with nc.Block() as block:

        if before is not None:
            @block.sync
            def _(sp):
                before(sp)

        @block.vector
        def _(dve):
            own = Tally(dve, vec)
            dve.tensor_tensor(masked_bk.rearrange("p (n h) -> p n h", n=NC), over(hd.bk_all, 2, HPC),
                              over(hd.head_mask, 1, NC), ALU.mult).then_inc(bk_masked, 1)
            norm_vector(dve, k, nm, own)
            if after:
                dve.wait_ge(nm.xt_turned, NB)
            dve.wait_ge(nm.xn_ready, NT)
            dve.tensor_tensor(target[:], target[:], over(k.row(bias_row), 1, NT), ALU.add).then_inc(biased, 1)
            for n, (c, heads) in enumerate(key_jobs):
                if n % 2 == 0:
                    dve.wait_ge(k_ready, n + 1)
                    for h in heads:
                        ins = dve.tensor_scalar(Kall[:, :, c * HPC + h, :], key_bank(n), hd.bk(c),
                                                hd.head_mask[:, h:h + 1], ALU.add, ALU.mult)
                    ins.then_inc(k_masked[0], 1)

            def add_out(n):
                dve.wait_ge(out_ready, n + 1)
                x = target[:, n, :]
                dve.tensor_tensor(x, x, PS[:, OUT, 0:D], ALU.add).then_inc(out_added, 1)

            def total(n, r):
                dve.wait_ge(exped, n + 1)
                own.settle(dve.tensor_reduce(tot[r], SS[r].rearrange("p (h c) -> p h c", c=C), AX.X, ALU.add))
                dve.reciprocal(rec[r], tot[r]).then_inc(summed, 1)

            def step(n, r):
                dve.wait_ge(score_ready, n + 1)
                if isinstance(n, int) and n == 2:
                    dve.wait_ge(vw_ready, B)
                if known(n, 4):
                    dve.wait_ge(p_turned, n - 3)
                sv = score[r % 2].rearrange("p (h c) -> p h c", c=C)
                own.settle(dve.tensor_reduce(top[r], sv, AX.X, ALU.max))
                dve.tensor_tensor(SS[r].rearrange("p (h c) -> p h c", c=C), sv, over(top[r], 2, C),
                                  ALU.subtract).then_inc(shifted, 1)
                if known(n, 1):
                    total(n - 1, (r - 1) % 4)
                if isinstance(n, int) and n == 3:
                    dve.wait_ge(biased, 1)
                if known(n, 3):
                    add_out(n - 3)
                if known(n, 4):
                    count_tile(dve, k, target, n - 4, out_added, n - 3, paced)

            for n in range(4):
                step(n, n)
            with dve.Fori(1, NT // 4) as i:
                own.enter(i - 1, 8)
                for r in range(4):
                    step(i * 4 + r, r)
            own.leave(NT // 4 - 1)
            total(NT - 1, 3)
            for n in range(NT - 3, NT):
                add_out(n)
                count_tile(dve, k, target, n - 1, out_added, n, paced)
            own.settle(count_tile(dve, k, target, NT - 1, out_added, NT, paced))
            if after:
                after.vector(dve, own, out_added)

        @block.scalar
        def _(act):
            def store_values():
                act.preload_act_table(ACT.Exp)
                for c in range(NC):
                    act.wait_ge(v_ready, c + 1)
                    act.activation(hd.VT[:, c, :], PS[:, 6 + c % 2, :], ACT.Identity,
                                   bias=hd.bv(c)).then_inc(v_biased, 1)

            def store_vw(b):
                act.wait_ge(vw_ready, b + 1)
                act.activation(VWflat[:, b, :], vw_ps[b % 2], ACT.Copy).then_inc(vw_stored, 1)

            norm_scalar(act, k, nm, first=store_values)
            act.wait_ge(bk_masked, 1)
            for n, (c, heads) in enumerate(key_jobs):
                if n % 2:
                    act.wait_ge(k_ready, n + 1)
                    for h in heads:
                        at = c * HPC + h
                        ins = act.activation(Kall[:, :, at, :], key_bank(n), ACT.Identity,
                                             bias=masked_bk[:, at:at + 1], scale=hd.head_mask[:, h:h + 1])
                    ins.then_inc(k_masked[1], 1)

            def store_q(b, slot, j, ahead=False):
                act.wait_ge(q_ready, b * JOBS + j + 1)
                bank = query_bank(b, j, ahead)
                for c in range(CPJ):
                    ins = act.activation(hd.QT[slot][:, j * CPJ + c, :], PS[:, bank, bass.ts(c, S)], ACT.Identity,
                                         bias=hd.bq(j * CPJ + c))
                ins.then_inc(q_stored, 1)

            def exp(n, r):
                act.wait_ge(shifted, n + 1)
                act.activation(SS[r], SS[r], ACT.Exp, scale=hd.scale).then_inc(exped, 1)

            def step(n, r, ahead):
                for b, slot, j in ahead:
                    store_q(b, slot, j)
                act.wait_ge(p_turned, n + 1)
                if known(n, 1):
                    act.wait_ge(out_ready, n)
                act.activation(PT, turn_ps, ACT.Copy).then_inc(p_stored, 1)
                if not isinstance(n, int) or n + 2 < NT:
                    exp(n + 2, (r + 2) % 4)

            for j in range(JOBS):
                store_q(0, 0, j, ahead=True)
            for b in range(B):
                store_vw(b)
                if b in (2, 4):
                    exp(b // 2 - 1, b // 2 - 1)
            for j in range(JOBS):
                store_q(1, 1, j, ahead=True)
            attention_steps(act, step, JOBS)
            if after:
                after.scalar(act)

        @block.gpsimd
        def _(pool):
            k.clear_last(pool)
            pool.wait_ge(v_biased, NC)

            def spread_values(b, r):
                if known(b, 2):
                    pool.wait_ge(vw_ready, b - 1)
                if NC == 1:
                    v = over(hd.VT[:, 0, bass.ts(b, C)], 1, H)
                    m = over(hd.head_mask, 2, C)
                    o = VM[r].rearrange("p (h c) -> p h c", c=C)
                else:
                    v = over(hd.VT[:, :, bass.ts(b, C)], 2, HPC)
                    m = over(over(hd.head_mask, 1, NC), 3, C)
                    o = VM[r].rearrange("p (n h c) -> p n h c", h=HPC, c=C)
                pool.tensor_tensor(o, v, m, ALU.mult).then_inc(v_spread, 1)

            rolled(pool, B, 2, spread_values)
            with pool.Fori(0, NT // 4) as i:
                for r in range(4):
                    pool.wait_ge(summed, i * 4 + r + 1)
                    sv = SS[r].rearrange("p (h c) -> p h c", c=C)
                    pool.tensor_tensor(sv, sv, over(rec[r], 2, C), ALU.mult).then_inc(normed, 1)
            if after:
                after.gpsimd(pool)

        @block.tensor
        def _(pe):
            for sm, n in weights_loaded:
                pe.wait_ge(sm, n)
            for c in range(NC):
                if c >= 2:
                    pe.wait_ge(v_biased, c - 1)
                pe.matmul(PS[:, 6 + c % 2, :], hd.wv(c), k.ctxT[:], start=True, stop=True).then_inc(v_ready, 1)

            def value_products(b):
                pe.wait_ge(v_spread, b + 1)
                if b >= 2:
                    pe.wait_ge(vw_stored, b - 1)
                for c in range(8):
                    mm = pe.matmul(vw_ps[b % 2][:, bass.ts(c, D)], VM[b % 2][:, bass.ts(c, P)], hd.wo(c),
                                   start=True, stop=True)
                mm.then_inc(vw_ready, 1)

            norm_tensor(pe, k, nm)
            pe.wait_ge(nm.xt_ready, 2)
            for n, (c, heads) in enumerate(key_jobs):
                if n >= 2:
                    pe.wait_ge(k_masked[n % 2], n // 2)
                pe.matmul(PS[:, n % 2, :], hd.wk(c), k.ctxT[:], start=True, stop=True).then_inc(k_ready, 1)
            pe.wait_ge(nm.xt_ready, NB)

            def make_q(b, slot, j, ahead=False):
                if not ahead:
                    pe.wait_ge(q_stored, b * JOBS + j)
                elif j >= 2:
                    pe.wait_ge(q_stored, b * JOBS + j - 1)
                bank = query_bank(b, j, ahead)
                for c in range(CPJ):
                    mm = pe.matmul(PS[:, bank, bass.ts(c, S)], hd.wq(j * CPJ + c), k.XT[:, bass.ts(b, S)],
                                   start=True, stop=True)
                mm.then_inc(q_ready, 1)

            def scores(n, b, r):
                pe.wait_ge(q_stored, (b + 1) * JOBS)
                q = lambda c, slot=r // 2: hd.QT[slot][:, c, bass.ts(r % 2, P)]
                to = score[r % 2]
                if known(n, 2):
                    pe.wait_ge(shifted, n - 1)
                masked = hd.mask is not None
                if NC == 1:
                    for half in range(2):
                        mm = pe.matmul(to[:, bass.ts(half, BLK)], q(0), Kflat[:, b, bass.ts(half, BLK)],
                                       start=True, stop=not masked)
                        if masked:
                            m = hd.mask[:, r % 2, :] if hd.per_tile else hd.mask[:, b, :]
                            mm = pe.matmul(to[:, bass.ts(half, BLK)].rearrange("p (h c) -> p h c", c=C),
                                           k.identb[:], over(m, 1, H // 2), start=False, stop=True)
                else:
                    for c in range(NC):
                        mm = pe.matmul(to[:, bass.ts(c, P)], q(c), Kflat[:, b, bass.ts(c, P)], start=True, stop=True)
                mm.then_inc(score_ready, 1)

            def turn(n, r):
                pe.wait_ge(normed, n + 1)
                if known(n, 1):
                    pe.wait_ge(p_stored, n)
                for c in range(8):
                    mm = pe.transpose(turn_ps[:, bass.ts(c, P)], SS[r][:, bass.ts(c, P)], k.identf[:])
                mm.then_inc(p_turned, 1)

            def output(n, b):
                pe.wait_ge(p_stored, n + 1)
                if known(n, 1):
                    pe.wait_ge(out_added, n)
                for c in range(8):
                    mm = pe.matmul(PS[:, OUT, 0:D], PT[:, bass.ts(c, P)], VW[:, b, c, :],
                                   start=(c == 0), stop=(c == 7))
                mm.then_inc(out_ready, 1)

            def step(n, r, ahead):
                if not isinstance(n, int) or n + 2 < NT:
                    scores(n + 2, step.b0 + (r + 2) // 2, (r + 2) % 4)
                for job in ahead[:1]:
                    make_q(*job)
                turn(n, r)
                for job in ahead[1:]:
                    make_q(*job)
                if known(n, 1):
                    output(n - 1, step.b0 + (r - 1) // 2)

            for j in range(JOBS):
                make_q(0, 0, j, ahead=True)
            for b in (0, 1):
                value_products(b)
            for sm in k_masked:
                pe.wait_ge(sm, len(key_jobs) // 2)
            scores(0, 0, 0)
            scores(1, 0, 1)
            for b in range(2, B):
                value_products(b)
            pe.wait_ge(vw_stored, B)
            for j in range(JOBS):
                make_q(1, 1, j, ahead=True)
            attention_steps(pe, step, JOBS)
            output(NT - 1, B - 1)


def attention_steps(eng, step, jobs):
    def ahead(b, r):
        share = range(0, (jobs + 1) // 2) if r % 2 == 0 else range((jobs + 1) // 2, jobs)
        return [(b + 2 + r // 2, r // 2, j) for j in share]

    for n in range(4):
        step.b0 = 0
        step(n, n, ahead(0, n))
    with eng.Fori(1, NT // 4 - 1) as i:
        step.b0 = i * 2
        for r in range(4):
            step(i * 4 + r, r, ahead(i * 2, r))
    for r in range(4):
        step.b0 = B - 2
        step(NT - 4 + r, r, [])


def narrow_attention(k, n, wa, mask, per_tile, before=None):
    place = k.RW[:, 3 * HC:3 * HC + 512]
    QT = [place[:, bass.ts(r, S)].rearrange("p (c q) -> p c q", c=1) for r in range(2)]
    VT = k.RW[:, 2 * HC:2 * HC + B * C].rearrange("p (c n) -> p c n", c=1)
    spare = [k.XN[:, bass.ts(r, NT // 2), :].rearrange("p t d -> p (t d)") for r in range(2)]
    wq, wk, wv, wo = (lambda c, m=m: wa[:, m, :] for m in range(4))
    hd = Heads(f"l{n}x", 1, wq, wk, wv, wo,
               lambda c: k.col(f"bq{n}"), lambda c: k.col(f"bk{n}"), lambda c: k.col(f"bv{n}"),
               (D // H) ** -0.5, k.head16[:], QT, VT, spare, k.col(f"bk{n}"), n == 1, mask, per_tile)
    heads_attention(k, hd, f"bo{n}", [(k.att_loaded, 64), (k.masks_made, 2)], before)


def attention_1(k):
    narrow_attention(k, 1, k.Wa[0], k.mask1_add, True)



def product_keys(k):
    nc, PS, RA, RB, RC = k.nc, k.PS, k.RA, k.RB, k.RC
    nm = Norm(k, "l1f", k.X, counted=True)
    s = lambda what: k.sem(f"l1f_{what}")
    vec, paced = s("vector"), s("paced")
    wf_ready, wf_stored = s("wf_ready"), s("wf_stored")
    bn_var, bn_std, bn_ready = s("bn_var"), s("bn_std"), s("bn_ready")
    z_ready, z_stored = s("z_ready"), s("z_stored")
    xb_ready, s_ready, s_stored = s("xb_ready"), s("s_ready"), s("s_stored")
    added, sig_ready, g_ready, g_turned = s("added"), s("sig_ready"), s("g_ready"), s("g_turned")
    m_ready, out_ready, out_added = s("m_ready"), s("out_ready"), s("out_added")

    w_q = RC[:, 0:2048].rearrange("p (n d) -> p n d", n=2 * NH)
    keysT = RC[:, 2048:2560].rearrange("p (n c) -> p n c", n=2 * NH)
    downT = RC[:, 2560:3584].rearrange("p (n c) -> p n c", n=8)
    up = RC[:, 3584:4608].rearrange("p (n c) -> p n c", n=8)
    Wf = RC[:, 4608:5120]
    zT = RB[:, :].rearrange("p (n t) -> p n t", n=8)
    A = [RA[:, bass.ts(h, NE)] for h in range(NH)]
    Ssb = [k.RW[:, bass.ts(r, 512)] for r in range(2)]
    M = [k.RW[:, bass.ts(1 + r, 1024)] for r in range(2)]
    xb = [k.RW[:, bass.ts(24 + r, P)] for r in range(2)]
    cand = k.RW[:, 3328:3840]
    t8 = k.RW[:, 3840:3968].rearrange("p (n j) -> p n j", j=8)
    v8 = k.RW[:, 3968:4032].rearrange("p (n j) -> p n j", j=8)
    bn = k.stats[:].rearrange("p t s -> p (t s)")
    mv, bstd, brstd, scale, shift, tmp = (k.mom[:, j, 0:2] for j in range(6))
    OUT, SP, Z, WF = 6, 7, 6, 7
    gt, *SG = (PS[:, 2 * n:2 * n + 2, :].rearrange("p a f -> p (a f)") for n in range(3))

    def pair_scores(r, h):
        s0 = over(Ssb[r][:, bass.ts(h, NK)], 2, NK)
        s1 = over(Ssb[r][:, bass.ts(NH + h, NK)], 1, NK)
        return A[h].rearrange("p (a b) -> p a b", a=NK), s0, s1

    with nc.Block() as block:

        @block.vector
        def _(dve):
            own = Tally(dve, vec)
            norm_vector(dve, k, nm, own)
            for q in range(NB):
                dve.wait_ge(nm.xt_ready, q + 1)
                own.mark(dve.bn_stats(bn[:, bass.ts(q, 6)], k.XT[:, bass.ts(q, BLK)]))
            own.wait()
            dve.bn_aggr(mv, bn[:, 0:24]).then_inc(bn_var, 1)
            dve.wait_ge(bn_std, 1)
            own.settle(dve.reciprocal(brstd[:, 0:1], bstd[:, 0:1]))
            own.settle(dve.tensor_tensor(scale[:, 0:1], brstd[:, 0:1], k.col("gamma"), ALU.mult))
            own.settle(dve.tensor_tensor(tmp[:, 0:1], scale[:, 0:1], mv[:, 0:1], ALU.mult))
            dve.tensor_tensor(shift[:, 0:1], k.col("beta"), tmp[:, 0:1], ALU.subtract).then_inc(bn_ready, 1)

            def picks(n, r):
                dve.wait_ge(s_stored, n + 1)
                dve.sem_inc(paced, 1)
                for j in range(2 * NH):
                    own.mark(dve.max(t8[:, j, :], Ssb[r][:, bass.ts(j, NK)]))
                own.wait()
                own.settle(dve.tensor_tensor(cand.rearrange("p (h a b) -> p h a b", h=NH, a=8),
                                             over(t8[:, 0:NH, :], 3, 8), over(t8[:, NH:, :], 2, 8), ALU.add))
                dve.sem_inc(paced, 1)
                for h in range(NH):
                    own.mark(dve.max(v8[:, h, :], cand[:, bass.ts(h, 64)]))
                own.wait()

            def weigh(n, r, q):
                dve.wait_ge(g_turned, (n + 1) * NH)
                dve.wait_ge(z_stored, (q + 1) * 8)
                if known(n, 2):
                    dve.wait_ge(out_ready, n - 1)
                dve.tensor_tensor(M[r].rearrange("p (c t) -> p c t", c=8), gt.rearrange("p (c t) -> p c t", c=8),
                                  zT[:, :, bass.ts(n, P)], ALU.mult).then_inc(m_ready, 1)

            def add_out(n):
                dve.wait_ge(out_ready, n + 1)
                dve.tensor_tensor(k.X[:, n, :], k.X[:, n, :], PS[:, OUT, 0:D], ALU.add).then_inc(out_added, 1)

            def step(n, t, q):
                r = t % 2
                picks(n, r)
                if known(n, 2):
                    add_out(n - 2)
                if known(n, 1):
                    weigh(n - 1, 1 - r, q if t else q - 1)
                for h in range(NH):
                    dve.wait_ge(sig_ready, n * NH + h + 1)
                    dve.scalar_tensor_tensor(A[h], A[h], v8[:, h, 7:8], SG[h % 2], ALU.is_ge,
                                             ALU.mult).then_inc(g_ready, 1)

            per = 2 * NH + 1 + NH
            for n in range(TPB):
                step(n, n, 0)
            with dve.Fori(1, NB) as i:
                own.enter(i - 1, TPB * per)
                for t in range(TPB):
                    step(i * TPB + t, t, i)
            own.leave(NB - 1)
            add_out(NT - 2)
            weigh(NT - 1, 1, NB - 1)
            add_out(NT - 1)

        @block.scalar
        def _(act):
            act.wait_ge(wf_ready, 1)
            act.activation(Wf, PS[:, WF, :], ACT.Copy).then_inc(wf_stored, 1)
            norm_scalar(act, k, nm)
            act.wait_ge(bn_var, 1)
            act.activation(bstd[:, 0:1], mv[:, 1:2], ACT.Sqrt, bias=k.eps[:, 0:1]).then_inc(bn_std, 1)
            act.wait_ge(bn_ready, 1)

            def gelu(m, c, q):
                act.wait_ge(z_ready, m + 1)
                act.activation(zT[:, c, bass.ts(q, BLK)], PS[:, Z + c % 2, :], ACT.Gelu).then_inc(z_stored, 1)

            def batch_normed(n, r):
                if known(n, 2):
                    act.wait_ge(s_ready, n - 1)
                act.activation(xb[r], k.XT[:, bass.ts(n, P)], ACT.Identity, bias=shift[:, 0:1],
                               scale=scale[:, 0:1]).then_inc(xb_ready, 1)

            def store_s(n, r):
                act.wait_ge(s_ready, n + 1)
                if known(n, 2):
                    act.wait_ge(added, (n - 1) * NH)
                act.activation(Ssb[r], PS[:, SP, :], ACT.Copy).then_inc(s_stored, 1)

            def sigmoid(n, h):
                act.wait_ge(added, n * NH + h + 1)
                if known(n, 1) or h >= 2:
                    act.wait_ge(g_ready, n * NH + h - 1)
                act.activation(SG[h % 2], A[h], ACT.Sigmoid).then_inc(sig_ready, 1)

            def step(n, t, q):
                r = t % 2
                for h in range(4):
                    sigmoid(n, h)
                if not isinstance(n, int) or n + 1 < NT:
                    store_s(n + 1, 1 - r)
                for h in range(4, NH):
                    sigmoid(n, h)
                if not isinstance(n, int) or n + 2 < NT:
                    batch_normed(n + 2, r)
                if not isinstance(n, int) or n + TPB < NT:
                    for c in (2 * t, 2 * t + 1):
                        gelu(n * 2 + 8 + c % 2, c, q + 1)

            batch_normed(0, 0)
            batch_normed(1, 1)
            store_s(0, 0)
            for c in range(8):
                gelu(c, c, 0)
            run_tiles(act, step)

        @block.gpsimd
        def _(pool):
            k.clear_last(pool)

            def step(n, t, q):
                r = t % 2
                pool.wait_ge(s_stored, n + 1)
                for h in range(NH):
                    if known(n, 1):
                        pool.wait_ge(g_turned, (n - 1) * NH + h + 1)
                    pool.tensor_tensor(*pair_scores(r, h), ALU.add).then_inc(added, 1)
            run_tiles(pool, step)

        @block.tensor
        def _(pe):
            pe.wait_ge(k.keys_loaded, 64)
            for n in range(2 * NH):
                mm = pe.matmul(PS[:, WF, bass.ts(n, NK)], w_q[:, n, :], keysT[:, n, :], start=True, stop=True)
            mm.then_inc(wf_ready, 1)
            norm_tensor(pe, k, nm)
            pe.wait_ge(wf_stored, 1)
            pe.wait_ge(nm.xt_ready, NB)

            def project(m, c, q):
                if known(m, 2):
                    pe.wait_ge(z_stored, m - 1)
                pe.matmul(PS[:, Z + c % 2, :], downT[:, c, :], k.XT[:, bass.ts(q, BLK)], start=True,
                          stop=True).then_inc(z_ready, 1)

            def halves(n, r, z=None):
                pe.wait_ge(xb_ready, n + 1)
                if z is not None:
                    pe.wait_ge(z_stored, z)
                pe.matmul(PS[:, SP, :], xb[r], Wf, start=True, stop=True).then_inc(s_ready, 1)

            def turn(n, r, h):
                pe.wait_ge(g_ready, n * NH + h + 1)
                for c in range(8):
                    mm = pe.matmul(gt[:, bass.ts(c, P)], A[h][:, bass.ts(c, P)], k.identf[:],
                                   start=(h == 0 and c % 4 == 0), stop=(h == NH - 1), is_transpose=True,
                                   skip_group_check=True)
                mm.then_inc(g_turned, 1)

            def output(n, r):
                pe.wait_ge(m_ready, n + 1)
                if known(n, 1):
                    pe.wait_ge(out_added, n)
                for c in range(8):
                    mm = pe.matmul(PS[:, OUT, 0:D], M[r][:, bass.ts(c, P)], up[:, c, :],
                                   start=(c == 0), stop=(c == 7))
                mm.then_inc(out_ready, 1)

            def step(n, t, q):
                r = t % 2
                last = isinstance(n, int) and n + TPB >= NT
                if not isinstance(n, int) or n + 1 < NT:
                    halves(n + 1, 1 - r, 8 * NB if last else n * 2 + 8)
                if not last:
                    if known(n, 2):
                        pe.wait_ge(out_added, n - 1)
                    project(n * 2 + 8, 2 * t, q + 1)
                for h in range(4):
                    turn(n, r, h)
                if not last:
                    pe.wait_ge(s_stored, n + 2)
                    project(n * 2 + 9, 2 * t + 1, q + 1)
                for h in range(4, NH):
                    turn(n, r, h)
                if not last:
                    pe.wait_ge(z_stored, n * 2 + 10)
                if known(n, 1):
                    output(n - 1, 1 - r)

            halves(0, 0)
            pe.wait_ge(s_stored, 1)
            for c in range(8):
                project(c, c, 0)
            run_tiles(pe, step)
            output(NT - 1, 1)


def attention_2(k):
    def load(sp):
        sp.wait_ge(k.l0f_loaded, 64)
        for g in range(2):
            for n, m in enumerate("gud"):
                sp.dma_start(k.RA[:, 6144 * g + 2048 * n:6144 * g + 2048 * (n + 1)],
                             k.dram[f"w{m}2_{g}"]).then_inc(k.l2f_loaded, 16)
    narrow_attention(k, 2, k.Wa[1], k.mask2_add, False, before=load)



def silu_experts(k):
    nm, r = Norm(k, "l2f", k.X, counted=True), Route(k, "l2f", E2, 2)
    n = E2 * FH
    rests = Rests(k, "l2f", [("RA", 0, 3 * n, "RB", 8320, P), ("XT", 0, T, "XN", 0, P),
                             *(("RA", (3 + m) * n, n, "RC", m * n, P) for m in range(3))])
    passes = []
    for g in range(2):
        w = [tuple(a[:, bass.ts(m, n)] for a in rests.parts[0][1:]) for m in range(3)] if g == 0 else \
            [part[1:] for part in rests.parts[2:]]
        chunk = lambda pair, c: tuple(a[:, bass.ts(c, P)] for a in pair)
        passes.append([Step(chunk(w[0], c), chunk(w[1], c), chunk(w[2], c), spread=(k.pair_sel[:, c, :], g))
                       for c in range(PAIRS)])
    ex = Experts(k, "l2f", passes, ACT.Silu, rests, xt=1, now=2)
    vec = k.sem("l2f_vector")

    with k.nc.Block() as block:

        @block.sync
        def _(sp):
            sp.wait_ge(k.l2f_loaded, 96)
            sp.wait_ge(ex.acc_read, NB)
            for n, m in enumerate("qkvo"):
                sp.dma_start(k.RA[:, bass.ts(n, 1024)], k.dram[f"w{m}3"]).then_inc(k.l3x_loaded, 16)

        @block.gpsimd
        def _(pool):
            k.clear_last(pool)
            ex.rests.gpsimd(pool)
            experts_gpsimd(pool, ex)

        @block.vector
        def _(dve):
            own = Tally(dve, vec)
            norm_vector(dve, k, nm, own)
            dve.wait_ge(k.l2f_loaded, 96)
            ex.vector_rests(dve, nm)
            route_top2(dve, k, r, own, None, renormalise=False)
            experts_vector(dve, ex)

        @block.scalar
        def _(act):
            norm_scalar(act, k, nm)
            route_exp(act, r)
            ex.scalar_rests(act, r.logits_ready)
            route_store(act, k, r)
            experts_scalar(act, ex)

        @block.tensor
        def _(pe):
            norm_tensor(pe, k, nm, behind=lambda b: route_logits(pe, k, r, nm, k.gates[:, 0:2 * E2], b))
            route_turn(pe, k, r)
            experts_tensor(pe, ex, r)



class PostNorm:

    def __init__(self, k):
        self.k, self.nm, self.shifted = k, Norm(k, "l3y", k.XN, turn=False, counted=True), k.sem("l3y_shifted")

    def vector(self, dve, own, out_added):
        k = self.k
        dve.wait_ge(out_added, NT)
        norm_vector(dve, k, self.nm, own)
        dve.wait_ge(self.nm.xn_ready, NT)
        own.settle(dve.tensor_tensor(k.XN[:], k.XN[:], over(k.row("ln_gamma"), 1, NT), ALU.mult))
        dve.wait_ge(self.shifted, 1)
        dve.tensor_tensor(k.X[:], k.X[:], k.XN[:], ALU.add)

    def scalar(self, act):
        norm_scalar(act, self.k, self.nm)

    def gpsimd(self, pool):
        k = self.k
        pool.tensor_tensor(k.X[:], k.X[:], over(k.row("ln_beta"), 1, NT), ALU.add).then_inc(self.shifted, 1)


def attention_3(k):
    def load(sp):
        sp.wait_ge(k.keys_loaded, 64)
        sp.wait_ge(k.att_loaded, 64)
        sp.dma_start(k.RC[:, 0:4096], k.dram["wg3"]).then_inc(k.l3f_loaded, 16)
        sp.dma_start(k.RC[:, 4096:8192], k.dram["wu3"]).then_inc(k.l3f_loaded, 16)
        sp.dma_start(k.RC[:, 8192:8256], k.dram["wgs3"]).then_inc(k.l3f_loaded, 16)
        sp.dma_start(k.RC[:, 8256:8320], k.dram["wus3"]).then_inc(k.l3f_loaded, 16)
        sp.dma_start(k.RC[0:FH, 8320:8448], k.dram["wds3"]).then_inc(k.l3f_loaded, 16)
    w = [k.RA[:, bass.ts(n, 1024)] for n in range(4)]
    chunk = lambda a: lambda c: a[:, bass.ts(c, P)]
    QT = [k.RA[:, bass.ts(2 + r, 2048)].rearrange("p (c q) -> p c q", c=8) for r in range(2)]
    VT = k.RA[:, 8192:12288].rearrange("p (c n) -> p c n", c=8)
    hd = Heads("l3x", 8, chunk(w[0]), chunk(w[1]), chunk(w[2]), chunk(w[3]),
               lambda c: k.col("bq3", c), lambda c: k.col("bk3", c), lambda c: k.col("bv3", c),
               64 ** -0.5, k.head2[:], QT, VT, w[1:3],
               k.cols[:, COLS["bk3"][0]:COLS["bk3"][0] + 8], counted=True)
    heads_attention(k, hd, "bo3", [(k.l3x_loaded, 64)], before=load, after=PostNorm(k))



def route_grouped(dve, k, r, own):
    full = lambda a: a.rearrange("p r e -> p (r e)")
    tokens = lambda a: full(a).rearrange("p (t e) -> p t e", e=E3)
    groups = lambda a: full(a).rearrange("p (g e) -> p g e", e=GE)
    four = lambda a: full(a).rearrange("p (t g h) -> p t g h", g=G3, h=G3)
    small = k.RB[:, 8320:8320 + 8 * NT * G3].rearrange("p (n g) -> p n g", n=8)
    total, rank, low = (small[:, n, :] for n in range(3))
    pg = lambda a: a.rearrange("p (t g) -> p t g", g=G3)

    dve.wait_ge(r.exped, 1)
    own.settle(dve.tensor_tensor(tokens(r.L), tokens(r.W), over(k.row("gate_bias"), 1, NT), ALU.add))
    def halves(a):
        pairs = a.rearrange("p (m two) -> p m two", two=2)
        return pairs[:, :, 0], pairs[:, :, 1]

    n = NT * G3
    best, second = full(r.T1)[:, 0:4 * n], full(r.T1)[:, 4 * n:8 * n]
    own.mark(dve.tensor_tensor(best, *halves(full(r.L)), ALU.max))
    own.settle(dve.tensor_tensor(second, *halves(full(r.L)), ALU.min))
    for places in ([full(r.T2)[:, bass.ts(j, 2 * n)] for j in range(3)], [small[:, 3 + j, :] for j in range(3)]):
        best_two, second_two = halves(best), halves(second)
        best, second, worse = places
        own.mark(dve.tensor_tensor(best, *best_two, ALU.max))
        own.mark(dve.tensor_tensor(worse, *best_two, ALU.min))
        own.settle(dve.tensor_tensor(second, *second_two, ALU.max))
        own.settle(dve.tensor_tensor(second, second, worse, ALU.max))
    own.settle(dve.tensor_tensor(total, best, second, ALU.add))
    mine, others = over(pg(total), 3, G3), over(pg(total), 2, G3)
    own.mark(dve.tensor_tensor(four(r.T1), others, mine, ALU.is_gt))
    own.settle(dve.tensor_tensor(four(r.T2), others, mine, ALU.is_equal))
    own.settle(dve.tensor_tensor(full(r.T2).rearrange("p (t n) -> p t n", t=NT),
                                 full(r.T2).rearrange("p (t n) -> p t n", t=NT), over(k.before[:], 1, NT), ALU.mult))
    own.settle(dve.tensor_tensor(full(r.T1), full(r.T1), full(r.T2), ALU.add))
    own.settle(dve.tensor_reduce(rank, groups(r.T1), AX.X, ALU.add))
    own.settle(dve.tensor_scalar(low, rank, TG - 0.5, FAR, ALU.is_gt, ALU.mult))
    own.settle(dve.tensor_tensor(groups(r.T1), groups(r.L), over(low, 2, GE), ALU.add))
    for t in range(NT):
        own.mark(dve.max(r.top[:, t, :], tokens(r.T1)[:, t, :]))
    own.wait()
    for t in range(NT):
        own.mark(dve.match_replace(tokens(r.T2)[:, t, :], r.top[:, t, :], tokens(r.T1)[:, t, :], -3.0e38))
    own.wait()
    own.settle(dve.tensor_tensor(full(r.T1), full(r.T1), full(r.T2), ALU.not_equal))
    own.settle(dve.tensor_tensor(full(r.W), full(r.W), full(r.T1), ALU.mult))
    z, rz = r.z[:, 0:NT], r.rz[:, 0:NT]
    own.settle(dve.tensor_reduce(z, tokens(r.W), AX.X, ALU.add))
    own.settle(dve.tensor_scalar(z, z, 1e-20, None, ALU.add))
    own.settle(dve.reciprocal(rz, z))
    own.settle(dve.tensor_scalar(rz, rz, 2.5, None, ALU.mult))
    own.settle(dve.tensor_tensor(tokens(r.W), tokens(r.W), over(rz, 2, E3), ALU.mult))
    route_parts(dve, r, own)


def grouped_experts(k):
    nm, r = Norm(k, "l3f", k.X), Route(k, "l3f", E2, 2)
    n = E3 * FH
    down = k.RB[:, 12288:16384]
    rests = Rests(k, "l3f", [("RC", 0, n, "RA", 0, P), ("RC", n, n, "RA", n, P), ("RB", 12288, n, "RA", 2 * n, P),
                             ("RC", 2 * n, 2 * FH, "RB", 9600, P), ("RC", 2 * n + 2 * FH, D, "RB", 9728, FH),
                             ("XT", 0, T, "XN", 0, P)])
    weights = [part[1:] for part in rests.parts[:3]]
    chunk = lambda pair, c: tuple(a[:, bass.ts(c, P)] for a in pair)
    steps = [Step(*(chunk(pair, c) for pair in weights), spread=(k.pair_sel[:, c % PAIRS, :], c // PAIRS))
             for c in range(2 * PAIRS)]
    own_in, own_down = (part[1:] for part in rests.parts[3:5])
    steps.append(Step(tuple(a[:, 0:FH] for a in own_in), tuple(a[:, FH:2 * FH] for a in own_in), own_down))
    out_stored = k.lasting_sem("out_stored")
    ex = Experts(k, "l3f", [steps], ACT.Silu, rests, xt=5, now=6)
    vec = k.sem("l3f_vector")

    with k.nc.Block() as block:

        @block.sync
        def _(sp):
            sp.dma_start(down, k.dram["wd3"]).then_inc(k.l3d_loaded, 16)
            ov = k.out.rearrange("b (j p) d -> p (b j) d", p=P)
            for q in range(NB):
                sp.wait_ge(ex.out_added, q + 1)
                tiles = slice(TPB * q, TPB * (q + 1))
                sp.dma_start(ov[:, tiles, :], k.X[:, tiles, :]).then_inc(out_stored, 16)
            sp.wait_ge(out_stored, 16 * NB)

        @block.gpsimd
        def _(pool):
            k.clear_last(pool)
            ex.rests.gpsimd(pool)
            experts_gpsimd(pool, ex)

        @block.vector
        def _(dve):
            own = Tally(dve, vec)
            norm_vector(dve, k, nm, own)
            dve.wait_ge(k.l3f_loaded, 80)
            dve.wait_ge(k.l3d_loaded, 16)
            ex.vector_rests(dve, nm)
            route_grouped(dve, k, r, own)
            experts_vector(dve, ex, count=False)

        @block.scalar
        def _(act):
            norm_scalar(act, k, nm)
            act.wait_ge(r.logits_ready, 1)
            act.activation(r.W.rearrange("p r e -> p (r e)"), r.logits, ACT.Sigmoid).then_inc(r.exped, 1)
            ex.scalar_rests(act, r.logits_ready)
            route_store(act, k, r)
            experts_scalar(act, ex)

        @block.tensor
        def _(pe):
            norm_tensor(pe, k, nm, behind=lambda b: route_logits(pe, k, r, nm, k.gates[:, 2 * E2:2 * E2 + E3], b))
            route_turn(pe, k, r)
            experts_tensor(pe, ex, r)


LAYERS = [similarity_attention, gelu_experts, attention_1, product_keys, attention_2, silu_experts,
          attention_3, grouped_experts]


def program(nc, dram, out):
    with ExitStack() as ctx:
        k = Core(nc, ctx, dram)
        setup(k)
        k.out = out
        for layer in LAYERS:
            layer(k)



def layouts(v):
    import numpy as np
    a = {}
    c = lambda z: np.ascontiguousarray(z)
    ctx = v["ctx_1024"]
    a["x"] = c(v["x"].reshape(T, D))
    a["ctxT"] = c(ctx.reshape(B * C, D).T)
    a["ctxK"] = c(ctx.transpose(1, 0, 2))
    a["Wqv"] = c(v["L0_xattn_W_qv"].reshape(4, D, D).transpose(1, 0, 2))
    a["w1_0"] = c(v["L0_ffn_w1"].transpose(1, 0, 2))
    a["w2_0"] = c(v["L0_ffn_w2"].reshape(E0, K0, P, D).transpose(2, 0, 1, 3))
    a["b2_0"] = c(v["L0_ffn_b2"])
    a["gw0"] = c(v["L0_ffn_gate_w"])
    a["wa1"] = c(np.stack([v[f"L1_xattn_W{m}"].T for m in "qkvo"], axis=1))
    kv = v["L2_xattn_kv_w"]
    a["wa2"] = c(np.stack([v["L2_xattn_q_w"], kv[:, :D], kv[:, D:], v["L2_xattn_proj_w"]], axis=1))
    a["mask1"] = c(v["mask_SxS2_if1"].reshape(2, P, C).transpose(1, 0, 2))
    a["mask2"] = c(v["mask_BxS2_bk0"].reshape(1, B * C)).view(np.int32)
    a["w_q"] = c(v["L1_ffn_w_q"].reshape(2 * NH, P, D).transpose(1, 0, 2).reshape(P, 2 * NH * D))
    a["keysT"] = c(v["L1_ffn_keys_p"].transpose(3, 2, 0, 1).reshape(P, 2 * NH * NK))
    a["downT"] = c(v["L1_ffn_down"][:NE].T)
    a["up"] = c(v["L1_ffn_up"][:NE].reshape(NE // P, P, D).transpose(1, 0, 2).reshape(P, NE // P * D))
    for g in range(2):
        a[f"wg2_{g}"] = c(v[f"L2_ffn_wg{g}"].transpose(1, 0, 2).reshape(D, E2 * FH))
        a[f"wu2_{g}"] = c(v[f"L2_ffn_wu{g}"].transpose(1, 0, 2).reshape(D, E2 * FH))
        a[f"wd2_{g}"] = c(v[f"L2_ffn_wd{g}"].reshape(PAIRS, P, D).transpose(1, 0, 2).reshape(P, PAIRS * D))
    a["router2"] = c(np.concatenate([v["L2_ffn_router_w0"], v["L2_ffn_router_w1"]], axis=1))
    for m in "qkv":
        a[f"w{m}3"] = c(v[f"L3_xattn_W{m}"])
    a["wo3"] = c(v["L3_xattn_Wo"].reshape(8, P, D).transpose(1, 0, 2).reshape(P, 8 * D))
    a["wg3"] = c(v["L3_ffn_We_gate"].transpose(1, 0, 2).reshape(D, E3 * FH))
    a["wu3"] = c(v["L3_ffn_We_up"].transpose(1, 0, 2).reshape(D, E3 * FH))
    a["wd3"] = c(v["L3_ffn_We_down"].reshape(2 * PAIRS, P, D).transpose(1, 0, 2).reshape(P, 2 * PAIRS * D))
    a["gw3"] = c(v["L3_ffn_gate_w"].T)
    a["wgs3"] = c(v["L3_ffn_Ws_gate"])
    a["wus3"] = c(v["L3_ffn_Ws_up"])
    a["wds3"] = c(v["L3_ffn_Ws_down"])
    col = lambda z: z.reshape(-1, P).T
    kb = v["L2_xattn_kv_b"]
    a["cols"] = c(np.concatenate([col(z) for z in (
        v["L0_xattn_w_sim"], v["L0_ffn_b1"].reshape(-1), v["L1_xattn_bq"], v["L1_xattn_bk"], v["L1_xattn_bv"],
        v["L1_ffn_bn_gamma"], v["L1_ffn_bn_beta"], v["L2_xattn_q_b"], kb[:D], kb[D:], v["L3_xattn_bq"],
        v["L3_xattn_bk"], v["L3_xattn_bv"])], axis=1))
    a["rows"] = c(np.concatenate([v["L0_xattn_b_qv"], v["L1_xattn_bo"], v["L2_xattn_proj_b"], v["L3_xattn_bo"],
                                  v["L3_xattn_ln_gamma"], v["L3_xattn_ln_beta"], v["L0_ffn_gate_b"],
                                  v["L3_ffn_gate_bias"], v["L0_xattn_b_sim"]])[None, :])
    return a


def kernel(**inputs):
    import numpy as _np
    import concourse.bacc as _bacc
    from concourse import mybir as _mybir
    from concourse.bass_utils import run_bass_kernel_spmd as _run

    arrays = layouts({name: _np.asarray(a) for name, a in inputs.items()})
    nc = _bacc.Bacc("TRN2", target_bir_lowering=False, num_devices=1)
    dram = {}
    for name, a in arrays.items():
        dram[name] = nc.dram_tensor(f"in_{name}", a.shape, _mybir.dt.from_np(a.dtype), kind="ExternalInput").ap()
    out = nc.dram_tensor("out_x", (B, S, D), _mybir.dt.float32, kind="ExternalOutput").ap()
    program(nc, dram, out)
    r = _run(nc, [{f"in_{name}": a for name, a in arrays.items()}], core_ids=[0])
    return r.results[0]["out_x"]
```
